# Optimizing a Trainium2 kernel written in Bass

```python
import numpy as np
import jax
import jax.numpy as jnp

def _softmax(x, axis=-1):
    return jax.nn.softmax(x, axis=axis)

def _gelu(x):
    return jax.nn.gelu(x, approximate=True)

def _silu(x):
    return jax.nn.silu(x)

def _sigmoid(x):
    return jax.nn.sigmoid(x)

def _layernorm(x, axis=-1, eps=1e-05):
    m = jnp.mean(x, axis=axis, keepdims=True)
    v = jnp.var(x, axis=axis, keepdims=True)
    return (x - m) / jnp.sqrt(v + eps)

def _scatter_add(tgt, idx, src, axis=0):
    return tgt.at[idx].add(src)

def _segment_sum(src, seg, n):
    return jax.ops.segment_sum(src, seg, n)
kernel_name = 'mk_xattn_ffn_d1_seqx_r4_336b1c'

def setup_inputs(seed: int=0):
    np.random.seed(seed)
    _w = jnp.asarray

    def _rec_inputs():
        import jax
        import jax.numpy as jnp
        _rk = jax.random.key(seed)
        x = -0.0002928 + 1 * jax.random.normal(jax.random.fold_in(_rk, 1), (8, 256, 256), jnp.float32)
        _lenS = 256 - jax.random.randint(jax.random.fold_in(_rk, 7), (8,), 0, max(1, 256 // 4) + 1, jnp.int32)
        _lenS2 = 256 - jax.random.randint(jax.random.fold_in(_rk, 8), (8,), 0, max(1, 256 // 4) + 1, jnp.int32)
        _ctx_1024P = jax.random.normal(jax.random.fold_in(_rk, 11), (8, 16, 256), jnp.float32)
        _ctx_1024c = jax.random.dirichlet(jax.random.fold_in(_rk, 511), 0.3 * jnp.ones((16,), jnp.float32), (8, 256))
        _ctx_1024t = jnp.einsum('bsk,bkd->bsd', _ctx_1024c, _ctx_1024P)
        _ctx_1024t = _ctx_1024t * jax.lax.rsqrt(jnp.mean(jnp.square(_ctx_1024t)) + 1e-12) * 0.953939
        ctx_1024 = -1.39393e-06 + 0.999914 * (_ctx_1024t + 0.3 * jax.random.normal(jax.random.fold_in(_rk, 611), (8, 256, 256), jnp.float32))
        return (x, ctx_1024)
    x, ctx_1024 = _rec_inputs()

    def _L0_xattn_setup():
        import jax, jax.numpy as jnp
        import numpy as np
        E_PHI = 256
        E_F = 256
        HID = 256
        N_HEADS = 16
        HEAD_DIM = HID // N_HEADS
        key = jax.random.key(seed)
        ks = jax.random.split(key, 9)
        B, S = (2, 512)
        s = 0.02
        return {'q': jax.random.normal(ks[0], (B, S, E_PHI), jnp.float32), 'k': jax.random.normal(ks[1], (B, S, E_PHI), jnp.float32), 'v': jax.random.normal(ks[2], (B, S, E_F), jnp.float32), 'W_q': jax.random.normal(ks[3], (E_PHI, HID), jnp.float32) * s, 'W_k': jax.random.normal(ks[4], (E_PHI, HID), jnp.float32) * s, 'W_v': jax.random.normal(ks[5], (E_F, HID), jnp.float32) * s, 'b_v': jax.random.normal(ks[6], (HID,), jnp.float32) * s, 'W_o': jax.random.normal(ks[7], (HID, E_F), jnp.float32) * s, 'b_o': jax.random.normal(ks[8], (E_F,), jnp.float32) * s}
    _L0_xattn_all = _L0_xattn_setup()
    _L0_xattn_in = {k: v for k, v in _L0_xattn_all.items() if k in ('W_q', 'W_k', 'W_v', 'b_v', 'W_o', 'b_o')}
    del _L0_xattn_all

    def _L0_ffn_setup():
        import jax, jax.numpy as jnp
        import numpy as np
        E = 8
        K = 2
        CAP_FACTOR = 1.0
        key = jax.random.key(seed)
        k0, k1, k2, k3 = jax.random.split(key, 4)
        B, S, M, H = (4, 512, 256, 1024)
        x = jax.random.normal(k0, (B, S, M), jnp.float32)
        wg = jax.random.normal(k1, (M, E), jnp.float32) * 0.02
        w1 = jax.random.normal(k2, (E, M, H), jnp.float32) * 0.02
        b1 = jnp.zeros((E, H), jnp.float32)
        w2 = jax.random.normal(k3, (E, H, M), jnp.float32) * 0.02
        b2 = jnp.zeros((E, M), jnp.float32)
        return {'x': x, 'wg': wg, 'w1': w1, 'b1': b1, 'w2': w2, 'b2': b2}
    _L0_ffn_all = _L0_ffn_setup()
    _L0_ffn_in = {k: v for k, v in _L0_ffn_all.items() if k in ('wg', 'w1', 'b1', 'w2', 'b2')}
    del _L0_ffn_all
    return {'x': x, 'ctx_1024': ctx_1024, 'L0_xattn_W_q': _L0_xattn_in['W_q'], 'L0_xattn_W_k': _L0_xattn_in['W_k'], 'L0_xattn_W_v': _L0_xattn_in['W_v'], 'L0_xattn_b_v': _L0_xattn_in['b_v'], 'L0_xattn_W_o': _L0_xattn_in['W_o'], 'L0_xattn_b_o': _L0_xattn_in['b_o'], 'L0_ffn_wg': _L0_ffn_in['wg'], 'L0_ffn_w1': _L0_ffn_in['w1'], 'L0_ffn_b1': _L0_ffn_in['b1'], 'L0_ffn_w2': _L0_ffn_in['w2'], 'L0_ffn_b2': _L0_ffn_in['b2']}

def reference(x, ctx_1024, L0_xattn_W_q, L0_xattn_W_k, L0_xattn_W_v, L0_xattn_b_v, L0_xattn_W_o, L0_xattn_b_o, L0_ffn_wg, L0_ffn_w1, L0_ffn_b1, L0_ffn_w2, L0_ffn_b2):
    import jax
    import jax.numpy as jnp

    def _L0_xattn_ref(q, k, v, W_q, W_k, W_v, b_v, W_o, b_o):
        import jax, jax.numpy as jnp
        import numpy as np
        E_PHI = 256
        E_F = 256
        HID = 256
        N_HEADS = 16
        HEAD_DIM = HID // N_HEADS
        B, S, _ = q.shape
        qh = (q @ W_q).reshape(B, S, N_HEADS, HEAD_DIM)
        kh = (k @ W_k).reshape(B, S, N_HEADS, HEAD_DIM)
        vh = (v @ W_v + b_v).reshape(B, S, N_HEADS, HEAD_DIM)
        scale = 1.0 / jnp.sqrt(jnp.float32(HEAD_DIM))
        scores = jnp.einsum('bihd,bjhd->bhij', qh, kh) * scale
        i = jnp.arange(S)[:, None]
        j = jnp.arange(S)[None, :]
        keep = (j < i) | (i == 0) & (j == 0)
        scores = jnp.where(keep, scores, jnp.float32(-jnp.inf))
        probs = jax.nn.softmax(scores, axis=-1)
        attn = jnp.einsum('bhij,bjhd->bihd', probs, vh).reshape(B, S, HID)
        return attn @ W_o + b_o

    def _L0_ffn_ref(x, wg, w1, b1, w2, b2):
        import jax, jax.numpy as jnp
        import numpy as np
        E = 8
        K = 2
        CAP_FACTOR = 1.0
        B, S, M = x.shape
        N = B * S
        capacity = int(CAP_FACTOR * K * N // E)
        xt = x.reshape(N, M)
        logits = xt @ wg
        scores = jax.nn.softmax(logits, axis=-1)
        topv, topi = jax.lax.top_k(scores, K)
        topv = topv / jnp.sum(topv, axis=-1, keepdims=True)
        masks = jax.nn.one_hot(topi.T, E, dtype=jnp.int32)
        flat = masks.reshape(K * N, E)
        locs = jnp.cumsum(flat, axis=0) - 1
        pos = jnp.sum(locs * flat, axis=-1).reshape(K, N).T
        valid = pos < capacity
        gate = topv * valid.astype(topv.dtype)
        pos_c = jnp.where(valid, pos, 0)
        xk = xt[:, None, :] * valid[..., None].astype(xt.dtype)
        disp = jnp.zeros((E, capacity, M), xt.dtype)
        disp = disp.at[topi, pos_c].add(xk)
        h = jax.nn.relu(jnp.einsum('ecm,emh->ech', disp, w1) + b1[:, None, :])
        y = jnp.einsum('ech,ehm->ecm', h, w2) + b2[:, None, :]
        out = jnp.sum(gate[..., None] * y[topi, pos_c], axis=1)
        return out.reshape(B, S, M)
    x = x + _L0_xattn_ref(_layernorm(x, axis=-1), ctx_1024, ctx_1024, L0_xattn_W_q, L0_xattn_W_k, L0_xattn_W_v, L0_xattn_b_v, L0_xattn_W_o, L0_xattn_b_o)
    x = x + _L0_ffn_ref(_layernorm(x, axis=-1), L0_ffn_wg, L0_ffn_w1, L0_ffn_b1, L0_ffn_w2, L0_ffn_b2)
    return x

_drawn_inputs = setup_inputs


def setup_inputs(seed=0):
    import zlib

    import numpy as np

    out = dict(_drawn_inputs(seed))
    spreads = {'L0_ffn_b1': (0.0, 0.1), 'L0_ffn_b2': (0.0, 0.1)}
    factors = {'L0_xattn_W_q': 7.937, 'L0_xattn_W_k': 7.055, 'L0_xattn_b_v': 4.772}
    for name, (base, spread) in spreads.items():
        noise = np.random.default_rng([zlib.crc32(name.encode()), seed]).standard_normal(out[name].shape)
        drawn = base * np.exp(spread * noise) if base else spread * noise
        out[name] = jnp.asarray(drawn.astype(out[name].dtype))
    for name, factor in factors.items():
        out[name] = (out[name] * factor).astype(out[name].dtype)
    return out
```

```python
from contextlib import ExitStack

import concourse.bass as bass
from concourse import mybir

P = 128
F32 = mybir.dt.float32
F32R = mybir.dt.float32r
BF16 = mybir.dt.bfloat16
I32 = mybir.dt.int32
U32 = mybir.dt.uint32
ALU = mybir.AluOpType
ACT = mybir.ActivationFunctionType
AX_X = mybir.AxisListType.X

HEADS = 16
HD = 16
HPG = 4
GROUPS = HEADS // HPG
VW = 32
ROWS = 3 * HD
EPS = 1e-5
MASKED = -1e38
EXPERTS = 8
TOPK = 2
HALVES = 2


def wait_alone(eng, started, semaphore, value):
    if not isinstance(value, int):
        value = eng.to_reg(value)
    eng.wait_ge(started, 1)
    eng.wait_ge(semaphore, value)


def attention(nc, sem, sb, persist, x, ctx_in, Wq, Wk, Wv, bv, Wo, bo, wg, w1, b1, w2, b2, xn_rows, y_rows):
    B, S, D = x.shape
    x_all, ident, dl_all, expert_all, ps = (persist[k] for k in ("x_all", "ident", "dl_all", "expert_all", "ps"))
    raw1, raw2, b1_sb, b2_bc, zeros = (persist[k] for k in ("raw1", "raw2", "b1_sb", "b2_bc", "zeros"))
    weights_loaded, biases_loaded = persist["weights_loaded"], persist["biases_loaded"]

    score = [ps[:, 0:3, :].rearrange("p a b -> p (a b)"), ps[:, 3:6, :].rearrange("p a b -> p (a b)")]
    bank = [ps[:, 6, :], ps[:, 7, :]]

    w_raw = sb("w_raw", [P, 4, 2, D], F32)
    w_hi = sb("w_hi", [P, 4, 2, D], F32R)
    w_lo = sb("w_lo", [P, 4, 2, D], F32R)
    bv_bc = sb("bv_bc", [P, D], F32)
    bo_bc = sb("bo_bc", [P, D], F32)
    wg_sb = sb("wg_sb", [P, 2, EXPERTS], F32)
    identb = sb("identb", [P, P], BF16)
    mask0 = sb("mask0", [P, HPG, P], BF16)
    mask1 = sb("mask1", [P, 2, P], BF16)
    half = sb("half", [P, 2], F32)
    c_sb = sb("c_sb", [P, 2, D], F32)
    xn = sb("xn", [P, 2, D], F32)
    st1 = sb("st1", [P, 2, 6], F32)
    mv1 = sb("mv1", [P, 2, 2], F32)
    ve1 = sb("ve1", [P, 2], F32)
    rs1 = sb("rs1", [P, 2], F32)
    st2 = sb("st2", [P, 2, 6], F32)
    mv2 = sb("mv2", [P, 2, 2], F32)
    ve2 = sb("ve2", [P, 2], F32)
    rs2 = sb("rs2", [P, 2], F32)
    xT_hi = sb("xT_hi", [P, 2, S], F32R)
    xT_lo = sb("xT_lo", [P, 2, S], F32R)
    cT_hi = sb("cT_hi", [P, 2, S], F32R)
    cT_lo = sb("cT_lo", [P, 2, S], F32R)
    q_hi = sb("q_hi", [P, 2, S], F32R)
    q_lo = sb("q_lo", [P, 2, S], F32R)
    k_hi = sb("k_hi", [P, 2, S], F32R)
    k_lo = sb("k_lo", [P, 2, S], F32R)
    Qs = [sb(f"Qs{q}", [ROWS + 2, HEADS, S], F32R) for q in range(2)]
    Ks = [sb(f"Ks{q}", [ROWS + 2, HEADS, S], F32R) for q in range(2)]
    V = [sb(f"V{q}", [P, 2, HEADS, VW], F32) for q in range(2)]
    nm = sb("nm", [P, 2, HEADS], F32)
    nm_s = sb("nm_s", [P, 2, 2, HEADS], F32R)
    nmT = sb("nmT", [2 * HEADS, S], F32)
    PT = [sb(f"PT{g}", [P, HPG * (S + P)], F32) for g in range(2)]
    OT = sb("OT", [P, GROUPS, S], F32)
    rec = sb("rec", [P, 2, HEADS], F32)
    attn = sb("attn", [P, 2, HEADS, HD], F32)
    aT_hi = sb("aT_hi", [P, 2, S], F32R)
    aT_lo = sb("aT_lo", [P, 2, S], F32R)
    x2n = sb("x2n", [P, 2, D], F32)
    x2T = sb("x2T", [P, 2, S], F32)
    lg = sb("lg", [P, 2, EXPERTS], F32)
    top8 = sb("top8", [P, 2, 8], F32)
    idx8 = sb("idx8", [P, 2, 8], U32)

    x0_loaded, x_loaded = sem("x0_loaded"), sem("x_loaded")
    ctx_loaded = sem("ctx_loaded")
    wqkvo_loaded = [sem(f"w{n}_loaded") for n in "qkvo"]
    small_loaded = sem("small_loaded")
    const_tmp, const_ready, ones_ready = sem("const_tmp"), sem("const_ready"), sem("ones_ready")
    w_hi_ready, w_lo_ready = sem("w_hi_ready"), sem("w_lo_ready")
    ln1_stats, ln1_pow, xn_ready, xbo_ready = sem("ln1_stats"), sem("ln1_pow"), sem("xn_ready"), sem("xbo_ready")
    tx_done, tc_done = sem("tx_done"), sem("tc_done")
    xT_hi_ready, xT_lo_ready = sem("xT_hi_ready"), sem("xT_lo_ready")
    cT_hi_ready, cT_lo_ready = sem("cT_hi_ready"), sem("cT_lo_ready")
    q_done, k_done, v_done = sem("q_done"), sem("k_done"), sem("v_done")
    q_hi_ready, q_lo_ready = sem("q_hi_ready"), sem("q_lo_ready")
    k_hi_ready, k_lo_ready = sem("k_hi_ready"), sem("k_lo_ready")
    v_ready = sem("v_ready")
    q_stacked, k_stacked, max_stacked = sem("q_stacked"), sem("k_stacked"), sem("max_stacked")
    a_done, max_done, nm_ready, nmT_done, nmT_ready = (sem(n) for n in ("a_done", "max_done", "nm_ready", "nmT_done", "nmT_ready"))
    b_done, exp_done, mask_done, av_done, ot_ready = (sem(n) for n in ("b_done", "exp_done", "mask_done", "av_done", "ot_ready"))
    ott_done, rec_ready, norm_done = sem("ott_done"), sem("rec_ready"), sem("norm_done")
    at_done, aT_hi_ready, aT_lo_ready, op_done = sem("at_done"), sem("aT_hi_ready"), sem("aT_lo_ready"), sem("op_done")
    x2_ready, ln2_stats, ln2_pow, x2n_ready, x2n_stored = (sem(n) for n in ("x2_ready", "ln2_stats", "ln2_pow", "x2n_ready", "x2n_stored"))
    x2t_done, x2T_ready, rt_done, lg_ready, top_ready, top_used = (sem(n) for n in ("x2t_done", "x2T_ready", "rt_done", "lg_ready", "top_ready", "top_used"))
    y_zeroed, started = persist["y_zeroed"], persist["zeros_ready"]

    x_tiles = x.rearrange("b (t p) m -> p (b t) m", p=P)
    ctx_tiles = ctx_in.rearrange("b (t p) m -> b p t m", p=P)
    xn_tiles = xn_rows.rearrange("(b t p) m -> b p t m", t=2, p=P)

    def steps(eng, step):
        step(-1, 1, score_part=False, out_part=False)
        step(0, 0, out_part=False)
        with eng.Fori(0, (B - 2) // 2) as it:
            step(2 * it + 1, 1)
            step(2 * it + 2, 0)
        step(B - 1, (B - 1) % 2, proj_part=False)
        step(B, B % 2, score_part=False, proj_part=False)

    def weight_views(n, dst):
        if n >= 2:
            return [(dst[:, n].rearrange("p a b -> p (a b)"), w_raw[:, n].rearrange("p a b -> p (a b)"))]
        out = []
        for k in range(2):
            src = w_raw[:, n, k, :].rearrange("p (h f d) -> p f d h", f=2, d=HD)
            to = dst[:, n, k, :].rearrange("p (f d h) -> p f d h", f=2, d=HD)
            out += [(to[:, f], src[:, f]) for f in range(2)]
        return out

    block = nc.Block()
    with block:

        @block.sync
        def _(sp):
            sp.dma_start(x_all[:, 0:2, :], x_tiles[:, 0:2, :]).then_inc(x0_loaded, 16)
            sp.dma_start(w_raw[:, 0], Wq.rearrange("(k p) n -> p k n", p=P)).then_inc(wqkvo_loaded[0], 16)
            sp.dma_start(w_raw[:, 1], Wk.rearrange("(k p) n -> p k n", p=P)).then_inc(wqkvo_loaded[1], 16)
            sp.dma_start(w_raw[:, 2], Wv.rearrange("(k p) n -> p k n", p=P)).then_inc(wqkvo_loaded[2], 16)
            sp.dma_start(w_raw[:, 3], Wo.rearrange("(k p) n -> p k n", p=P)).then_inc(wqkvo_loaded[3], 16)
            sp.dma_start(x_all[:, 2:, :], x_tiles[:, 2:, :]).then_inc(x_loaded, 16)

            def stack(dst, row, src, done):
                sp.dma_start(dst[row:row + HD, :, :].rearrange("d (h f) t -> d h (f t)", f=2).bitcast(F32),
                             src[:, :, :].rearrange("p f t -> p (f t)").bitcast(F32)).then_inc(done, 16)

            def step(s, q, score_part=True, proj_part=True, out_part=True):
                if proj_part:
                    if not (isinstance(s, int) and s < 0):
                        wait_alone(sp, started, tc_done, s + 1)
                    sp.dma_start(c_sb[:, :, :], ctx_tiles[s + 1]).then_inc(ctx_loaded, 16)
                if score_part:
                    sp.wait_ge(nmT_ready, s + 1)
                    sp.dma_start(Qs[q][ROWS:ROWS + 2, :, :].bitcast(F32),
                                 nmT[:, :]).then_inc(max_stacked, 16)
                if proj_part:
                    r = 1 - q
                    if isinstance(s, int) and s < 1:
                        sp.wait_ge(ones_ready, 4)
                    else:
                        wait_alone(sp, started, b_done, GROUPS * s)
                    sp.wait_ge(q_hi_ready, s + 2)
                    stack(Qs[r], 0, q_hi, q_stacked)
                    stack(Qs[r], 2 * HD, q_hi, q_stacked)
                    sp.wait_ge(q_lo_ready, s + 2)
                    stack(Qs[r], HD, q_lo, q_stacked)
                    sp.wait_ge(k_hi_ready, s + 2)
                    stack(Ks[r], 0, k_hi, k_stacked)
                    stack(Ks[r], HD, k_hi, k_stacked)
                    sp.wait_ge(k_lo_ready, s + 2)
                    stack(Ks[r], 2 * HD, k_lo, k_stacked)
                if out_part:
                    wait_alone(sp, started, x2n_ready, 2 * s)
                    sp.dma_start(xn_tiles[s - 1], x2n[:, :, :]).then_inc(x2n_stored, 16)

            steps(sp, step)
            sp.wait_ge(x2n_stored, 16 * B)
            sp.wait_ge(y_zeroed, 16)

        @block.gpsimd
        def _(pool):
            pool.dma_start(bv_bc[:, :], bv.rearrange("(a n) -> a n", a=1).broadcast_to([P, D])).then_inc(small_loaded, 16)
            pool.dma_start(bo_bc[:, :], bo.rearrange("(a n) -> a n", a=1).broadcast_to([P, D])).then_inc(small_loaded, 16)
            pool.dma_start(wg_sb[:, :, :], wg.rearrange("(k p) e -> p k e", p=P)).then_inc(small_loaded, 16)
            pool.memset(ident[:, :], 1.0).then_inc(const_tmp, 1)
            pool.memset(identb[:, :], 1.0).then_inc(const_tmp, 1)
            pool.memset(mask0[:, :, :], 0.0).then_inc(const_tmp, 1)
            pool.memset(mask1[:, :, :], 0.0).then_inc(const_tmp, 1)
            pool.memset(half[:, :], -0.5).then_inc(const_ready, 1)
            pool.wait_ge(const_tmp, 4)
            pool.affine_select(ident[:, :], ident[:, :], [[-1, P]], ALU.is_equal, 0.0, base=0, channel_multiplier=1).then_inc(const_ready, 1)
            pool.affine_select(identb[:, :], identb[:, :], [[-1, P]], ALU.is_equal, 0.0, base=0, channel_multiplier=1).then_inc(const_ready, 1)
            pool.affine_select(mask1[:, :, :], mask1[:, :, :], [[0, 2], [-1, P]], ALU.is_gt, MASKED, base=0, channel_multiplier=1).then_inc(const_ready, 1)
            pool.affine_select(mask0[:, :, :], mask0[:, :, :], [[0, HPG], [-1, P]], ALU.is_gt, MASKED, base=0, channel_multiplier=1).then_inc(const_tmp, 1)
            pool.wait_ge(const_tmp, 5)
            pool.memset(mask0[0:1, :, 0:1], 0.0).then_inc(const_ready, 1)
            for q in range(2):
                pool.memset(Ks[q][:, :, :].bitcast(F32), 1.0).then_inc(ones_ready, 1)
                pool.memset(V[q][:, :, :, HD:], 0.0).then_inc(const_tmp, 1)
                pool.wait_ge(const_tmp, 6 + q)
                pool.memset(V[q][:, :, :, HD:HD + 1], 1.0).then_inc(ones_ready, 1)

            def powers(n, stats, mv, ve, rs, done):
                wait_alone(pool, started, stats, 4 * n + 4)
                pool.tensor_scalar(ve[:, :], mv[:, :, 1], EPS, None, ALU.add).then_inc(done, 1)
                pool.wait_ge(done, 2 * n + 1)
                pool.tensor_tensor(rs[:, :], ve[:, :], half[:, :], ALU.pow).then_inc(done, 1)

            def step(s, q, score_part=True, proj_part=True, out_part=True):
                if proj_part:
                    powers(s + 1, ln1_stats, mv1, ve1, rs1, ln1_pow)
                    pool.wait_ge(xn_ready, 2 * (s + 2))
                    if isinstance(s, int) and s < 0:
                        pool.wait_ge(small_loaded, 48)
                    xs = x_all[:, bass.ds(2 * (s + 1), 2), :]
                    pool.tensor_tensor(xs, xs, bo_bc[:, :].unsqueeze(1).broadcast_to([P, 2, D]), ALU.add).then_inc(xbo_ready, 1)
                if out_part:
                    powers(s - 1, ln2_stats, mv2, ve2, rs2, ln2_pow)
                if score_part:
                    for g in range(GROUPS):
                        wait_alone(pool, started, exp_done, GROUPS * s + g + 1)
                        p0 = PT[g % 2][:, 0:HPG * S].rearrange("p (h i) -> p h i", h=HPG)
                        p1 = PT[g % 2][:, HPG * S:].rearrange("p (h i) -> p h i", h=HPG)
                        pool.affine_select(p0[:, :, 0:1], p0[:, :, 0:1], [[0, HPG], [0, 1]], ALU.is_ge, 0.0, base=0, channel_multiplier=-1)
                        pool.affine_select(p0[:, :, 1:P], p0[:, :, 1:P], [[0, HPG], [1, P - 1]], ALU.is_gt, 0.0, base=1, channel_multiplier=-1).then_inc(mask_done, 1)
                        pool.affine_select(p1, p1, [[0, HPG], [1, P]], ALU.is_gt, 0.0, base=0, channel_multiplier=-1).then_inc(mask_done, 1)

            steps(pool, step)

        @block.scalar
        def _(act):
            act.wait_ge(persist["zeros_ready"], 1)
            act.dma_start(y_rows.rearrange("(p a) m -> p a m", p=P), zeros[:, :].unsqueeze(1).broadcast_to([P, y_rows.shape[0] // P, D])).then_inc(y_zeroed, 16)
            for e in range(2):
                act.dma_start(raw1[e][:, :, :], w1[e].rearrange("(k p) h -> p k h", p=P)).then_inc(weights_loaded[e], 16)
                act.dma_start(raw2[e][:, :, :], w2[e].rearrange("(p c) m -> p c m", p=P)).then_inc(weights_loaded[e], 16)
                act.dma_start(b1_sb[e][:, :], b1[e].rearrange("(p c) -> p c", p=P)).then_inc(biases_loaded[e], 16)
                act.dma_start(b2_bc[e][:, :], b2[e:e + 1, :].broadcast_to([P, D])).then_inc(biases_loaded[e], 16)
            for n in range(4):
                act.wait_ge(wqkvo_loaded[n], 16)
                for dst, src in weight_views(n, w_hi):
                    act.activation(dst, src, ACT.Copy).then_inc(w_hi_ready, 1)

            def step(s, q, score_part=True, proj_part=True, out_part=True):
                if out_part:
                    act.wait_ge(at_done, s)
                    if not (isinstance(s, int) and s < 2):
                        act.wait_ge(op_done, s - 1)
                    act.activation(aT_hi[:, :, :].rearrange("p a b -> p (a b)"), bank[0], ACT.Copy).then_inc(aT_hi_ready, 1)
                if score_part:
                    act.wait_ge(nmT_done, s + 1)
                    if not (isinstance(s, int) and s < 1):
                        act.wait_ge(max_stacked, 16 * s)
                    act.activation(nmT[:, :], bank[1][0:2 * HEADS, 0:S], ACT.Copy).then_inc(nmT_ready, 1)
                if proj_part:
                    act.wait_ge(tx_done, s + 2)
                    if not (isinstance(s, int) and s < 0):
                        act.wait_ge(q_done, s + 1)
                        act.wait_ge(v_done, s + 1)
                    act.activation(xT_hi[:, :, :].rearrange("p a b -> p (a b)"), bank[1], ACT.Copy).then_inc(xT_hi_ready, 1)
                    act.wait_ge(tc_done, s + 2)
                    act.activation(cT_hi[:, :, :].rearrange("p a b -> p (a b)"), bank[0], ACT.Copy).then_inc(cT_hi_ready, 1)
                    act.wait_ge(q_done, s + 2)
                    if not (isinstance(s, int) and s < 0):
                        act.wait_ge(q_stacked, 48 * (s + 1))
                    act.activation(q_hi[:, :, :].rearrange("p a b -> p (a b)"), bank[1], ACT.Copy).then_inc(q_hi_ready, 1)
                    act.wait_ge(k_done, s + 2)
                    if not (isinstance(s, int) and s < 0):
                        act.wait_ge(k_stacked, 48 * (s + 1))
                    act.activation(k_hi[:, :, :].rearrange("p a b -> p (a b)"), bank[0], ACT.Copy).then_inc(k_hi_ready, 1)

                def exp(g):
                    act.wait_ge(b_done, GROUPS * s + g + 1)
                    if g >= 2:
                        act.wait_ge(av_done, GROUPS * s + g - 1)
                    elif not (isinstance(s, int) and s < 1):
                        act.wait_ge(av_done, GROUPS * (s - 1) + g + 3)
                    act.activation(PT[g % 2][:, :], score[g % 2], ACT.Exp, scale=float(HD) ** -0.5).then_inc(exp_done, 1)

                def values(n):
                    act.wait_ge(av_done, GROUPS * s + 2 * n + 2)
                    if not (isinstance(s, int) and s < 1):
                        act.wait_ge(ott_done, 2 * s)
                    act.activation(OT[:, 2 * n:2 * n + 2, :].rearrange("p a b -> p (a b)"), bank[n], ACT.Copy).then_inc(ot_ready, 1)

                if score_part:
                    exp(0)
                if out_part:
                    act.wait_ge(x2t_done, s)
                    if not (isinstance(s, int) and s < 2):
                        act.wait_ge(rt_done, s - 1)
                    act.activation(x2T[:, :, :].rearrange("p a b -> p (a b)"), bank[0], ACT.Copy).then_inc(x2T_ready, 1)
                if score_part:
                    exp(1)
                    exp(2)
                    values(0)
                    exp(3)
                    values(1)

            steps(act, step)

        @block.vector
        def _(dve):
            dve.memset(zeros[:, :], 0.0).then_inc(persist["zeros_ready"], 1)

            def norm_stats(tiles, st, mv, stats, n):
                for t in range(2):
                    dve.bn_stats(st[:, t, :], tiles[:, t, :]).then_inc(stats, 1)
                wait_alone(dve, started, stats, 4 * n + 2)
                for t in range(2):
                    dve.bn_aggr(mv[:, t, :], st[:, t, :]).then_inc(stats, 1)

            def norm_apply(out, tiles, mv, rs, done):
                for t in range(2):
                    dve.tensor_scalar(out[:, t, :], tiles[:, t, :], mv[:, t, 0:1], rs[:, t:t + 1],
                                      ALU.subtract, ALU.mult).then_inc(done, 1)

            def split_weights():
                n_hi = 0
                for n in range(4):
                    for (lo, src), (hi, _) in zip(weight_views(n, w_lo), weight_views(n, w_hi)):
                        n_hi += 1
                        dve.wait_ge(w_hi_ready, n_hi)
                        dve.tensor_tensor(lo, src, hi.bitcast(F32), ALU.subtract).then_inc(w_lo_ready, 1)

            def split_lo(lo, hi, src, hi_ready, n, done):
                dve.wait_ge(hi_ready, n)
                dve.tensor_tensor(lo[:, :, :].rearrange("p a b -> p (a b)"), src,
                                  hi[:, :, :].rearrange("p a b -> p (a b)").bitcast(F32), ALU.subtract).then_inc(done, 1)

            def step(s, q, score_part=True, proj_part=True, out_part=True):
                r = 1 - q

                def maxima(g):
                    dve.wait_ge(a_done, GROUPS * s + g + 1)
                    h = slice(HPG * g, HPG * g + HPG)
                    dve.tensor_reduce(nm[:, 1, h], score[g % 2][:, 0:HPG * S].rearrange("p (h j) -> p h j", h=HPG),
                                      AX_X, ALU.max, negate=True)
                    dve.tensor_reduce(nm[:, 0, h], score[g % 2][:, HPG * S:].rearrange("p (h j) -> p h j", h=HPG),
                                      AX_X, ALU.max, negate=True).then_inc(max_done, 1)

                def normalise(t):
                    dve.wait_ge(ott_done, 2 * (s - 1) + t + 1)
                    heads = bank[t].rearrange("p (h c) -> p h c", c=VW)
                    dve.reciprocal(rec[:, t, :], heads[:, :, HD]).then_inc(rec_ready, 1)
                    dve.wait_ge(rec_ready, 2 * (s - 1) + t + 1)
                    if not (isinstance(s, int) and s < 2):
                        dve.wait_ge(at_done, s - 1)
                    dve.tensor_tensor(attn[:, t], heads[:, :, 0:HD], rec[:, t, :].unsqueeze(2).broadcast_to([P, HEADS, HD]),
                                      ALU.mult).then_inc(norm_done, 1)

                if proj_part:
                    if isinstance(s, int) and s < 1:
                        dve.wait_ge((x0_loaded, x_loaded)[s + 1], 16)
                    norm_stats(x_all[:, bass.ds(2 * (s + 1), 2), :], st1, mv1, ln1_stats, s + 1)
                if score_part:
                    if not (isinstance(s, int) and s < 1):
                        dve.wait_ge(nm_ready, 2 * s)
                    maxima(0)
                    maxima(1)
                if out_part:
                    normalise(0)
                if score_part:
                    maxima(2)
                if out_part:
                    normalise(1)
                if score_part:
                    maxima(3)
                    dve.wait_ge(max_done, GROUPS * s + GROUPS)
                    if not (isinstance(s, int) and s < 1):
                        dve.wait_ge(nmT_done, s)
                    dve.tensor_copy(nm_s[:, :, 0, :], nm[:, :, :]).then_inc(nm_ready, 1)
                    dve.wait_ge(nm_ready, 2 * s + 1)
                    dve.tensor_tensor(nm_s[:, :, 1, :], nm[:, :, :], nm_s[:, :, 0, :].bitcast(F32), ALU.subtract).then_inc(nm_ready, 1)
                if proj_part:
                    dve.wait_ge(ln1_pow, 2 * (s + 2))
                    if not (isinstance(s, int) and s < 0):
                        dve.wait_ge(tx_done, s + 1)
                    norm_apply(xn, x_all[:, bass.ds(2 * (s + 1), 2), :], mv1, rs1, xn_ready)
                    if isinstance(s, int) and s < 0:
                        split_weights()
                if out_part:
                    split_lo(aT_lo, aT_hi, bank[0], aT_hi_ready, s, aT_lo_ready)
                    x2 = x_all[:, bass.ds(2 * (s - 1), 2), :]
                    dve.wait_ge(op_done, s)
                    dve.wait_ge(xbo_ready, s)
                    dve.tensor_tensor(x2, bank[0].rearrange("p (t m) -> p t m", t=2), x2, ALU.add).then_inc(x2_ready, 1)
                    wait_alone(dve, started, x2_ready, s)
                    norm_stats(x2, st2, mv2, ln2_stats, s - 1)
                if proj_part:
                    split_lo(xT_lo, xT_hi, bank[1], xT_hi_ready, s + 2, xT_lo_ready)
                    split_lo(cT_lo, cT_hi, bank[0], cT_hi_ready, s + 2, cT_lo_ready)
                if out_part:
                    dve.wait_ge(ln2_pow, 2 * s)
                    if not (isinstance(s, int) and s < 2):
                        dve.wait_ge(x2n_stored, 16 * (s - 1))
                        dve.wait_ge(x2t_done, s - 1)
                    norm_apply(x2n, x2, mv2, rs2, x2n_ready)
                if proj_part:
                    split_lo(q_lo, q_hi, bank[1], q_hi_ready, s + 2, q_lo_ready)
                    split_lo(k_lo, k_hi, bank[0], k_hi_ready, s + 2, k_lo_ready)
                    dve.wait_ge(v_done, s + 2)
                    if isinstance(s, int) and s < 1:
                        dve.wait_ge(ones_ready, 4)
                        dve.wait_ge(small_loaded, 48)
                    else:
                        dve.wait_ge(av_done, GROUPS * s)
                    dve.tensor_tensor(V[r][:, :, :, 0:HD],
                                      bank[1].rearrange("p (t h d) -> p t h d", t=2, h=HEADS),
                                      bv_bc[:, :].rearrange("p (h d) -> p h d", h=HEADS).unsqueeze(1).broadcast_to([P, 2, HEADS, HD]),
                                      ALU.add).then_inc(v_ready, 1)
                if out_part:
                    dve.wait_ge(rt_done, s)
                    dve.tensor_copy(lg[:, :, :], bank[1][:, 0:2 * EXPERTS].rearrange("p (t e) -> p t e", t=2)).then_inc(lg_ready, 1)
                    wait_alone(dve, started, lg_ready, s)
                    for t in range(2):
                        dve.max(top8[:, t, :], lg[:, t, :]).then_inc(top_ready, 1)
                    wait_alone(dve, started, top_ready, 4 * (s - 1) + 2)
                    for t in range(2):
                        dve.max_index(idx8[:, t, :], top8[:, t, :], lg[:, t, :]).then_inc(top_ready, 1)
                    dve.tensor_tensor(dl_all[:, bass.ds(2 * (s - 1), 2)], top8[:, :, 1], top8[:, :, 0], ALU.subtract).then_inc(top_used, 1)
                    dve.wait_ge(top_ready, 4 * (s - 1) + 4)
                    for k in range(TOPK):
                        dve.tensor_copy(expert_all[:, k, bass.ds(2 * (s - 1), 2)], idx8[:, :, k]).then_inc(top_used, 1)

            steps(dve, step)
            dve.wait_ge(top_used, 3 * B)

        @block.tensor
        def _(pe):
            def split_product(out, parts, halves, first=True):
                n = 0
                for k in range(halves):
                    for a, b in ((0, 0), (1, 0), (0, 1)):
                        n += 1
                        last = pe.matmul(out, parts[0][a](k), parts[1][b](k), start=(n == 1), stop=(n == 3 * halves))
                return last

            def transposes(dst, srcs):
                for to, src in zip(dst, srcs):
                    last = pe.transpose(to, src, ident[:, :])
                return last

            def step(s, q, score_part=True, proj_part=True, out_part=True):
                r = 1 - q

                def a_scores(g):
                    sc = score[g % 2]
                    if g == 0 and isinstance(s, int) and s == 0:
                        pe.wait_ge(const_ready, 5)
                    if g == 0:
                        pe.wait_ge(q_stacked, 48 * (s + 1))
                        pe.wait_ge(k_stacked, 48 * (s + 1))
                    if g >= 2:
                        pe.wait_ge(max_done, GROUPS * s + g - 1)
                    elif not (isinstance(s, int) and s < 1):
                        pe.wait_ge(exp_done, GROUPS * (s - 1) + g + 3)
                    for pair in range(2):
                        for o in range(2):
                            hh = 2 * pair + o
                            h = HPG * g + hh
                            pe.matmul(sc[:, hh * S:(hh + 1) * S], Qs[q][0:ROWS, h, P:S], Ks[q][0:ROWS, h, :],
                                      start=(o == 0), stop=False, skip_group_check=True)
                        diag = sc[:, 2 * pair * S:(2 * pair + 2) * S].rearrange("p (h j) -> p h j", h=2)[:, :, P:S]
                        pe.matmul(diag, identb[:, :], mask1[:, :, :], start=False, stop=True, skip_group_check=True)
                    for hh in range(HPG):
                        h = HPG * g + hh
                        pe.matmul(sc[:, HPG * S + hh * P:HPG * S + (hh + 1) * P], Qs[q][0:ROWS, h, 0:P], Ks[q][0:ROWS, h, 0:P],
                                  start=(hh == 0), stop=False, skip_group_check=True)
                    pe.matmul(sc[:, HPG * S:], identb[:, :], mask0[:, :, :].rearrange("p h j -> p (h j)"),
                              start=False, stop=True, skip_group_check=True).then_inc(a_done, 1)

                def b_scores(g):
                    sc = score[g % 2]
                    if g == 0:
                        pe.wait_ge(max_stacked, 16 * (s + 1))
                    if g < 2:
                        pe.wait_ge(max_done, GROUPS * s + g + 3)
                    else:
                        pe.wait_ge(exp_done, GROUPS * s + g - 1)
                    for hh in range(HPG):
                        h = HPG * g + hh
                        pe.matmul(sc[:, hh * S:(hh + 1) * S], Ks[q][:, h, 0:P], Qs[q][:, h, :], start=True, stop=True)
                    for hh in range(HPG):
                        h = HPG * g + hh
                        last = pe.matmul(sc[:, HPG * S + hh * P:HPG * S + (hh + 1) * P], Ks[q][:, h, P:S], Qs[q][:, h, P:S],
                                         start=True, stop=True)
                    last.then_inc(b_done, 1)

                def values(g):
                    pe.wait_ge(mask_done, 2 * (GROUPS * s + g + 1))
                    if g == 0:
                        pe.wait_ge(v_ready, s + 1)
                    for hh in range(HPG):
                        h = HPG * g + hh
                        out = bank[g // 2][VW * hh:VW * hh + VW, (g % 2) * S:(g % 2) * S + S]
                        pe.matmul(out, V[q][:, 0, h, :], PT[g % 2][:, hh * S:(hh + 1) * S], start=True, stop=False)
                        last = pe.matmul(out[:, P:S], V[q][:, 1, h, :], PT[g % 2][:, HPG * S + hh * P:HPG * S + (hh + 1) * P],
                                         start=False, stop=True)
                    last.then_inc(av_done, 1)

                def turn_values(t):
                    pe.wait_ge(ot_ready, 2 * s)
                    for g in range(GROUPS):
                        last = pe.transpose(bank[t][:, g * P:(g + 1) * P], OT[:, g, t * P:(t + 1) * P], ident[:, :])
                    last.then_inc(ott_done, 1)

                if score_part:
                    a_scores(0)
                    a_scores(1)
                if out_part:
                    turn_values(0)
                if score_part:
                    a_scores(2)
                if out_part:
                    turn_values(1)
                if score_part:
                    a_scores(3)
                if out_part:
                    pe.wait_ge(norm_done, 2 * s)
                    for k in range(2):
                        for t in range(2):
                            last = pe.transpose(bank[0][:, k * S + t * P:k * S + (t + 1) * P],
                                                attn[:, t].rearrange("p h d -> p (h d)")[:, k * P:(k + 1) * P], ident[:, :])
                    last.then_inc(at_done, 1)
                if score_part:
                    pe.wait_ge(nm_ready, 2 * (s + 1))
                    if isinstance(s, int) and s == 0:
                        pe.wait_ge(v_ready, 1)
                    for t in range(2):
                        last = pe.transpose(bank[1][0:2 * HEADS, t * P:(t + 1) * P],
                                            nm_s[:, t].rearrange("p a h -> p (a h)").bitcast(F32), ident[:, :])
                    last.then_inc(nmT_done, 1)
                if out_part:
                    pe.wait_ge(aT_lo_ready, s)
                    for t in range(2):
                        n = 0
                        for k in range(2):
                            for a, w in ((aT_hi, w_hi), (aT_lo, w_hi), (aT_hi, w_lo)):
                                n += 1
                                last = pe.matmul(bank[0][:, t * D:(t + 1) * D], a[:, k, t * P:(t + 1) * P], w[:, 3, k, :],
                                                 start=(n == 1), stop=(n == 6))
                    last.then_inc(op_done, 1)
                if proj_part:
                    pe.wait_ge(xn_ready, 2 * (s + 2))
                    if score_part:
                        pe.wait_ge(nmT_ready, s + 1)
                    else:
                        pe.wait_ge(const_ready, 5)
                    for k in range(2):
                        for t in range(2):
                            last = pe.transpose(bank[1][:, k * S + t * P:k * S + (t + 1) * P], xn[:, t, k * P:(k + 1) * P], ident[:, :])
                    last.then_inc(tx_done, 1)
                    pe.wait_ge(ctx_loaded, 16 * (s + 2))
                    if out_part:
                        pe.wait_ge(x2_ready, s)
                    elif score_part:
                        pe.wait_ge(k_lo_ready, 1)
                    for k in range(2):
                        for t in range(2):
                            last = pe.transpose(bank[0][:, k * S + t * P:k * S + (t + 1) * P], c_sb[:, t, k * P:(k + 1) * P], ident[:, :])
                    last.then_inc(tc_done, 1)

                    def project(n, out, hi, lo, done):
                        for f in range(2):
                            m = 0
                            for k in range(2):
                                for w, a in ((w_hi, hi), (w_lo, hi), (w_hi, lo)):
                                    m += 1
                                    last = pe.matmul(out[:, f * S:(f + 1) * S], w[:, n, k, f * P:(f + 1) * P], a[:, k, :],
                                                     start=(m == 1), stop=(m == 6))
                        last.then_inc(done, 1)

                    if isinstance(s, int) and s < 0:
                        pe.wait_ge(w_lo_ready, 10)
                    pe.wait_ge(xT_lo_ready, s + 2)
                    project(0, bank[1], xT_hi, xT_lo, q_done)
                    pe.wait_ge(cT_lo_ready, s + 2)
                    project(1, bank[0], cT_hi, cT_lo, k_done)
                if score_part:
                    b_scores(0)
                if proj_part:
                    pe.wait_ge(q_lo_ready, s + 2)
                    for t in range(2):
                        n = 0
                        for k in range(2):
                            for a, w in ((cT_hi, w_hi), (cT_lo, w_hi), (cT_hi, w_lo)):
                                n += 1
                                last = pe.matmul(bank[1][:, t * D:(t + 1) * D], a[:, k, t * P:(t + 1) * P], w[:, 2, k, :],
                                                 start=(n == 1), stop=(n == 6))
                    last.then_inc(v_done, 1)
                if out_part:
                    pe.wait_ge(x2n_ready, 2 * s)
                    if proj_part:
                        pe.wait_ge(k_lo_ready, s + 2)
                    for k in range(2):
                        for t in range(2):
                            last = pe.transpose(bank[0][:, k * S + t * P:k * S + (t + 1) * P], x2n[:, t, k * P:(k + 1) * P], ident[:, :])
                    last.then_inc(x2t_done, 1)
                if score_part:
                    b_scores(1)
                if out_part:
                    pe.wait_ge(x2T_ready, s)
                    if isinstance(s, int) and s < 2:
                        pe.wait_ge(small_loaded, 48)
                    if proj_part:
                        pe.wait_ge(v_ready, s + 2)
                    elif score_part:
                        pe.wait_ge(nmT_ready, s + 1)
                    for t in range(2):
                        for k in range(2):
                            last = pe.matmul(bank[1][:, t * EXPERTS:(t + 1) * EXPERTS], x2T[:, k, t * P:(t + 1) * P],
                                             wg_sb[:, k, :], start=(k == 0), stop=(k == 1))
                    last.then_inc(rt_done, 1)
                if score_part:
                    if not out_part:
                        pe.wait_ge(k_lo_ready, 2)
                    values(0)
                    b_scores(2)
                    values(1)
                    b_scores(3)
                    if out_part:
                        pe.wait_ge(lg_ready, s)
                    else:
                        pe.wait_ge(v_ready, s + 2)
                    values(2)
                    values(3)

            steps(pe, step)


def experts(nc, sem, sb, persist, out, w1, b1, w2, b2, xn_rows, y_rows):
    E, D, H = w1.shape
    T = xn_rows.shape[0]
    TILES = T // P
    KT = TOPK * TILES
    CAP = TOPK * T // E
    ST = CAP // P
    SLOTS = E * ST
    C = H // P
    x_all, ident, dl_all, expert_all, ps = (persist[k] for k in ("x_all", "ident", "dl_all", "expert_all", "ps"))
    raw1, raw2, b1_sb, b2_bc = (persist[k] for k in ("raw1", "raw2", "b1_sb", "b2_bc"))
    weights_loaded, biases_loaded, y_zeroed, started = (persist[k] for k in ("weights_loaded", "biases_loaded", "y_zeroed", "zeros_ready"))

    tri = sb("tri", [P, P], BF16)
    onesb = sb("onesb", [P, P], BF16)
    iota_e = sb("iota_e", [P, E], F32)
    iota_s = sb("iota_s", [P, P], BF16)
    iota_g = sb("iota_g", [P, SLOTS], F32)
    iota_k = sb("iota_k", [P, KT], F32)
    iota_p = sb("iota_p", [P, 1], F32)
    carry = sb("carry", [P, E, KT], F32)
    onehot = sb("onehot", [P, E, KT], BF16)
    base = sb("base", [P, E, KT], F32)
    pos = sb("pos", [P, KT], F32)
    c3 = sb("c3", [P, KT], F32)
    spart = sb("spart", [P, KT], F32)
    grp = sb("grp", [P, KT], F32)
    in_slot = sb("in_slot", [P, KT, P], BF16)
    in_tile = sb("in_tile", [P, KT, 2, SLOTS], BF16)
    eq = sb("eq", [P, KT, SLOTS], BF16)
    row = sb("row", [P, SLOTS], F32)
    adj = sb("adj", [P, SLOTS], F32)
    from_row = sb("from_row", [P, SLOTS], F32)
    to_row = sb("to_row", [P, SLOTS], F32)
    ratio = sb("ratio", [P, TILES], F32)
    den = sb("den", [P, TILES], F32)
    gates = sb("gates", [P, TOPK, TILES], F32)
    gather_idx = [sb(f"gather_idx{q}", [P, ST], I32) for q in range(2)]
    scatter_idx = [sb(f"scatter_idx{q}", [P, ST], I32) for q in range(2)]
    w1_hi = [sb(f"w1_hi{q}", [P, 2, C, P], F32R) for q in range(2)]
    w1_lo = [sb(f"w1_lo{q}", [P, 2, C, P], F32R) for q in range(2)]
    w2_hi = [sb(f"w2_hi{q}", [P, C, D], F32R) for q in range(2)]
    w2_lo = [sb(f"w2_lo{q}", [P, C, D], F32R) for q in range(2)]
    Xg = [sb(f"Xg{q}", [P, ST, D], F32) for q in range(2)]
    XT_hi = [sb(f"XT_hi{q}", [P, 2, CAP], F32R) for q in range(2)]
    XT_lo = [sb(f"XT_lo{q}", [P, 2, CAP], F32R) for q in range(2)]
    hr = [sb(f"hr{c}", [P, CAP], F32) for c in range(2)]
    h_hi = [sb(f"h_hi{c}", [P, CAP], F32R) for c in range(4)]
    h_lo = [sb(f"h_lo{c}", [P, CAP], F32R) for c in range(4)]
    Y = [sb(f"Y{q}", [P, ST, D], F32) for q in range(2)]
    YC = [sb(f"YC{q}", [P, TOPK, 2, D], F32) for q in range(2)]

    consts2, step_ready = sem("consts2"), sem("step_ready")
    counted, placed_a, placed_b, table_done = sem("counted"), sem("placed_a"), sem("placed_b"), sem("table_done")
    rows_ready, ratio_ready, gates_ready = sem("rows_ready"), sem("ratio_ready"), sem("gates_ready")
    gidx_ready, sidx_ready = sem("gidx_ready"), sem("sidx_ready")
    gathered = [sem(f"gathered{q}") for q in range(2)]
    scattered = [sem(f"scattered{q}") for q in range(2)]
    xt_done, xt_hi_ready, xt_lo_ready = sem("xt_done"), sem("xt_hi_ready"), sem("xt_lo_ready")
    wh_ready, wl_ready = sem("wh_ready"), sem("wl_ready")
    h_done, hr_ready, hh_ready, hl_ready = sem("h_done"), sem("hr_ready"), sem("hh_ready"), sem("hl_ready")
    f2_part, y_ready = sem("f2_part"), sem("y_ready")
    yc_loaded = [sem(f"yc_loaded{q}") for q in range(2)]
    sum_a, sum_ready, stored = sem("sum_a"), sem("sum_ready"), sem("stored")

    xt_bank = ps[:, 0:2, :]
    h_bank = [ps[:, 2, :], ps[:, 3, :], ps[:, 4, :], ps[:, 7, :]]
    y_bank = [ps[:, 5, :], ps[:, 6, :]]
    out_tiles = out.rearrange("b (t p) m -> p (b t) m", p=P)
    y_tiles = y_rows.rearrange("(k t p) m -> p k t m", k=TOPK, p=P)
    CH = 2

    def steps(step):
        def run(eng):
            step(0, 0, 0)
            step(1, 1, 0)
            with eng.Fori(1, E // 2 - 1) as it:
                step(2 * it, 0, it)
                step(2 * it + 1, 1, it)
            step(E - 2, 0, E // 2 - 1)
            step(E - 1, 1, E // 2 - 1)
        return run

    def static(e, n):
        return isinstance(e, int) and e >= n

    block = nc.Block()
    with block:

        @block.sync
        def _(sp):
            def step(e, q, it):
                if static(e, E - 2):
                    return
                sp.wait_ge(wh_ready, 4 * (e + 1))
                wait_alone(sp, started, wl_ready, 4 * (e + 1))
                sp.dma_start(raw1[q][:, :, :], w1[e + 2].rearrange("(k p) h -> p k h", p=P)).then_inc(weights_loaded[q], 16)
                sp.dma_start(raw2[q][:, :, :], w2[e + 2].rearrange("(p c) m -> p c m", p=P)).then_inc(weights_loaded[q], 16)
                wait_alone(sp, started, hr_ready, C * (e + 1))
                sp.dma_start(b1_sb[q][:, :], b1[e + 2].rearrange("(p c) -> p c", p=P)).then_inc(biases_loaded[q], 16)
                wait_alone(sp, started, y_ready, 2 * (e + 1))
                sp.dma_start(b2_bc[q][:, :], b2[bass.ds(e + 2, 1), :].broadcast_to([P, D])).then_inc(biases_loaded[q], 16)

            steps(step)(sp)
            for q in range(2):
                sp.wait_ge(scattered[q], 16 * ST * (E // 2))
            for n in range(TILES // CH):
                if n >= 2:
                    sp.wait_ge(sum_ready, CH * (n - 1))
                for k in range(TOPK):
                    sp.dma_start(YC[n % 2][:, k], y_tiles[:, k, CH * n:CH * n + CH, :]).then_inc(yc_loaded[n % 2], 16)

        @block.gpsimd
        def _(pool):
            pool.memset(tri[:, :], 1.0).then_inc(step_ready, 1)
            pool.memset(onesb[:, :], 1.0).then_inc(consts2, 1)
            pool.memset(carry[:, :, :], 1.0).then_inc(step_ready, 1)
            pool.iota(iota_e[:, :], [[1, E]], base=0, channel_multiplier=0, allow_small_or_imprecise_dtypes=True).then_inc(consts2, 1)
            pool.iota(iota_s[:, :], [[1, P]], base=0, channel_multiplier=0, allow_small_or_imprecise_dtypes=True).then_inc(consts2, 1)
            pool.iota(iota_g[:, :], [[1, SLOTS]], base=0, channel_multiplier=0, allow_small_or_imprecise_dtypes=True).then_inc(consts2, 1)
            pool.iota(iota_k[:, :], [[1, KT]], base=1, channel_multiplier=0, allow_small_or_imprecise_dtypes=True).then_inc(consts2, 1)
            pool.iota(iota_p[:, :], [[1, 1]], base=0, channel_multiplier=1, allow_small_or_imprecise_dtypes=True).then_inc(consts2, 1)
            pool.wait_ge(step_ready, 2)
            pool.affine_select(tri[:, :], tri[:, :], [[1, P]], ALU.is_gt, 0.0, base=0, channel_multiplier=-1).then_inc(consts2, 1)
            pool.memset(carry[:, :, 0:1], 0.0).then_inc(consts2, 1)
            pool.wait_ge(y_zeroed, 16)

            def gather(e, q):
                wait_alone(pool, started, gidx_ready, e + 1)
                if not (isinstance(e, int) and e < 2):
                    wait_alone(pool, started, xt_done, e - 1)
                for j in range(ST):
                    pool.indirect_dma_start(Xg[q][:, j, :], None, xn_rows[:, :],
                                            bass.IndirectOffsetOnAxis(ap=gather_idx[q][:, j:j + 1], axis=0)).then_inc(gathered[q], 16)

            def step(e, q, it):
                if not static(e, E - 2):
                    gather(e + 2, q)
                pool.wait_ge(sidx_ready, e + 1)
                wait_alone(pool, started, y_ready, 2 * e + 2)
                for j in range(ST):
                    pool.indirect_dma_start(y_rows[:, :], bass.IndirectOffsetOnAxis(ap=scatter_idx[q][:, j:j + 1], axis=0),
                                            Y[q][:, j, :], None, bounds_check=TOPK * T - 1, oob_is_err=False).then_inc(scattered[q], 16)

            gather(0, 0)
            gather(1, 1)
            steps(step)(pool)

        @block.scalar
        def _(act):
            act.activation(ratio[:, :], dl_all[:, :], ACT.Exp).then_inc(ratio_ready, 1)

            def split_weights(e, q, it):
                act.wait_ge(weights_loaded[q], 32 * (it + 1))
                if not (isinstance(e, int) and e < 2):
                    act.wait_ge(f2_part, C * (e - 1))
                for k in range(2):
                    act.activation(w1_hi[q][:, k].rearrange("p c j -> p j c"), raw1[q][:, k, :].rearrange("p (j c) -> p j c", c=C), ACT.Copy).then_inc(wh_ready, 1)
                for k in range(2):
                    act.activation(w2_hi[q][:, 4 * k:4 * k + 4], raw2[q][:, 4 * k:4 * k + 4], ACT.Copy).then_inc(wh_ready, 1)

            def turn_rows(e, q):
                act.wait_ge(xt_done, e + 1)
                if not (isinstance(e, int) and e < 2):
                    act.wait_ge(h_done, C * (e - 1))
                for k in range(2):
                    act.activation(XT_hi[q][:, k, :], xt_bank[:, k, :], ACT.Copy).then_inc(xt_hi_ready, 1)

            def step(e, q, it):
                act.wait_ge(biases_loaded[q], 32 * (it + 1))
                for c in range(C):
                    act.wait_ge(h_done, C * e + c + 1)
                    if c >= 2:
                        act.wait_ge(hl_ready, C * e + c - 1)
                    elif not (isinstance(e, int) and e < 1):
                        act.wait_ge(hl_ready, C * e + c - 1)
                    act.activation(hr[c % 2][:, :], h_bank[c % 4], ACT.Relu, bias=b1_sb[q][:, c:c + 1]).then_inc(hr_ready, 1)
                    if c == 1 and not static(e, E - 1):
                        split_weights(e + 1, 1 - q, it + q)
                if not static(e, E - 1):
                    turn_rows(e + 1, 1 - q)

            split_weights(0, 0, 0)
            turn_rows(0, 0)
            steps(step)(act)
            for n in range(TILES // CH):
                act.wait_ge(sum_ready, CH * (n + 1))
                act.dma_start(out_tiles[:, CH * n:CH * n + CH, :], x_all[:, CH * n:CH * n + CH, :]).then_inc(stored, 16)
            act.wait_ge(stored, 16 * (TILES // CH))

        @block.vector
        def _(dve):
            chain = [0]

            def then(ins):
                chain[0] += 1
                ins.then_inc(placed_a, 1)
                dve.wait_ge(placed_a, chain[0])

            queue = expert_all[:, :, :].rearrange("p k t -> p (k t)")
            dve.wait_ge(consts2, 8)
            then(dve.tensor_tensor(onehot[:, :, :], queue.unsqueeze(1).broadcast_to([P, E, KT]),
                                   iota_e[:, :].unsqueeze(2).broadcast_to([P, E, KT]), ALU.is_equal))
            dve.wait_ge(counted, 1)
            before = ps[:, 0, 0:E * KT]
            total = ps[:, 0, E * KT:2 * E * KT]
            flat = base[:, :, :].rearrange("p e n -> p (e n)")
            then(dve.tensor_tensor_scan(flat, carry[:, :, :].rearrange("p e n -> p (e n)"), total, 0.0, ALU.mult, ALU.add))
            then(dve.tensor_tensor(flat, flat, total, ALU.subtract))
            then(dve.tensor_tensor(flat, flat, before, ALU.add))
            then(dve.tensor_tensor(flat, flat, onehot[:, :, :].rearrange("p e n -> p (e n)"), ALU.mult))
            then(dve.tensor_reduce(pos[:, :], base[:, :, :].rearrange("p e n -> p n e"), AX_X, ALU.add))
            then(dve.tensor_scalar(c3[:, :], pos[:, :], float(P), None, ALU.is_ge))
            for n in range(2, ST):
                then(dve.scalar_tensor_tensor(c3[:, :], pos[:, :], float(n * P), c3[:, :], ALU.is_ge, ALU.add))
            then(dve.scalar_tensor_tensor(spart[:, :], c3[:, :], -float(P), pos[:, :], ALU.mult, ALU.add))
            then(dve.scalar_tensor_tensor(grp[:, :], queue, float(ST), c3[:, :], ALU.mult, ALU.add))
            then(dve.tensor_tensor(eq[:, :, :], grp[:, :].unsqueeze(2).broadcast_to([P, KT, SLOTS]),
                                   iota_g[:, :].unsqueeze(1).broadcast_to([P, KT, SLOTS]), ALU.is_equal))
            dve.tensor_scalar(in_tile[:, :, 0, :], eq[:, :, :], iota_p[:, 0:1], None, ALU.mult).then_inc(placed_b, 1)
            dve.tensor_tensor(in_tile[:, :, 1, :], eq[:, :, :], iota_k[:, :].unsqueeze(2).broadcast_to([P, KT, SLOTS]),
                              ALU.mult).then_inc(placed_b, 1)
            for n in range(KT // 8):
                dve.tensor_tensor(in_slot[:, 8 * n:8 * n + 8, :], spart[:, 8 * n:8 * n + 8].unsqueeze(2).broadcast_to([P, 8, P]),
                                  iota_s[:, :].unsqueeze(1).broadcast_to([P, 8, P]), ALU.is_equal).then_inc(placed_b, 1)
            dve.wait_ge(ratio_ready, 1)
            then(dve.tensor_scalar(den[:, :], ratio[:, :], 1.0, None, ALU.add))
            then(dve.reciprocal(gates[:, 0, :], den[:, :]))
            then(dve.tensor_tensor(gates[:, 1, :], gates[:, 0, :], ratio[:, :], ALU.mult))
            gflat = gates[:, :, :].rearrange("p k t -> p (k t)")
            then(dve.scalar_tensor_tensor(gflat, pos[:, :], float(CAP), gflat, ALU.is_lt, ALU.mult))
            dve.wait_ge(table_done, 1)
            then(dve.tensor_scalar(row[:, :], ps[:, 1, SLOTS:2 * SLOTS], float(P), -float(P), ALU.mult, ALU.add))
            then(dve.tensor_tensor(row[:, :], row[:, :], ps[:, 1, 0:SLOTS], ALU.add))
            then(dve.tensor_scalar(adj[:, :], row[:, :], float(T), -float(T), ALU.is_ge, ALU.mult))
            then(dve.tensor_tensor(from_row[:, :], row[:, :], adj[:, :], ALU.add))
            then(dve.tensor_scalar(from_row[:, :], from_row[:, :], 0.0, None, ALU.max))
            then(dve.tensor_scalar(adj[:, :], row[:, :], 0.0, 1e6, ALU.is_lt, ALU.mult))
            then(dve.tensor_tensor(to_row[:, :], row[:, :], adj[:, :], ALU.add))

            def scatter_rows(e, q, it):
                if not (isinstance(e, int) and e < 2):
                    dve.wait_ge(scattered[q], 16 * ST * it)
                dve.tensor_copy(scatter_idx[q][:, :], to_row[:, bass.ds(ST * e, ST)]).then_inc(sidx_ready, 1)

            def weights_part(e, q, n):
                dve.wait_ge(wh_ready, 4 * e + n + 1)
                if n < 2:
                    dve.tensor_tensor(w1_lo[q][:, n].rearrange("p c j -> p j c"), raw1[q][:, n, :].rearrange("p (j c) -> p j c", c=C),
                                      w1_hi[q][:, n].rearrange("p c j -> p j c").bitcast(F32), ALU.subtract).then_inc(wl_ready, 1)
                else:
                    k = n - 2
                    dve.tensor_tensor(w2_lo[q][:, 4 * k:4 * k + 4], raw2[q][:, 4 * k:4 * k + 4],
                                      w2_hi[q][:, 4 * k:4 * k + 4].bitcast(F32), ALU.subtract).then_inc(wl_ready, 1)

            def turn_rows(e, q):
                for k in range(2):
                    dve.wait_ge(xt_hi_ready, 2 * e + k + 1)
                    dve.tensor_tensor(XT_lo[q][:, k, :], xt_bank[:, k, :], XT_hi[q][:, k, :].bitcast(F32), ALU.subtract).then_inc(xt_lo_ready, 1)

            def step(e, q, it):
                if not static(e, E - 2):
                    dve.wait_ge(gathered[q], 16 * ST * (it + 1))
                    dve.tensor_copy(gather_idx[q][:, :], from_row[:, bass.ds(ST * (e + 2), ST)]).then_inc(gidx_ready, 1)
                for c in range(C):
                    dve.wait_ge(hr_ready, C * e + c + 1)
                    if not (isinstance(e, int) and e < 1 and c < 4):
                        dve.wait_ge(f2_part, C * e + c - 3)
                    dve.tensor_copy(h_hi[c % 4][:, :], hr[c % 2][:, :]).then_inc(hh_ready, 1)
                    dve.wait_ge(hh_ready, C * e + c + 1)
                    dve.tensor_tensor(h_lo[c % 4][:, :], hr[c % 2][:, :], h_hi[c % 4][:, :].bitcast(F32), ALU.subtract).then_inc(hl_ready, 1)
                    if c % 2 and not static(e, E - 1):
                        weights_part(e + 1, 1 - q, c // 2)
                if not static(e, E - 1):
                    turn_rows(e + 1, 1 - q)
                scatter_rows(e, q, it)
                dve.wait_ge(f2_part, C * (e + 1))
                for n in range(2):
                    dve.tensor_tensor(Y[q][:, 2 * n:2 * n + 2, :], y_bank[n].rearrange("p (j m) -> p j m", j=2),
                                      b2_bc[q][:, :].unsqueeze(1).broadcast_to([P, 2, D]), ALU.add).then_inc(y_ready, 1)

            for e in range(2):
                dve.tensor_copy(gather_idx[e][:, :], from_row[:, ST * e:ST * e + ST]).then_inc(gidx_ready, 1)
            for n in range(4):
                weights_part(0, 0, n)
            turn_rows(0, 0)
            steps(step)(dve)

            for n in range(TILES // CH):
                dve.wait_ge(yc_loaded[n % 2], 16 * TOPK * (n // 2 + 1))
                for k in range(TOPK):
                    for j in range(CH):
                        t = CH * n + j
                        if k:
                            dve.wait_ge(sum_a, t + 1)
                        ins = dve.scalar_tensor_tensor(x_all[:, t, :], YC[n % 2][:, k, j, :], gates[:, k, t:t + 1],
                                                       x_all[:, t, :], ALU.mult, ALU.add)
                        ins.then_inc(sum_ready if k else sum_a, 1)

        @block.tensor
        def _(pe):
            pe.wait_ge(placed_a, 1)
            pe.wait_ge(consts2, 8)
            oh = onehot[:, :, :].rearrange("p e n -> p (e n)")
            pe.matmul(ps[:, 0, 0:E * KT], tri[:, :], oh, start=True, stop=True)
            pe.matmul(ps[:, 0, E * KT:2 * E * KT], onesb[:, :], oh, start=True, stop=True).then_inc(counted, 1)
            for n in range(KT):
                if n % 8 == 0:
                    pe.wait_ge(placed_b, 3 + n // 8)
                last = pe.matmul(ps[:, 1, 0:2 * SLOTS], in_slot[:, n, :], in_tile[:, n].rearrange("p a g -> p (a g)"),
                                 start=(n == 0), stop=(n == KT - 1))
            last.then_inc(table_done, 1)

            def turn_rows(e, q, it):
                pe.wait_ge(gathered[q], 16 * ST * (it + 1))
                if isinstance(e, int) and e < 1:
                    pe.wait_ge(gidx_ready, 2)
                else:
                    pe.wait_ge(xt_lo_ready, 2 * e)
                for k in range(2):
                    for j in range(ST):
                        last = pe.transpose(xt_bank[:, k, j * P:(j + 1) * P], Xg[q][:, j, k * P:(k + 1) * P], ident[:, :])
                last.then_inc(xt_done, 1)

            def step(e, q, it):
                def layer1(c):
                    if c == 0:
                        pe.wait_ge(xt_lo_ready, 2 * (e + 1))
                        pe.wait_ge(wl_ready, 4 * (e + 1))
                    if not (isinstance(e, int) and e < 1 and c < 4):
                        pe.wait_ge(hr_ready, C * e + c - 3)
                    n = 0
                    for k in range(2):
                        for w, a in ((w1_hi, XT_hi), (w1_lo, XT_hi), (w1_hi, XT_lo)):
                            n += 1
                            last = pe.matmul(h_bank[c % 4], w[q][:, k, c, :], a[q][:, k, :], start=(n == 1), stop=(n == 6))
                    last.then_inc(h_done, 1)

                def layer2(c):
                    pe.wait_ge(hl_ready, C * e + c + 1)
                    if c == 0 and not (isinstance(e, int) and e < 1):
                        pe.wait_ge(y_ready, 2 * e)
                    for j in range(ST):
                        for n, (a, w) in enumerate(((h_hi, w2_hi), (h_lo, w2_hi), (h_hi, w2_lo))):
                            last = pe.matmul(y_bank[j // 2][:, (j % 2) * D:(j % 2 + 1) * D], a[c % 4][:, j * P:(j + 1) * P], w[q][:, c, :],
                                             start=(c == 0 and n == 0 and j % 2 == 0), stop=(c == C - 1 and n == 2), skip_group_check=True)
                    last.then_inc(f2_part, 1)

                layer1(0)
                layer1(1)
                layer1(2)
                for c in range(C):
                    layer2(c)
                    if c + 3 < C:
                        layer1(c + 3)
                    if c == C - 4 and not static(e, E - 1):
                        turn_rows(e + 1, 1 - q, it + q)

            turn_rows(0, 0, 0)
            steps(step)(pe)


def program(nc, x, ctx_1024, Wq, Wk, Wv, bv, Wo, bo, wg, w1, b1, w2, b2, out):
    B, S, D = x.shape
    T = B * S
    C = w1.shape[2] // P
    with ExitStack() as ctx:
        def sem(name):
            return ctx.enter_context(nc.semaphore(name))

        def sb(name, shape, dt):
            return ctx.enter_context(nc.sbuf_tensor(name, shape, dt))

        xn_rows = nc.dram_tensor("xn_rows", [T, D], F32, kind="Internal").ap()
        y_rows = nc.dram_tensor("y_rows", [TOPK * T, D], F32, kind="Internal").ap()
        persist = {
            "x_all": sb("x_all", [P, T // P, D], F32),
            "ident": sb("ident", [P, P], F32),
            "dl_all": sb("dl_all", [P, T // P], F32),
            "expert_all": sb("expert_all", [P, TOPK, T // P], F32),
            "zeros": sb("zeros", [P, D], F32),
            "raw1": [sb(f"raw1_{q}", [P, 2, C * P], F32) for q in range(2)],
            "raw2": [sb(f"raw2_{q}", [P, C, D], F32) for q in range(2)],
            "b1_sb": [sb(f"b1_sb{q}", [P, C], F32) for q in range(2)],
            "b2_bc": [sb(f"b2_bc{q}", [P, D], F32) for q in range(2)],
            "ps": ctx.enter_context(nc.psum_tensor("ps", [P, 8, 512], F32)),
            "weights_loaded": [sem(f"weights_loaded{q}") for q in range(2)],
            "biases_loaded": [sem(f"biases_loaded{q}") for q in range(2)],
            "zeros_ready": sem("zeros_ready"),
            "y_zeroed": sem("y_zeroed"),
        }
        for part, args in ((attention, (x, ctx_1024, Wq, Wk, Wv, bv, Wo, bo, wg, w1, b1, w2, b2, xn_rows, y_rows)),
                           (experts, (out, w1, b1, w2, b2, xn_rows, y_rows))):
            with ExitStack() as own:
                part(nc, sem, lambda n, s, d: own.enter_context(nc.sbuf_tensor(n, s, d)), persist, *args)


_INS = ['x', 'ctx_1024', 'L0_xattn_W_q', 'L0_xattn_W_k', 'L0_xattn_W_v', 'L0_xattn_b_v', 'L0_xattn_W_o', 'L0_xattn_b_o',
        'L0_ffn_wg', 'L0_ffn_w1', 'L0_ffn_b1', 'L0_ffn_w2', 'L0_ffn_b2']


def kernel(**inputs):
    import numpy as _np
    import concourse.bacc as _bacc
    from concourse import mybir as _mybir
    from concourse.bass_utils import run_bass_kernel_spmd as _run

    nc = _bacc.Bacc("TRN2", target_bir_lowering=False, num_devices=1)
    arrays, args = {}, []
    for name in _INS:
        a = _np.ascontiguousarray(inputs[name])
        arrays[f"in_{name}_dram"] = a
        args.append(nc.dram_tensor(f"in_{name}_dram", a.shape, _mybir.dt.from_np(a.dtype), kind="ExternalInput").ap())
    out = nc.dram_tensor("out_0_dram", inputs["x"].shape, F32, kind="ExternalOutput").ap()
    program(nc, *args, out)
    r = _run(nc, [arrays], core_ids=[0])
    return r.results[0]["out_0_dram"]
```

```python
from contextlib import ExitStack

import concourse.bass as bass
from concourse import mybir

P = 128
F32 = mybir.dt.float32
F32R = mybir.dt.float32r
BF16 = mybir.dt.bfloat16
I32 = mybir.dt.int32
U32 = mybir.dt.uint32
ALU = mybir.AluOpType
ACT = mybir.ActivationFunctionType
AX_X = mybir.AxisListType.X

HEADS = 16
HD = 16
HPG = 4
GROUPS = HEADS // HPG
VW = 32
ROWS = 3 * HD
EPS = 1e-5
MASKED = -1e38
UNITS = 3 * GROUPS
EXPERTS = 8
TOPK = 2
HALVES = 2


def wait_alone(eng, started, semaphore, value):
    if not isinstance(value, int):
        value = eng.to_reg(value)
    eng.wait_ge(started, 1)
    eng.wait_ge(semaphore, value)


def attention(nc, sem, sb, persist, x, ctx_in, Wq, Wk, Wv, bv, Wo, bo, wg, w1, b1, w2, b2, xn_rows, out):
    B, S, D = x.shape
    x_all, ident, dl_all, expert_all, ps = (persist[k] for k in ("x_all", "ident", "dl_all", "expert_all", "ps"))
    raw1, raw2, b1_sb, b2_bc = (persist[k] for k in ("raw1", "raw2", "b1_sb", "b2_bc"))
    tri, onesb, carry = (persist[k] for k in ("tri", "onesb", "carry"))
    iota_e, iota_s, iota_g, iota_k, iota_p = (persist[k] for k in ("iota_e", "iota_s", "iota_g", "iota_k", "iota_p"))
    started = persist["started"]
    weights_loaded, biases_loaded = persist["weights_loaded"], persist["biases_loaded"]

    max_bank = [ps[:, 0, :], ps[:, 1, :]]
    prob_score = ps[:, 3:6, :].rearrange("p a b -> p (a b)")
    value_bank = ps[:, 7, :]
    bank = [ps[:, 2, :], ps[:, 6, :]]

    w_raw = sb("w_raw", [P, 4, 2, D], F32)
    w_hi = sb("w_hi", [P, 4, 2, D], F32R)
    w_lo = sb("w_lo", [P, 4, 2, D], F32R)
    bv_bc = sb("bv_bc", [P, D], F32)
    bo_bc = sb("bo_bc", [P, D], F32)
    wg_sb = sb("wg_sb", [P, 2, EXPERTS], F32)
    identb = sb("identb", [P, P], BF16)
    mask0 = sb("mask0", [P, HPG, P], BF16)
    mask1 = sb("mask1", [P, 2, P], BF16)
    half = sb("half", [P, 2], F32)
    c_sb = sb("c_sb", [P, 2, D], F32)
    xn = sb("xn", [P, 2, D], F32)
    st1 = sb("st1", [P, 2, 6], F32)
    mv1 = sb("mv1", [P, 2, 2], F32)
    ve1 = sb("ve1", [P, 2, 2], F32)
    rs1 = sb("rs1", [P, 2, 2], F32)
    st2 = sb("st2", [P, 2, 6], F32)
    mv2 = sb("mv2", [P, 2, 2], F32)
    ve2 = sb("ve2", [P, 2, 2], F32)
    rs2 = sb("rs2", [P, 2, 2], F32)
    xT_hi = sb("xT_hi", [P, 2, S], F32R)
    xT_lo = sb("xT_lo", [P, 2, S], F32R)
    cT_hi = sb("cT_hi", [P, 2, S], F32R)
    cT_lo = sb("cT_lo", [P, 2, S], F32R)
    q_hi = sb("q_hi", [P, 2, S], F32R)
    q_lo = sb("q_lo", [P, 2, S], F32R)
    k_hi = sb("k_hi", [P, 2, S], F32R)
    k_lo = sb("k_lo", [P, 2, S], F32R)
    Qs = [sb(f"Qs{q}", [ROWS + 2, HEADS, S], F32R) for q in range(2)]
    Ks = [sb(f"Ks{q}", [ROWS + 2, HEADS, S], F32R) for q in range(2)]
    V = [sb(f"V{q}", [P, 2, HEADS, VW], F32) for q in range(2)]
    nm = sb("nm", [P, 2, HEADS], F32)
    nm_s = sb("nm_s", [P, 2, 2, HEADS], F32R)
    nmT = sb("nmT", [2 * HEADS, S], F32)
    PT = [sb(f"PT{g}", [P, HPG * (S + P)], F32) for g in range(2)]
    OT = sb("OT", [P, GROUPS, S], F32)
    rec = sb("rec", [P, 2, HEADS], F32)
    attn = sb("attn", [P, 2, HEADS, HD], F32)
    aT_hi = sb("aT_hi", [P, 2, S], F32R)
    aT_lo = sb("aT_lo", [P, 2, S], F32R)
    x2n = sb("x2n", [P, 2, D], F32)
    x2T = sb("x2T", [P, 2, S], F32)
    lg = sb("lg", [P, 2, EXPERTS], F32)
    top8 = sb("top8", [P, 2, 8], F32)
    idx8 = sb("idx8", [P, 2, 8], U32)

    x0_loaded, x_loaded = sem("x0_loaded"), sem("x_loaded")
    ctx_loaded = sem("ctx_loaded")
    wqkvo_loaded = [sem(f"w{n}_loaded") for n in "qkvo"]
    small_loaded = sem("small_loaded")
    const_tmp, const_ready, ones_ready = sem("const_tmp"), sem("const_ready"), sem("ones_ready")
    w_hi_ready, w_lo_ready = sem("w_hi_ready"), sem("w_lo_ready")
    ln1_stats, ln1_pow, xn_ready, xbo_ready = sem("ln1_stats"), sem("ln1_pow"), sem("xn_ready"), sem("xbo_ready")
    tx_done, tc_done = sem("tx_done"), sem("tc_done")
    xT_hi_ready, xT_lo_ready = sem("xT_hi_ready"), sem("xT_lo_ready")
    cT_hi_ready, cT_lo_ready = sem("cT_hi_ready"), sem("cT_lo_ready")
    q_done, k_done, v_done = sem("q_done"), sem("k_done"), sem("v_done")
    q_hi_ready, q_lo_ready = sem("q_hi_ready"), sem("q_lo_ready")
    k_hi_ready, k_lo_ready = sem("k_hi_ready"), sem("k_lo_ready")
    v_ready = sem("v_ready")
    q_stacked, k_stacked, max_stacked = sem("q_stacked"), sem("k_stacked"), sem("max_stacked")
    a_done, max_done, nm_ready, nmT_done, nmT_ready = (sem(n) for n in ("a_done", "max_done", "nm_ready", "nmT_done", "nmT_ready"))
    b_done, exp_done, mask_done, av_done, ot_ready = (sem(n) for n in ("b_done", "exp_done", "mask_done", "av_done", "ot_ready"))
    ott_done, rec_ready, norm_done = sem("ott_done"), sem("rec_ready"), sem("norm_done")
    at_done, aT_hi_ready, aT_lo_ready, op_done = sem("at_done"), sem("aT_hi_ready"), sem("aT_lo_ready"), sem("op_done")
    x2_ready, ln2_stats, ln2_pow, x2n_ready, x2n_stored = (sem(n) for n in ("x2_ready", "ln2_stats", "ln2_pow", "x2n_ready", "x2n_stored"))
    x2t_done, x2T_ready, rt_done, lg_ready, top_ready, top_used = (sem(n) for n in ("x2t_done", "x2T_ready", "rt_done", "lg_ready", "top_ready", "top_used"))
    x2_stored = sem("x2_stored")

    x_tiles = x.rearrange("b (t p) m -> p (b t) m", p=P)
    ctx_tiles = ctx_in.rearrange("b (t p) m -> b p t m", p=P)
    out_tiles = out.rearrange("b (t p) m -> b p t m", p=P)
    xn_tiles = xn_rows.rearrange("(b t p) m -> b p t m", t=2, p=P)

    def steps(eng, step):
        step(-2, 0, max_part=False, score_part=False, out_part=False)
        step(-1, 1, score_part=False, out_part=False)
        step(0, 0, out_part=False)
        with eng.Fori(0, (B - 4) // 2) as it:
            step(2 * it + 1, 1)
            step(2 * it + 2, 0)
        step(B - 3, (B - 3) % 2)
        step(B - 2, (B - 2) % 2, proj_part=False)
        step(B - 1, (B - 1) % 2, proj_part=False, max_part=False)
        step(B, B % 2, proj_part=False, max_part=False, score_part=False)

    def max_unit(u):
        g, part = divmod(u, 3)
        return (1, HPG * g + 2 * part, 2) if part < 2 else (0, HPG * g, HPG)

    def first(s, n):
        return isinstance(s, int) and s < n

    def weight_views(n, dst):
        if n >= 2:
            return [(dst[:, n].rearrange("p a b -> p (a b)"), w_raw[:, n].rearrange("p a b -> p (a b)"))]
        out = []
        for k in range(2):
            src = w_raw[:, n, k, :].rearrange("p (h f d) -> p f d h", f=2, d=HD)
            to = dst[:, n, k, :].rearrange("p (f d h) -> p f d h", f=2, d=HD)
            out += [(to[:, f], src[:, f]) for f in range(2)]
        return out

    block = nc.Block()
    with block:

        @block.sync
        def _(sp):
            sp.dma_start(x_all[:, 0:2, :], x_tiles[:, 0:2, :]).then_inc(x0_loaded, 16)
            sp.dma_start(c_sb[:, :, :], ctx_tiles[0]).then_inc(ctx_loaded, 16)
            sp.dma_start(w_raw[:, 0], Wq.rearrange("(k p) n -> p k n", p=P)).then_inc(wqkvo_loaded[0], 16)
            sp.dma_start(w_raw[:, 1], Wk.rearrange("(k p) n -> p k n", p=P)).then_inc(wqkvo_loaded[1], 16)
            sp.dma_start(w_raw[:, 2], Wv.rearrange("(k p) n -> p k n", p=P)).then_inc(wqkvo_loaded[2], 16)
            sp.dma_start(w_raw[:, 3], Wo.rearrange("(k p) n -> p k n", p=P)).then_inc(wqkvo_loaded[3], 16)
            sp.dma_start(x_all[:, 2:, :], x_tiles[:, 2:, :]).then_inc(x_loaded, 16)

            def stack(dst, row, src, done):
                sp.dma_start(dst[row:row + HD, :, :].rearrange("d (h f) t -> d h (f t)", f=2).bitcast(F32),
                             src[:, :, :].rearrange("p f t -> p (f t)").bitcast(F32)).then_inc(done, 16)

            def step(s, q, proj_part=True, max_part=True, score_part=True, out_part=True):
                if proj_part and not (isinstance(s, int) and s + 3 >= B):
                    wait_alone(sp, started, tc_done, s + 3)
                    sp.dma_start(c_sb[:, :, :], ctx_tiles[s + 3]).then_inc(ctx_loaded, 16)
                if out_part:
                    wait_alone(sp, started, x2n_ready, 2 * s)
                    sp.dma_start(xn_tiles[s - 1], x2n[:, :, :]).then_inc(x2n_stored, 16)
                    sp.dma_start(out_tiles[s - 1], x_all[:, bass.ds(2 * (s - 1), 2), :]).then_inc(x2_stored, 16)
                if proj_part:
                    if first(s, 0):
                        sp.wait_ge(ones_ready, 4)
                    else:
                        wait_alone(sp, started, b_done, GROUPS * (s + 1))
                    sp.wait_ge(q_hi_ready, s + 3)
                    stack(Qs[q], 0, q_hi, q_stacked)
                    stack(Qs[q], 2 * HD, q_hi, q_stacked)
                    sp.wait_ge(q_lo_ready, s + 3)
                    stack(Qs[q], HD, q_lo, q_stacked)
                    wait_alone(sp, started, k_hi_ready, s + 3)
                    stack(Ks[q], 0, k_hi, k_stacked)
                    stack(Ks[q], HD, k_hi, k_stacked)
                    sp.wait_ge(k_lo_ready, s + 3)
                    stack(Ks[q], 2 * HD, k_lo, k_stacked)
                if max_part:
                    wait_alone(sp, started, nmT_ready, s + 2)
                    sp.dma_start(Qs[1 - q][ROWS:ROWS + 2, :, :].bitcast(F32),
                                 nmT[:, :]).then_inc(max_stacked, 16)

            steps(sp, step)
            sp.wait_ge(x2n_stored, 16 * (B + 1))
            sp.wait_ge(x2_stored, 16 * B)

        @block.gpsimd
        def _(pool):
            pool.dma_start(bv_bc[:, :], bv.rearrange("(a n) -> a n", a=1).broadcast_to([P, D])).then_inc(small_loaded, 16)
            pool.dma_start(bo_bc[:, :], bo.rearrange("(a n) -> a n", a=1).broadcast_to([P, D])).then_inc(small_loaded, 16)
            pool.dma_start(wg_sb[:, :, :], wg.rearrange("(k p) e -> p k e", p=P)).then_inc(small_loaded, 16)
            pool.memset(ident[:, :], 1.0).then_inc(const_tmp, 1)
            pool.wait_ge(const_tmp, 1)
            pool.affine_select(ident[:, :], ident[:, :], [[-1, P]], ALU.is_equal, 0.0, base=0, channel_multiplier=1).then_inc(const_ready, 1)

            def constants():
                for q in range(2):
                    pool.memset(Ks[q][:, :, :].bitcast(F32), 1.0).then_inc(ones_ready, 1)
                for q in range(2):
                    pool.memset(V[q][:, :, :, HD:], 0.0).then_inc(const_tmp, 1)
                    pool.wait_ge(const_tmp, 2 + q)
                    pool.memset(V[q][:, :, :, HD:HD + 1], 1.0).then_inc(ones_ready, 1)
                pool.memset(identb[:, :], 1.0).then_inc(const_tmp, 1)
                pool.memset(mask0[:, :, :], 0.0).then_inc(const_tmp, 1)
                pool.memset(mask1[:, :, :], 0.0).then_inc(const_tmp, 1)
                pool.wait_ge(const_tmp, 6)
                pool.affine_select(identb[:, :], identb[:, :], [[-1, P]], ALU.is_equal, 0.0, base=0, channel_multiplier=1).then_inc(const_ready, 1)
                pool.affine_select(mask1[:, :, :], mask1[:, :, :], [[0, 2], [-1, P]], ALU.is_gt, MASKED, base=0, channel_multiplier=1).then_inc(const_ready, 1)
                pool.affine_select(mask0[:, :, :], mask0[:, :, :], [[0, HPG], [-1, P]], ALU.is_gt, MASKED, base=0, channel_multiplier=1).then_inc(const_tmp, 1)
                pool.wait_ge(const_tmp, 7)
                pool.memset(mask0[0:1, :, 0:1], 0.0).then_inc(const_ready, 1)
                exact = dict(allow_small_or_imprecise_dtypes=True)
                pool.memset(tri[:, :], -1.0).then_inc(const_tmp, 1)
                pool.memset(onesb[:, :], 1.0).then_inc(const_tmp, 1)
                pool.memset(carry[:, :, :], 1.0).then_inc(const_tmp, 1)
                pool.iota(iota_e[:, :], [[1, EXPERTS]], base=0, channel_multiplier=0, **exact).then_inc(const_tmp, 1)
                pool.iota(iota_s[:, :], [[1, P]], base=0, channel_multiplier=0, **exact).then_inc(const_tmp, 1)
                pool.iota(iota_g[:, :], [[1, iota_g.shape[1]]], base=0, channel_multiplier=0, **exact).then_inc(const_tmp, 1)
                pool.iota(iota_k[:, :], [[1, iota_k.shape[1]]], base=1, channel_multiplier=0, **exact).then_inc(const_tmp, 1)
                pool.iota(iota_p[:, :], [[1, 1]], base=0, channel_multiplier=1, **exact).then_inc(const_tmp, 1)
                pool.wait_ge(const_tmp, 10)
                pool.affine_select(tri[:, :], tri[:, :], [[-1, P]], ALU.is_ge, 0.0, base=0, channel_multiplier=1).then_inc(const_tmp, 1)
                pool.memset(carry[:, :, 0:1], 0.0).then_inc(const_tmp, 1)

            def powers(n, stats, mv, ve, rs, done):
                wait_alone(pool, started, stats, 4 * n + 4)
                pool.tensor_scalar(ve[:, 0, :], mv[:, :, 1], EPS, None, ALU.add).then_inc(done, 1)
                pool.tensor_scalar(ve[:, 1, :], mv[:, :, 0], -1.0, None, ALU.mult).then_inc(done, 1)
                wait_alone(pool, started, done, 4 * n + 2)
                pool.tensor_tensor(rs[:, 0, :], ve[:, 0, :], half[:, :], ALU.pow).then_inc(done, 1)
                wait_alone(pool, started, done, 4 * n + 3)
                pool.tensor_tensor(rs[:, 1, :], ve[:, 1, :], rs[:, 0, :], ALU.mult).then_inc(done, 1)

            def norm_powers(n):
                powers(n, ln1_stats, mv1, ve1, rs1, ln1_pow)

            def add_bias(n):
                pool.wait_ge(xn_ready, 2 * (n + 1))
                if first(n, 1):
                    pool.wait_ge(small_loaded, 48)
                xs = x_all[:, bass.ds(2 * n, 2), :]
                pool.tensor_tensor(xs, xs, bo_bc[:, :].unsqueeze(1).broadcast_to([P, 2, D]), ALU.add).then_inc(xbo_ready, 1)

            def step(s, q, proj_part=True, max_part=True, score_part=True, out_part=True):
                def mask(g):
                    wait_alone(pool, started, exp_done, GROUPS * s + g + 1)
                    p0 = PT[g % 2][:, 0:HPG * S].rearrange("p (h i) -> p h i", h=HPG)
                    p1 = PT[g % 2][:, HPG * S:].rearrange("p (h i) -> p h i", h=HPG)
                    pool.affine_select(p0[:, :, 0:1], p0[:, :, 0:1], [[0, HPG], [0, 1]], ALU.is_ge, 0.0, base=0, channel_multiplier=-1)
                    pool.affine_select(p0[:, :, 1:P], p0[:, :, 1:P], [[0, HPG], [1, P - 1]], ALU.is_gt, 0.0, base=1, channel_multiplier=-1).then_inc(mask_done, 1)
                    pool.affine_select(p1, p1, [[0, HPG], [1, P]], ALU.is_gt, 0.0, base=0, channel_multiplier=-1).then_inc(mask_done, 1)

                if first(s, -1):
                    norm_powers(0)
                if proj_part:
                    add_bias(s + 2)
                if first(s, -1):
                    constants()
                if score_part:
                    mask(0)
                if out_part:
                    powers(s - 1, ln2_stats, mv2, ve2, rs2, ln2_pow)
                if score_part:
                    mask(1)
                if proj_part and not (isinstance(s, int) and s + 3 >= B):
                    norm_powers(s + 3)
                if score_part:
                    mask(2)
                    mask(3)

            steps(pool, step)
            pool.wait_ge(const_tmp, 17)

        @block.scalar
        def _(act):
            def prefetch(n):
                e = n // 2
                if n % 2 == 0:
                    act.dma_start(raw1[e][:, :, :], w1[e].rearrange("(k p) h -> p k h", p=P)).then_inc(weights_loaded[e], 16)
                    act.dma_start(b1_sb[e][:, :], b1[e].rearrange("(p c) -> p c", p=P)).then_inc(biases_loaded[e], 16)
                else:
                    act.dma_start(raw2[e][:, :, :], w2[e].rearrange("(p c) m -> p c m", p=P)).then_inc(weights_loaded[e], 16)
                    act.dma_start(b2_bc[e][:, :], b2[e:e + 1, :].broadcast_to([P, D])).then_inc(biases_loaded[e], 16)

            def round_weights():
                for n in range(4):
                    act.wait_ge(wqkvo_loaded[n], 16)
                    for dst, src in weight_views(n, w_hi):
                        act.activation(dst, src, ACT.Copy).then_inc(w_hi_ready, 1)

            def round_bank(dst, src):
                return act.activation(dst[:, :, :].rearrange("p a b -> p (a b)"), src, ACT.Copy)

            def normalise(dst, n, mean_scale, done):
                for t in range(2):
                    x_tile = x_all[:, bass.ds(2 * n + t, 1), :].rearrange("p a m -> p (a m)")
                    act.activation(dst[:, t, :], x_tile, ACT.Identity, bias=mean_scale[:, 1, t:t + 1],
                                   scale=mean_scale[:, 0, t:t + 1]).then_inc(done, 1)

            def norm_x(n):
                wait_alone(act, started, ln1_pow, 4 * (n + 1))
                if not first(n, 1):
                    wait_alone(act, started, tx_done, n)
                normalise(xn, n, rs1, xn_ready)

            def step(s, q, proj_part=True, max_part=True, score_part=True, out_part=True):
                def exp(g):
                    act.wait_ge(b_done, GROUPS * s + g + 1)
                    if g >= 2:
                        act.wait_ge(av_done, GROUPS * s + g - 1)
                    elif not first(s, 1):
                        act.wait_ge(av_done, GROUPS * (s - 1) + g + 3)
                    act.activation(PT[g % 2][:, :], prob_score, ACT.Exp, scale=float(HD) ** -0.5).then_inc(exp_done, 1)

                def values(n):
                    act.wait_ge(av_done, GROUPS * s + 2 * n + 2)
                    if not first(s, 1):
                        act.wait_ge(ott_done, 2 * s)
                    act.activation(OT[:, 2 * n:2 * n + 2, :].rearrange("p a b -> p (a b)"), value_bank, ACT.Copy).then_inc(ot_ready, 1)

                if out_part:
                    act.wait_ge(at_done, s)
                    round_bank(aT_hi, bank[1]).then_inc(aT_hi_ready, 1)
                if proj_part:
                    act.wait_ge(tx_done, s + 3)
                    if not first(s, -1):
                        act.wait_ge(q_done, s + 2)
                    round_bank(xT_hi, bank[0]).then_inc(xT_hi_ready, 1)
                if score_part:
                    exp(0)
                    exp(1)
                if proj_part:
                    act.wait_ge(tc_done, s + 3)
                    if not first(s, -1):
                        act.wait_ge(v_done, s + 2)
                    round_bank(cT_hi, bank[0]).then_inc(cT_hi_ready, 1)
                    act.wait_ge(q_done, s + 3)
                    if not first(s, -1):
                        act.wait_ge(q_stacked, 48 * (s + 2))
                    round_bank(q_hi, bank[1]).then_inc(q_hi_ready, 1)
                if out_part:
                    act.wait_ge(ln2_pow, 4 * s)
                    act.wait_ge(x2n_stored, 16 * s)
                    normalise(x2n, s - 1, rs2, x2n_ready)
                if proj_part:
                    act.wait_ge(k_done, s + 3)
                    if not first(s, -1):
                        act.wait_ge(k_stacked, 48 * (s + 2))
                    round_bank(k_hi, bank[0]).then_inc(k_hi_ready, 1)
                if out_part:
                    act.wait_ge(x2t_done, s)
                    round_bank(x2T, bank[1]).then_inc(x2T_ready, 1)
                if score_part:
                    exp(2)
                if isinstance(s, int) and s in prefetch_steps:
                    prefetch(prefetch_steps.index(s))
                if proj_part and not (isinstance(s, int) and s + 3 >= B):
                    norm_x(s + 3)
                if score_part:
                    values(0)
                    exp(3)
                    values(1)
                if max_part:
                    act.wait_ge(nmT_done, s + 2)
                    if not first(s, 0):
                        act.wait_ge(max_stacked, 16 * (s + 1))
                    act.activation(nmT[:, :], bank[1][0:2 * HEADS, 0:S], ACT.Copy).then_inc(nmT_ready, 1)

            prefetch_steps = [-1, 0, B - 3, B - 2]
            round_weights()
            norm_x(0)
            steps(act, step)

        @block.vector
        def _(dve):
            dve.memset(half[:, :], -0.5).then_inc(started, 1)
            dve.memset(x2n[:, :, :], 0.0).then_inc(x2n_stored, 16)

            def norm_stats(tiles, st, mv, stats, n):
                for t in range(2):
                    dve.bn_stats(st[:, t, :], tiles[:, t, :]).then_inc(stats, 1)
                wait_alone(dve, started, stats, 4 * n + 2)
                for t in range(2):
                    dve.bn_aggr(mv[:, t, :], st[:, t, :]).then_inc(stats, 1)

            def split_weights():
                n_hi = 0
                for n in range(4):
                    for (lo, src), (hi, _) in zip(weight_views(n, w_lo), weight_views(n, w_hi)):
                        n_hi += 1
                        dve.wait_ge(w_hi_ready, n_hi)
                        dve.tensor_tensor(lo, src, hi.bitcast(F32), ALU.subtract).then_inc(w_lo_ready, 1)

            def split_lo(lo, hi, src, hi_ready, n, done):
                dve.wait_ge(hi_ready, n)
                dve.tensor_tensor(lo[:, :, :].rearrange("p a b -> p (a b)"), src,
                                  hi[:, :, :].rearrange("p a b -> p (a b)").bitcast(F32), ALU.subtract).then_inc(done, 1)

            def top_two(n):
                wait_alone(dve, started, lg_ready, n + 1)
                for t in range(2):
                    dve.max(top8[:, t, :], lg[:, t, :]).then_inc(top_ready, 1)
                wait_alone(dve, started, top_ready, 4 * n + 2)
                for t in range(2):
                    dve.max_index(idx8[:, t, :], top8[:, t, :], lg[:, t, :]).then_inc(top_ready, 1)
                dve.tensor_tensor(dl_all[:, bass.ds(2 * n, 2)], top8[:, :, 1], top8[:, :, 0], ALU.subtract).then_inc(top_used, 1)
                dve.wait_ge(top_ready, 4 * n + 4)
                for k in range(TOPK):
                    dve.tensor_copy(expert_all[:, k, bass.ds(2 * n, 2)], idx8[:, :, k]).then_inc(top_used, 1)

            def step(s, q, proj_part=True, max_part=True, score_part=True, out_part=True):
                def maxima(pair):
                    for u in (2 * pair, 2 * pair + 1):
                        dve.wait_ge(a_done, UNITS * (s + 1) + u + 1)
                        if u == 0 and not first(s, 0):
                            dve.wait_ge(nm_ready, 2 * (s + 1))
                        tile, h, count = max_unit(u)
                        dve.tensor_reduce(nm[:, tile, h:h + count], max_bank[u % 2].rearrange("p (h j) -> p h j", h=count),
                                          AX_X, ALU.max, negate=True).then_inc(max_done, 1)

                def normalise(t):
                    dve.wait_ge(ott_done, 2 * (s - 1) + t + 1)
                    heads = bank[t].rearrange("p (h c) -> p h c", c=VW)
                    dve.reciprocal(rec[:, t, :], heads[:, :, HD]).then_inc(rec_ready, 1)
                    dve.wait_ge(rec_ready, 2 * (s - 1) + t + 1)
                    dve.tensor_tensor(attn[:, t], heads[:, :, 0:HD], rec[:, t, :].unsqueeze(2).broadcast_to([P, HEADS, HD]),
                                      ALU.mult).then_inc(norm_done, 1)

                if first(s, -1):
                    dve.wait_ge(x0_loaded, 16)
                    norm_stats(x_all[:, 0:2, :], st1, mv1, ln1_stats, 0)
                    split_weights()
                if out_part:
                    normalise(0)
                    normalise(1)
                if max_part:
                    dve.wait_ge(v_done, s + 2)
                    if first(s, 0):
                        dve.wait_ge(ones_ready, 4)
                        dve.wait_ge(small_loaded, 48)
                    dve.tensor_tensor(V[1 - q][:, :, :, 0:HD],
                                      bank[0].rearrange("p (t h d) -> p t h d", t=2, h=HEADS),
                                      bv_bc[:, :].rearrange("p (h d) -> p h d", h=HEADS).unsqueeze(1).broadcast_to([P, 2, HEADS, HD]),
                                      ALU.add).then_inc(v_ready, 1)
                if out_part:
                    split_lo(aT_lo, aT_hi, bank[1], aT_hi_ready, s, aT_lo_ready)
                if proj_part:
                    split_lo(xT_lo, xT_hi, bank[0], xT_hi_ready, s + 3, xT_lo_ready)
                if max_part:
                    maxima(0)
                if out_part:
                    x2 = x_all[:, bass.ds(2 * (s - 1), 2), :]
                    dve.wait_ge(op_done, s)
                    dve.wait_ge(xbo_ready, s)
                    dve.tensor_tensor(x2, bank[1].rearrange("p (t m) -> p t m", t=2), x2, ALU.add).then_inc(x2_ready, 1)
                    wait_alone(dve, started, x2_ready, s)
                    norm_stats(x2, st2, mv2, ln2_stats, s - 1)
                if max_part:
                    maxima(1)
                if proj_part:
                    split_lo(cT_lo, cT_hi, bank[0], cT_hi_ready, s + 3, cT_lo_ready)
                    split_lo(q_lo, q_hi, bank[1], q_hi_ready, s + 3, q_lo_ready)
                if proj_part and not (isinstance(s, int) and s + 3 >= B):
                    if first(s, -1):
                        dve.wait_ge(x_loaded, 16)
                    dve.wait_ge(xn_ready, 2 * (s + 3))
                    norm_stats(x_all[:, bass.ds(2 * (s + 3), 2), :], st1, mv1, ln1_stats, s + 3)
                if proj_part:
                    split_lo(k_lo, k_hi, bank[0], k_hi_ready, s + 3, k_lo_ready)
                if max_part:
                    maxima(2)
                    maxima(3)
                if out_part:
                    dve.wait_ge(rt_done, s)
                    dve.tensor_copy(lg[:, :, :], bank[0][:, 0:2 * EXPERTS].rearrange("p (t e) -> p t e", t=2)).then_inc(lg_ready, 1)
                    top_two(s - 1)
                if max_part:
                    maxima(4)
                    maxima(5)
                    dve.wait_ge(max_done, UNITS * (s + 2))
                    if not first(s, 0):
                        dve.wait_ge(nmT_done, s + 1)
                    dve.tensor_copy(nm_s[:, :, 0, :], nm[:, :, :]).then_inc(nm_ready, 1)
                    dve.wait_ge(nm_ready, 2 * (s + 1) + 1)
                    dve.tensor_tensor(nm_s[:, :, 1, :], nm[:, :, :], nm_s[:, :, 0, :].bitcast(F32), ALU.subtract).then_inc(nm_ready, 1)

            steps(dve, step)
            dve.wait_ge(top_used, 3 * B)

        @block.tensor
        def _(pe):
            def step(s, q, proj_part=True, max_part=True, score_part=True, out_part=True):
                def a_scores(pair):
                    Q, K = Qs[1 - q], Ks[1 - q]
                    for u in (2 * pair, 2 * pair + 1):
                        if u == 0:
                            pe.wait_ge(q_stacked, 48 * (s + 2))
                            pe.wait_ge(k_stacked, 48 * (s + 2))
                            if first(s, 0):
                                pe.wait_ge(const_ready, 4)
                        if not (first(s, 0) and u < 2):
                            pe.wait_ge(max_done, UNITS * (s + 1) + u - 1)
                        tile, h0, count = max_unit(u)
                        width = (tile + 1) * P
                        for h in range(count):
                            pe.matmul(max_bank[u % 2][:, h * width:(h + 1) * width], Q[0:ROWS, h0 + h, tile * P:(tile + 1) * P],
                                      K[0:ROWS, h0 + h, 0:width], start=(h == 0), stop=False, skip_group_check=True)
                        diag = max_bank[u % 2].rearrange("p (h j) -> p h j", h=count)[:, :, tile * P:]
                        pe.matmul(diag, identb[:, :], mask1[:, :, :] if tile else mask0[:, :, :],
                                  start=False, stop=True, skip_group_check=True).then_inc(a_done, 1)

                def b_scores(g):
                    if g == 0:
                        pe.wait_ge(max_stacked, 16 * (s + 1))
                    if not (first(s, 1) and g == 0):
                        pe.wait_ge(exp_done, GROUPS * s + g)
                    for hh in range(HPG):
                        h = HPG * g + hh
                        pe.matmul(prob_score[:, hh * S:(hh + 1) * S], Ks[q][:, h, 0:P], Qs[q][:, h, :], start=True, stop=True)
                    for hh in range(HPG):
                        h = HPG * g + hh
                        last = pe.matmul(prob_score[:, HPG * S + hh * P:HPG * S + (hh + 1) * P], Ks[q][:, h, P:S], Qs[q][:, h, P:S],
                                         start=True, stop=True)
                    last.then_inc(b_done, 1)

                def values(g):
                    pe.wait_ge(mask_done, 2 * (GROUPS * s + g + 1))
                    if g == 0:
                        pe.wait_ge(v_ready, s + 1)
                        if not first(s, 1):
                            pe.wait_ge(ot_ready, 2 * s)
                    if g == 2:
                        pe.wait_ge(ot_ready, 2 * s + 1)
                    for hh in range(HPG):
                        h = HPG * g + hh
                        out = value_bank[VW * hh:VW * hh + VW, (g % 2) * S:(g % 2) * S + S]
                        pe.matmul(out, V[q][:, 0, h, :], PT[g % 2][:, hh * S:(hh + 1) * S], start=True, stop=False)
                        last = pe.matmul(out[:, P:S], V[q][:, 1, h, :], PT[g % 2][:, HPG * S + hh * P:HPG * S + (hh + 1) * P],
                                         start=False, stop=True)
                    last.then_inc(av_done, 1)

                def turn_values(t):
                    if t == 0:
                        pe.wait_ge(ot_ready, 2 * s)
                        if isinstance(s, int) and s > B - 1:
                            pe.wait_ge(lg_ready, s - 1)
                    elif not (isinstance(s, int) and s > B - 1):
                        pe.wait_ge(nmT_ready, s + 1)
                    for g in range(GROUPS):
                        last = pe.transpose(bank[t][:, g * P:(g + 1) * P], OT[:, g, t * P:(t + 1) * P], ident[:, :])
                    last.then_inc(ott_done, 1)

                def turn(to, tile, done):
                    for k in range(2):
                        for t in range(2):
                            last = pe.transpose(to[:, k * S + t * P:k * S + (t + 1) * P], tile(t)[:, k * P:(k + 1) * P], ident[:, :])
                    last.then_inc(done, 1)

                def turn_x():
                    pe.wait_ge(xn_ready, 2 * (s + 3))
                    if max_part:
                        pe.wait_ge(v_ready, s + 2)
                    else:
                        pe.wait_ge(const_ready, 1)
                    turn(bank[0], lambda t: xn[:, t, :], tx_done)

                def turn_context():
                    pe.wait_ge(ctx_loaded, 16 * (s + 3))
                    pe.wait_ge(xT_lo_ready, s + 3)
                    turn(bank[0], lambda t: c_sb[:, t, :], tc_done)

                def turn_attention():
                    pe.wait_ge(norm_done, 2 * s)
                    turn(bank[1], lambda t: attn[:, t].rearrange("p h d -> p (h d)"), at_done)

                def turn_x2():
                    pe.wait_ge(x2n_ready, 2 * s)
                    if proj_part:
                        pe.wait_ge(q_lo_ready, s + 3)
                    turn(bank[1], lambda t: x2n[:, t, :], x2t_done)

                def turn_maxima():
                    pe.wait_ge(nm_ready, 2 * (s + 2))
                    if out_part:
                        pe.wait_ge(lg_ready, s)
                    else:
                        pe.wait_ge(k_lo_ready, s + 3)
                    for t in range(2):
                        last = pe.transpose(bank[1][0:2 * HEADS, t * P:(t + 1) * P],
                                            nm_s[:, t].rearrange("p a h -> p (a h)").bitcast(F32), ident[:, :])
                    last.then_inc(nmT_done, 1)

                def project_turned(to, n, hi, lo, done):
                    for f in range(2):
                        m = 0
                        for k in range(2):
                            for w, a in ((w_hi, hi), (w_lo, hi), (w_hi, lo)):
                                m += 1
                                last = pe.matmul(to[:, f * S:(f + 1) * S], w[:, n, k, f * P:(f + 1) * P], a[:, k, :],
                                                 start=(m == 1), stop=(m == 6))
                    last.then_inc(done, 1)

                def project(to, n, hi, lo, done):
                    for t in range(2):
                        m = 0
                        for k in range(2):
                            for a, w in ((hi, w_hi), (lo, w_hi), (hi, w_lo)):
                                m += 1
                                last = pe.matmul(to[:, t * D:(t + 1) * D], a[:, k, t * P:(t + 1) * P], w[:, n, k, :],
                                                 start=(m == 1), stop=(m == 6))
                    last.then_inc(done, 1)

                def queries():
                    pe.wait_ge(xT_lo_ready, s + 3)
                    if first(s, -1):
                        pe.wait_ge(w_lo_ready, 10)
                    elif out_part:
                        pe.wait_ge(x2_ready, s)
                    elif first(s, 0):
                        pe.wait_ge(q_lo_ready, s + 2)
                    else:
                        pe.wait_ge(nmT_ready, s + 1)
                    project_turned(bank[1], 0, xT_hi, xT_lo, q_done)

                def keys():
                    pe.wait_ge(cT_lo_ready, s + 3)
                    project_turned(bank[0], 1, cT_hi, cT_lo, k_done)

                def project_values():
                    if out_part:
                        pe.wait_ge(norm_done, 2 * s - 1)
                    else:
                        pe.wait_ge(k_lo_ready, s + 2)
                    project(bank[0], 2, cT_hi, cT_lo, v_done)

                def outputs():
                    pe.wait_ge(aT_lo_ready, s)
                    project(bank[1], 3, aT_hi, aT_lo, op_done)

                def router():
                    pe.wait_ge(x2T_ready, s)
                    if first(s, 2):
                        pe.wait_ge(small_loaded, 48)
                    if proj_part:
                        pe.wait_ge(k_lo_ready, s + 3)
                    elif max_part:
                        pe.wait_ge(v_ready, s + 2)
                    for t in range(2):
                        for k in range(2):
                            last = pe.matmul(bank[0][:, t * EXPERTS:(t + 1) * EXPERTS], x2T[:, k, t * P:(t + 1) * P],
                                             wg_sb[:, k, :], start=(k == 0), stop=(k == 1))
                    last.then_inc(rt_done, 1)

                if out_part:
                    turn_values(0)
                if out_part:
                    turn_values(1)
                if max_part:
                    project_values()
                if out_part:
                    turn_attention()
                if score_part:
                    b_scores(0)
                if proj_part:
                    turn_x()
                if max_part:
                    a_scores(0)
                if out_part:
                    outputs()
                if score_part:
                    b_scores(1)
                if proj_part:
                    turn_context()
                if max_part:
                    a_scores(1)
                if proj_part:
                    queries()
                if score_part:
                    values(0)
                if proj_part:
                    keys()
                if max_part:
                    a_scores(2)
                if out_part:
                    turn_x2()
                if score_part:
                    b_scores(2)
                if max_part:
                    a_scores(3)
                if out_part:
                    router()
                if score_part:
                    values(1)
                if max_part:
                    a_scores(4)
                if score_part:
                    b_scores(3)
                if score_part:
                    values(2)
                if max_part:
                    a_scores(5)
                if score_part:
                    values(3)
                if max_part:
                    turn_maxima()

            steps(pe, step)


def experts(nc, sem, sb, persist, out, w1, b1, w2, b2, xn_rows):
    E, D, H = w1.shape
    T = xn_rows.shape[0]
    TILES = T // P
    KT = TOPK * TILES
    CAP = TOPK * T // E
    ST = CAP // P
    SLOTS = E * ST
    C = H // P
    ident, dl_all, expert_all, ps = (persist[k] for k in ("ident", "dl_all", "expert_all", "ps"))
    raw1, raw2, b1_sb, b2_bc = (persist[k] for k in ("raw1", "raw2", "b1_sb", "b2_bc"))
    tri, onesb, carry = (persist[k] for k in ("tri", "onesb", "carry"))
    iota_e, iota_s, iota_g, iota_k, iota_p = (persist[k] for k in ("iota_e", "iota_s", "iota_g", "iota_k", "iota_p"))
    weights_loaded, biases_loaded, started = (persist[k] for k in ("weights_loaded", "biases_loaded", "started"))

    onehot = sb("onehot", [P, E, KT], BF16)
    base = sb("base", [P, E, KT], F32)
    pos = sb("pos", [P, KT], F32)
    c3 = sb("c3", [P, KT], F32)
    spart = sb("spart", [P, KT], F32)
    grp = sb("grp", [P, KT], F32)
    in_slot = sb("in_slot", [P, KT, P], BF16)
    in_tile = sb("in_tile", [P, KT, 2, SLOTS], BF16)
    eq = sb("eq", [P, KT, SLOTS], BF16)
    row = sb("row", [P, SLOTS], F32)
    adj = sb("adj", [P, SLOTS], F32)
    from_row = sb("from_row", [P, SLOTS], F32)
    to_row = sb("to_row", [P, SLOTS], F32)
    ratio = sb("ratio", [P, TILES], F32)
    den = sb("den", [P, TILES], F32)
    gates = sb("gates", [P, TOPK, TILES], F32)
    part = sb("part", [P, 3, KT], BF16)
    rest = sb("rest", [P, 2, KT], F32)
    in_gate = sb("in_gate", [P, KT, 3, SLOTS], BF16)
    slot_gate = sb("slot_gate", [P, SLOTS], F32)
    gather_idx = [sb(f"gather_idx{q}", [P, ST], I32) for q in range(2)]
    scatter_idx = [sb(f"scatter_idx{q}", [P, ST], I32) for q in range(2)]
    w1_hi = [sb(f"w1_hi{q}", [P, 2, C, P], F32R) for q in range(2)]
    w1_lo = [sb(f"w1_lo{q}", [P, 2, C, P], F32R) for q in range(2)]
    w2_hi = [sb(f"w2_hi{q}", [P, C, D], F32R) for q in range(2)]
    w2_lo = [sb(f"w2_lo{q}", [P, C, D], F32R) for q in range(2)]
    Xg = [sb(f"Xg{q}", [P, ST, D], F32) for q in range(2)]
    XT_hi = [sb(f"XT_hi{q}", [P, 2, CAP], F32R) for q in range(2)]
    XT_lo = [sb(f"XT_lo{q}", [P, 2, CAP], F32R) for q in range(2)]
    hr = [sb(f"hr{c}", [P, CAP], F32) for c in range(2)]
    h_hi = [sb(f"h_hi{c}", [P, CAP], F32R) for c in range(4)]
    h_lo = [sb(f"h_lo{c}", [P, CAP], F32R) for c in range(4)]
    Yb = sb("Yb", [P, ST, D], F32)
    Y = [sb(f"Y{q}", [P, ST, D], F32) for q in range(2)]

    counted, placed_a, placed_b, table_done = sem("counted"), sem("placed_a"), sem("placed_b"), sem("table_done")
    placed_k, ratio_ready = sem("placed_k"), sem("ratio_ready")
    gate_parts, in_gate_ready, gate_table_done, slot_gate_ready = (sem(n) for n in ("gate_parts", "in_gate_ready", "gate_table_done", "slot_gate_ready"))
    biased = sem("biased")
    gidx_ready, sidx_ready = sem("gidx_ready"), sem("sidx_ready")
    gathered = [[sem(f"gathered{q}_{j}") for j in range(ST)] for q in range(2)]
    scattered = [sem(f"scattered{q}") for q in range(2)]
    xt_done, xt_hi_ready, xt_lo_ready = sem("xt_done"), sem("xt_hi_ready"), sem("xt_lo_ready")
    wh_ready, wl_ready = sem("wh_ready"), sem("wl_ready")
    h_done, hr_ready, hh_ready, hl_ready = sem("h_done"), sem("hr_ready"), sem("hh_ready"), sem("hl_ready")
    f2_part, y_ready = sem("f2_part"), sem("y_ready")

    xt_bank = ps[:, 0:2, :]
    h_bank = [ps[:, 2, :], ps[:, 3, :], ps[:, 4, :], ps[:, 7, :]]
    y_bank = [ps[:, 5, :], ps[:, 6, :]]
    out_rows = out.rearrange("b s m -> (b s) m")

    def steps(step):
        def run(eng):
            step(0, 0, 0)
            step(1, 1, 0)
            with eng.Fori(1, E // 2 - 1) as it:
                step(2 * it, 0, it)
                step(2 * it + 1, 1, it)
            step(E - 2, 0, E // 2 - 1)
            step(E - 1, 1, E // 2 - 1)
        return run

    def static(e, n):
        return isinstance(e, int) and e >= n

    block = nc.Block()
    with block:

        @block.sync
        def _(sp):
            def step(e, q, it):
                if static(e, E - 2):
                    return
                sp.wait_ge(wh_ready, 4 * (e + 1))
                wait_alone(sp, started, wl_ready, 4 * (e + 1))
                sp.dma_start(raw1[q][:, :, :], w1[e + 2].rearrange("(k p) h -> p k h", p=P)).then_inc(weights_loaded[q], 16)
                sp.dma_start(raw2[q][:, :, :], w2[e + 2].rearrange("(p c) m -> p c m", p=P)).then_inc(weights_loaded[q], 16)
                wait_alone(sp, started, hr_ready, C * (e + 1))
                sp.dma_start(b1_sb[q][:, :], b1[e + 2].rearrange("(p c) -> p c", p=P)).then_inc(biases_loaded[q], 16)
                wait_alone(sp, started, biased, 2 * (e + 1))
                sp.dma_start(b2_bc[q][:, :], b2[bass.ds(e + 2, 1), :].broadcast_to([P, D])).then_inc(biases_loaded[q], 16)

            steps(step)(sp)
            for q in range(2):
                sp.wait_ge(scattered[q], 16 * ST * (E // 2))

        @block.gpsimd
        def _(pool):
            def gather(e, q):
                wait_alone(pool, started, gidx_ready, e + 1)
                if not (isinstance(e, int) and e < 2):
                    wait_alone(pool, started, xt_done, e - 1)
                for j in range(ST):
                    pool.indirect_dma_start(Xg[q][:, j, :], None, xn_rows[:, :],
                                            bass.IndirectOffsetOnAxis(ap=gather_idx[q][:, j:j + 1], axis=0)).then_inc(gathered[q][j], 16)

            def step(e, q, it):
                if not static(e, E - 2):
                    gather(e + 2, q)
                pool.wait_ge(sidx_ready, e + 1)
                wait_alone(pool, started, y_ready, ST * (e + 1))
                if not (isinstance(e, int) and e < 1):
                    wait_alone(pool, started, scattered[1 - q], 16 * ST * (it + q))
                for j in range(ST):
                    pool.indirect_dma_start(out_rows[:, :], bass.IndirectOffsetOnAxis(ap=scatter_idx[q][:, j:j + 1], axis=0),
                                            Y[q][:, j, :], None, bounds_check=T - 1, oob_is_err=False, compute_op=ALU.add).then_inc(scattered[q], 16)

            pool.wait_ge(placed_b, 1)
            pool.tensor_tensor(in_tile[:, :, 1, :], eq[:, :, :], iota_k[:, :].unsqueeze(2).broadcast_to([P, KT, SLOTS]), ALU.mult).then_inc(placed_k, 1)
            gather(0, 0)
            gather(1, 1)
            pool.wait_ge(gate_parts, 5)
            for n in range(3):
                pool.tensor_tensor(in_gate[:, :, n, :], eq[:, :, :], part[:, n, :].unsqueeze(2).broadcast_to([P, KT, SLOTS]), ALU.mult).then_inc(in_gate_ready, 1)
            steps(step)(pool)

        @block.scalar
        def _(act):
            act.activation(ratio[:, :], dl_all[:, :], ACT.Exp).then_inc(ratio_ready, 1)

            def split_weights(e, q, it):
                act.wait_ge(weights_loaded[q], 32 * (it + 1))
                if not (isinstance(e, int) and e < 2):
                    act.wait_ge(f2_part, C * (e - 1))
                for k in range(2):
                    act.activation(w1_hi[q][:, k].rearrange("p c j -> p j c"), raw1[q][:, k, :].rearrange("p (j c) -> p j c", c=C), ACT.Copy).then_inc(wh_ready, 1)
                for k in range(2):
                    act.activation(w2_hi[q][:, 4 * k:4 * k + 4], raw2[q][:, 4 * k:4 * k + 4], ACT.Copy).then_inc(wh_ready, 1)

            def turn_rows(e, q):
                act.wait_ge(xt_done, e + 1)
                if not (isinstance(e, int) and e < 2):
                    act.wait_ge(h_done, C * (e - 1))
                for k in range(2):
                    act.activation(XT_hi[q][:, k, :], xt_bank[:, k, :], ACT.Copy).then_inc(xt_hi_ready, 1)

            def step(e, q, it):
                act.wait_ge(biases_loaded[q], 32 * (it + 1))
                for c in range(C):
                    act.wait_ge(h_done, C * e + c + 1)
                    if c >= 2:
                        act.wait_ge(hl_ready, C * e + c - 1)
                    elif not (isinstance(e, int) and e < 1):
                        act.wait_ge(hl_ready, C * e + c - 1)
                    act.activation(hr[c % 2][:, :], h_bank[c % 4], ACT.Relu, bias=b1_sb[q][:, c:c + 1]).then_inc(hr_ready, 1)
                    if c == 1 and not static(e, E - 1):
                        split_weights(e + 1, 1 - q, it + q)
                if not static(e, E - 1):
                    turn_rows(e + 1, 1 - q)

            act.wait_ge(placed_b, 1)
            act.activation(in_tile[:, :, 0, :], eq[:, :, :], ACT.Copy, scale=iota_p[:, 0:1]).then_inc(placed_k, 1)
            split_weights(0, 0, 0)
            turn_rows(0, 0)
            steps(step)(act)

        @block.vector
        def _(dve):
            chain = [0]

            def then(ins):
                chain[0] += 1
                ins.then_inc(placed_a, 1)
                dve.wait_ge(placed_a, chain[0])

            queue = expert_all[:, :, :].rearrange("p k t -> p (k t)")
            then(dve.tensor_tensor(onehot[:, :, :], queue.unsqueeze(1).broadcast_to([P, E, KT]),
                                   iota_e[:, :].unsqueeze(2).broadcast_to([P, E, KT]), ALU.is_equal))
            dve.wait_ge(counted, 1)
            not_before = ps[:, 0, 0:E * KT]
            total = ps[:, 0, E * KT:2 * E * KT]
            flat = base[:, :, :].rearrange("p e n -> p (e n)")
            then(dve.tensor_tensor_scan(flat, carry[:, :, :].rearrange("p e n -> p (e n)"), total, 0.0, ALU.mult, ALU.add))
            then(dve.tensor_tensor(flat, flat, not_before, ALU.add))
            then(dve.tensor_tensor(flat, flat, onehot[:, :, :].rearrange("p e n -> p (e n)"), ALU.mult))
            then(dve.tensor_reduce(pos[:, :], base[:, :, :].rearrange("p e n -> p n e"), AX_X, ALU.add))
            then(dve.tensor_scalar(c3[:, :], pos[:, :], float(P), None, ALU.is_ge))
            for n in range(2, ST):
                then(dve.scalar_tensor_tensor(c3[:, :], pos[:, :], float(n * P), c3[:, :], ALU.is_ge, ALU.add))
            then(dve.scalar_tensor_tensor(spart[:, :], c3[:, :], -float(P), pos[:, :], ALU.mult, ALU.add))
            then(dve.scalar_tensor_tensor(grp[:, :], queue, float(ST), c3[:, :], ALU.mult, ALU.add))
            dve.tensor_tensor(eq[:, :, :], grp[:, :].unsqueeze(2).broadcast_to([P, KT, SLOTS]),
                              iota_g[:, :].unsqueeze(1).broadcast_to([P, KT, SLOTS]), ALU.is_equal).then_inc(placed_b, 1)
            for n in range(KT // 8):
                dve.tensor_tensor(in_slot[:, 8 * n:8 * n + 8, :], spart[:, 8 * n:8 * n + 8].unsqueeze(2).broadcast_to([P, 8, P]),
                                  iota_s[:, :].unsqueeze(1).broadcast_to([P, 8, P]), ALU.is_equal).then_inc(placed_b, 1)
            dve.wait_ge(table_done, 1)
            then(dve.tensor_scalar(row[:, :], ps[:, 1, SLOTS:2 * SLOTS], float(P), -float(P), ALU.mult, ALU.add))
            then(dve.tensor_tensor(row[:, :], row[:, :], ps[:, 1, 0:SLOTS], ALU.add))
            then(dve.tensor_scalar(adj[:, :], row[:, :], float(T), -float(T), ALU.is_ge, ALU.mult))
            then(dve.tensor_tensor(row[:, :], row[:, :], adj[:, :], ALU.add))
            then(dve.tensor_scalar(from_row[:, :], row[:, :], 0.0, None, ALU.max))
            dve.tensor_copy(gather_idx[0][:, :], from_row[:, 0:ST]).then_inc(gidx_ready, 1)
            dve.tensor_copy(gather_idx[1][:, :], from_row[:, ST:2 * ST]).then_inc(gidx_ready, 1)
            then(dve.tensor_scalar(adj[:, :], row[:, :], 0.0, 1e6, ALU.is_lt, ALU.mult))
            then(dve.tensor_tensor(to_row[:, :], row[:, :], adj[:, :], ALU.add))

            def scatter_rows(e, q, it):
                if not (isinstance(e, int) and e < 2):
                    dve.wait_ge(scattered[q], 16 * ST * it)
                dve.tensor_copy(scatter_idx[q][:, :], to_row[:, bass.ds(ST * e, ST)]).then_inc(sidx_ready, 1)

            def weights_part(e, q, n):
                dve.wait_ge(wh_ready, 4 * e + n + 1)
                if n < 2:
                    dve.tensor_tensor(w1_lo[q][:, n].rearrange("p c j -> p j c"), raw1[q][:, n, :].rearrange("p (j c) -> p j c", c=C),
                                      w1_hi[q][:, n].rearrange("p c j -> p j c").bitcast(F32), ALU.subtract).then_inc(wl_ready, 1)
                else:
                    k = n - 2
                    dve.tensor_tensor(w2_lo[q][:, 4 * k:4 * k + 4], raw2[q][:, 4 * k:4 * k + 4],
                                      w2_hi[q][:, 4 * k:4 * k + 4].bitcast(F32), ALU.subtract).then_inc(wl_ready, 1)

            def turn_rows(e, q):
                for k in range(2):
                    dve.wait_ge(xt_hi_ready, 2 * e + k + 1)
                    dve.tensor_tensor(XT_lo[q][:, k, :], xt_bank[:, k, :], XT_hi[q][:, k, :].bitcast(F32), ALU.subtract).then_inc(xt_lo_ready, 1)

            def step(e, q, it):
                if not static(e, E - 2):
                    dve.wait_ge(xt_done, e + 1)
                    dve.tensor_copy(gather_idx[q][:, :], from_row[:, bass.ds(ST * (e + 2), ST)]).then_inc(gidx_ready, 1)
                for c in range(C):
                    dve.wait_ge(hr_ready, C * e + c + 1)
                    if not (isinstance(e, int) and e < 1 and c < 4):
                        dve.wait_ge(f2_part, C * e + c - 3)
                    dve.tensor_copy(h_hi[c % 4][:, :], hr[c % 2][:, :]).then_inc(hh_ready, 1)
                    dve.wait_ge(hh_ready, C * e + c + 1)
                    dve.tensor_tensor(h_lo[c % 4][:, :], hr[c % 2][:, :], h_hi[c % 4][:, :].bitcast(F32), ALU.subtract).then_inc(hl_ready, 1)
                    if c % 2 and not static(e, E - 1):
                        weights_part(e + 1, 1 - q, c // 2)
                    if isinstance(e, int) and e < 1 and c == C - 1:
                        dve.wait_ge(gate_table_done, 1)
                        dve.tensor_reduce(slot_gate[:, :], h_bank[0][:, 0:3 * SLOTS].rearrange("p (a g) -> p g a", a=3), AX_X, ALU.add).then_inc(slot_gate_ready, 1)
                        dve.wait_ge(slot_gate_ready, 1)
                if not static(e, E - 1):
                    turn_rows(e + 1, 1 - q)
                scatter_rows(e, q, it)
                dve.wait_ge(f2_part, C * (e + 1))
                for n in range(2):
                    dve.tensor_tensor(Yb[:, 2 * n:2 * n + 2, :], y_bank[n].rearrange("p (j m) -> p j m", j=2),
                                      b2_bc[q][:, :].unsqueeze(1).broadcast_to([P, 2, D]), ALU.add).then_inc(biased, 1)
                for j in range(ST):
                    if j % 2 == 0:
                        wait_alone(dve, started, biased, 2 * e + j // 2 + 1)
                    dve.tensor_scalar(Y[q][:, j, :], Yb[:, j, :], slot_gate[:, bass.ds(ST * e + j, 1)], None, ALU.mult).then_inc(y_ready, 1)

            for n in range(4):
                weights_part(0, 0, n)
            dve.wait_ge(ratio_ready, 1)
            then(dve.tensor_scalar(den[:, :], ratio[:, :], 1.0, None, ALU.add))
            then(dve.reciprocal(gates[:, 0, :], den[:, :]))
            then(dve.tensor_tensor(gates[:, 1, :], gates[:, 0, :], ratio[:, :], ALU.mult))
            left = gates[:, :, :].rearrange("p k t -> p (k t)")
            for n in range(3):
                dve.tensor_copy(part[:, n, :], left).then_inc(gate_parts, 1)
                if n < 2:
                    dve.wait_ge(gate_parts, 2 * n + 1)
                    dve.tensor_tensor(rest[:, n, :], left, part[:, n, :], ALU.subtract).then_inc(gate_parts, 1)
                    left = rest[:, n, :]
                    dve.wait_ge(gate_parts, 2 * n + 2)
            turn_rows(0, 0)
            steps(step)(dve)

        @block.tensor
        def _(pe):
            pe.wait_ge(placed_a, 1)
            oh = onehot[:, :, :].rearrange("p e n -> p (e n)")
            pe.matmul(ps[:, 0, 0:E * KT], tri[:, :], oh, start=True, stop=True)
            pe.matmul(ps[:, 0, E * KT:2 * E * KT], onesb[:, :], oh, start=True, stop=True).then_inc(counted, 1)
            pe.wait_ge(placed_k, 2)
            for n in range(KT):
                if n % 8 == 0:
                    pe.wait_ge(placed_b, n // 8 + 2)
                last = pe.matmul(ps[:, 1, 0:2 * SLOTS], in_slot[:, n, :], in_tile[:, n].rearrange("p a g -> p (a g)"),
                                 start=(n == 0), stop=(n == KT - 1))
            last.then_inc(table_done, 1)

            def turn_rows(e, q, it):
                if isinstance(e, int) and e < 1:
                    pe.wait_ge(gidx_ready, 2)
                else:
                    pe.wait_ge(xt_lo_ready, 2 * e)
                for j in range(ST):
                    pe.wait_ge(gathered[q][j], 16 * (it + 1))
                    for k in range(2):
                        last = pe.transpose(xt_bank[:, k, j * P:(j + 1) * P], Xg[q][:, j, k * P:(k + 1) * P], ident[:, :])
                last.then_inc(xt_done, 1)

            def step(e, q, it):
                def layer1(c):
                    if c == 0:
                        pe.wait_ge(wl_ready, 4 * (e + 1))
                    if not (isinstance(e, int) and e < 1 and c < 4):
                        pe.wait_ge(hr_ready, C * e + c - 3)
                    if isinstance(e, int) and e == 1 and c == 0:
                        pe.wait_ge(slot_gate_ready, 1)
                    n = 0
                    for k in range(2):
                        if c == 0:
                            pe.wait_ge(xt_lo_ready, 2 * e + k + 1)
                        for w, a in ((w1_hi, XT_hi), (w1_lo, XT_hi), (w1_hi, XT_lo)):
                            n += 1
                            last = pe.matmul(h_bank[c % 4], w[q][:, k, c, :], a[q][:, k, :], start=(n == 1), stop=(n == 6))
                    last.then_inc(h_done, 1)

                def layer2(c):
                    pe.wait_ge(hl_ready, C * e + c + 1)
                    if c == 0 and not (isinstance(e, int) and e < 1):
                        pe.wait_ge(biased, 2 * e)
                    for j in range(ST):
                        for n, (a, w) in enumerate(((h_hi, w2_hi), (h_lo, w2_hi), (h_hi, w2_lo))):
                            last = pe.matmul(y_bank[j // 2][:, (j % 2) * D:(j % 2 + 1) * D], a[c % 4][:, j * P:(j + 1) * P], w[q][:, c, :],
                                             start=(c == 0 and n == 0 and j % 2 == 0), stop=(c == C - 1 and n == 2), skip_group_check=True)
                    last.then_inc(f2_part, 1)

                layer1(0)
                layer1(1)
                layer1(2)
                for c in range(C):
                    layer2(c)
                    if c + 3 < C:
                        layer1(c + 3)
                    if c == C - 4 and isinstance(e, int) and e < 1:
                        pe.wait_ge(in_gate_ready, 3)
                        pe.wait_ge(hr_ready, 5)
                        for n in range(KT):
                            last = pe.matmul(h_bank[0][:, 0:3 * SLOTS], in_slot[:, n, :], in_gate[:, n].rearrange("p a g -> p (a g)"),
                                             start=(n == 0), stop=(n == KT - 1))
                        last.then_inc(gate_table_done, 1)
                    if c == C - 4 and not static(e, E - 1):
                        turn_rows(e + 1, 1 - q, it + q)

            turn_rows(0, 0, 0)
            steps(step)(pe)


def program(nc, x, ctx_1024, Wq, Wk, Wv, bv, Wo, bo, wg, w1, b1, w2, b2, out):
    B, S, D = x.shape
    T = B * S
    C = w1.shape[2] // P
    KT = TOPK * T // P
    with ExitStack() as ctx:
        def sem(name):
            return ctx.enter_context(nc.semaphore(name))

        def sb(name, shape, dt):
            return ctx.enter_context(nc.sbuf_tensor(name, shape, dt))

        xn_rows = nc.dram_tensor("xn_rows", [T, D], F32, kind="Internal").ap()
        persist = {
            "x_all": sb("x_all", [P, T // P, D], F32),
            "ident": sb("ident", [P, P], F32),
            "dl_all": sb("dl_all", [P, T // P], F32),
            "expert_all": sb("expert_all", [P, TOPK, T // P], F32),
            "tri": sb("tri", [P, P], BF16),
            "onesb": sb("onesb", [P, P], BF16),
            "carry": sb("carry", [P, EXPERTS, KT], F32),
            "iota_e": sb("iota_e", [P, EXPERTS], F32),
            "iota_s": sb("iota_s", [P, P], BF16),
            "iota_g": sb("iota_g", [P, TOPK * T // P], F32),
            "iota_k": sb("iota_k", [P, KT], F32),
            "iota_p": sb("iota_p", [P, 1], F32),
            "raw1": [sb(f"raw1_{q}", [P, 2, C * P], F32) for q in range(2)],
            "raw2": [sb(f"raw2_{q}", [P, C, D], F32) for q in range(2)],
            "b1_sb": [sb(f"b1_sb{q}", [P, C], F32) for q in range(2)],
            "b2_bc": [sb(f"b2_bc{q}", [P, D], F32) for q in range(2)],
            "ps": ctx.enter_context(nc.psum_tensor("ps", [P, 8, 512], F32)),
            "weights_loaded": [sem(f"weights_loaded{q}") for q in range(2)],
            "biases_loaded": [sem(f"biases_loaded{q}") for q in range(2)],
            "started": sem("started"),
        }
        for part, args in ((attention, (x, ctx_1024, Wq, Wk, Wv, bv, Wo, bo, wg, w1, b1, w2, b2, xn_rows, out)),
                           (experts, (out, w1, b1, w2, b2, xn_rows))):
            with ExitStack() as own:
                part(nc, sem, lambda n, s, d: own.enter_context(nc.sbuf_tensor(n, s, d)), persist, *args)


_INS = ['x', 'ctx_1024', 'L0_xattn_W_q', 'L0_xattn_W_k', 'L0_xattn_W_v', 'L0_xattn_b_v', 'L0_xattn_W_o', 'L0_xattn_b_o',
        'L0_ffn_wg', 'L0_ffn_w1', 'L0_ffn_b1', 'L0_ffn_w2', 'L0_ffn_b2']


def kernel(**inputs):
    import numpy as _np
    import concourse.bacc as _bacc
    from concourse import mybir as _mybir
    from concourse.bass_utils import run_bass_kernel_spmd as _run

    nc = _bacc.Bacc("TRN2", target_bir_lowering=False, num_devices=1)
    arrays, args = {}, []
    for name in _INS:
        a = _np.ascontiguousarray(inputs[name])
        arrays[f"in_{name}_dram"] = a
        args.append(nc.dram_tensor(f"in_{name}_dram", a.shape, _mybir.dt.from_np(a.dtype), kind="ExternalInput").ap())
    out = nc.dram_tensor("out_0_dram", inputs["x"].shape, F32, kind="ExternalOutput").ap()
    program(nc, *args, out)
    r = _run(nc, [arrays], core_ids=[0])
    return r.results[0]["out_0_dram"]
```

```python
from contextlib import ExitStack

import concourse.bass as bass
from concourse import mybir

P = 128
F32 = mybir.dt.float32
F32R = mybir.dt.float32r
BF16 = mybir.dt.bfloat16
I32 = mybir.dt.int32
U32 = mybir.dt.uint32
ALU = mybir.AluOpType
ACT = mybir.ActivationFunctionType
AX_X = mybir.AxisListType.X

HEADS = 16
HD = 16
HPG = 4
GROUPS = HEADS // HPG
VW = 32
ROWS = 3 * HD
EPS = 1e-5
MASKED = -1e38
WEIGHT_PARTS = (0, 4, 8, 9, 10)
UNITS = 3 * GROUPS
EXPERTS = 8
TOPK = 2


def wait_alone(eng, started, semaphore, value):
    if not isinstance(value, int):
        value = eng.to_reg(value)
    eng.wait_ge(started, 1)
    eng.wait_ge(semaphore, value)


def attention(nc, sem, sb, persist, x, ctx_in, Wq, Wk, Wv, bv, Wo, bo, wg, w1, b1, w2, b2, xn_rows, out):
    B, S, D = x.shape
    x_all, ident, dl_all, expert_all, ps = (persist[k] for k in ("x_all", "ident", "dl_all", "expert_all", "ps"))
    raw1, raw2, b1_sb, b2_bc = (persist[k] for k in ("raw1", "raw2", "b1_sb", "b2_bc"))
    tri, onesb, carry = (persist[k] for k in ("tri", "onesb", "carry"))
    iota_e, iota_s, iota_g, iota_k, iota_p = (persist[k] for k in ("iota_e", "iota_s", "iota_g", "iota_k", "iota_p"))
    started = persist["started"]
    weights_loaded, biases_loaded = persist["weights_loaded"], persist["biases_loaded"]

    max_bank = [ps[:, 0, :], ps[:, 1, :]]
    prob_score = ps[:, 3:6, :].rearrange("p a b -> p (a b)")
    value_bank = ps[:, 7, :]
    bank = [ps[:, 2, :], ps[:, 6, :]]

    w_raw = sb("w_raw", [P, 4, 2, D], F32)
    w_hi = sb("w_hi", [P, 4, 2, D], F32R)
    w_lo = sb("w_lo", [P, 4, 2, D], F32R)
    bv_bc = sb("bv_bc", [P, D], F32)
    bo_bc = sb("bo_bc", [P, D], F32)
    wg_sb = sb("wg_sb", [P, 2, EXPERTS], F32)
    identb = sb("identb", [P, P], BF16)
    mask0 = sb("mask0", [P, HPG, P], BF16)
    mask1 = sb("mask1", [P, 2, P], BF16)
    half = sb("half", [P, 2], F32)
    c_sb = sb("c_sb", [P, 2, D], F32)
    xn = sb("xn", [P, 2, D], F32)
    st1 = sb("st1", [P, 2, 6], F32)
    mv1 = sb("mv1", [P, 2, 2], F32)
    ve1 = sb("ve1", [P, 2, 2], F32)
    rs1 = sb("rs1", [P, 2, 2], F32)
    st2 = sb("st2", [P, 2, 6], F32)
    mv2 = sb("mv2", [P, 2, 2], F32)
    ve2 = sb("ve2", [P, 2, 2], F32)
    rs2 = sb("rs2", [P, 2, 2], F32)
    xT_hi = sb("xT_hi", [P, 2, S], F32R)
    xT_lo = sb("xT_lo", [P, 2, S], F32R)
    cT_hi = sb("cT_hi", [P, 2, S], F32R)
    cT_lo = sb("cT_lo", [P, 2, S], F32R)
    q_hi = sb("q_hi", [P, 2, S], F32R)
    q_lo = sb("q_lo", [P, 2, S], F32R)
    k_hi = sb("k_hi", [P, 2, S], F32R)
    k_lo = sb("k_lo", [P, 2, S], F32R)
    Qs = [sb(f"Qs{q}", [ROWS + 2, HEADS, S], F32R) for q in range(2)]
    Ks = [sb(f"Ks{q}", [ROWS + 2, HEADS, S], F32R) for q in range(2)]
    V = [sb(f"V{q}", [P, 2, HEADS, VW], F32) for q in range(2)]
    nm = sb("nm", [P, 2, HEADS], F32)
    nm_s = sb("nm_s", [P, 2, 2, HEADS], F32R)
    nmT = sb("nmT", [2 * HEADS, S], F32)
    PT = [sb(f"PT{g}", [P, HPG * (S + P)], F32) for g in range(2)]
    OT = sb("OT", [P, GROUPS, S], F32)
    rec = sb("rec", [P, 2, HEADS], F32)
    attn = sb("attn", [P, 2, HEADS, HD], F32)
    aT_hi = sb("aT_hi", [P, 2, S], F32R)
    aT_lo = sb("aT_lo", [P, 2, S], F32R)
    x2n = sb("x2n", [P, 2, D], F32)
    x2T = sb("x2T", [P, 2, S], F32)
    lg = sb("lg", [P, 2, EXPERTS], F32)
    top8 = sb("top8", [P, 2, 8], F32)
    idx8 = sb("idx8", [P, 2, 8], U32)

    x0_loaded, x_loaded = sem("x0_loaded"), sem("x_loaded")
    ctx_loaded = sem("ctx_loaded")
    wqkvo_loaded = [sem(f"w{n}_loaded") for n in "qkvo"]
    small_loaded = sem("small_loaded")
    const_tmp, const_ready, ones_ready, v_padded = sem("const_tmp"), sem("const_ready"), sem("ones_ready"), sem("v_padded")
    w_hi_ready, w_lo_ready = sem("w_hi_ready"), sem("w_lo_ready")
    ln1_stats, ln1_pow, xn_ready, xbo_ready = sem("ln1_stats"), sem("ln1_pow"), sem("xn_ready"), sem("xbo_ready")
    tx_done, tc_done = sem("tx_done"), sem("tc_done")
    xT_hi_ready, xT_lo_ready = sem("xT_hi_ready"), sem("xT_lo_ready")
    cT_hi_ready, cT_lo_ready = sem("cT_hi_ready"), sem("cT_lo_ready")
    q_done, k_done, v_done = sem("q_done"), sem("k_done"), sem("v_done")
    q_hi_ready, q_lo_ready = sem("q_hi_ready"), sem("q_lo_ready")
    k_hi_ready, k_lo_ready = sem("k_hi_ready"), sem("k_lo_ready")
    v_ready = sem("v_ready")
    q_stacked, k_stacked, max_stacked = sem("q_stacked"), sem("k_stacked"), sem("max_stacked")
    a_done, max_done, nm_ready, nmT_done, nmT_ready = (sem(n) for n in ("a_done", "max_done", "nm_ready", "nmT_done", "nmT_ready"))
    b_done, exp_done, mask_done, av_done, ot_ready = (sem(n) for n in ("b_done", "exp_done", "mask_done", "av_done", "ot_ready"))
    ott_done, rec_ready, norm_done = sem("ott_done"), sem("rec_ready"), sem("norm_done")
    at_done, aT_hi_ready, aT_lo_ready, op_done = sem("at_done"), sem("aT_hi_ready"), sem("aT_lo_ready"), sem("op_done")
    x2_ready, ln2_stats, ln2_pow, x2n_ready, x2n_stored = (sem(n) for n in ("x2_ready", "ln2_stats", "ln2_pow", "x2n_ready", "x2n_stored"))
    x2t_done, x2T_ready, rt_done, lg_ready, top_ready, top_used = (sem(n) for n in ("x2t_done", "x2T_ready", "rt_done", "lg_ready", "top_ready", "top_used"))
    x2_stored = sem("x2_stored")

    x_tiles = x.rearrange("b (t p) m -> p (b t) m", p=P)
    ctx_tiles = ctx_in.rearrange("b (t p) m -> b p t m", p=P)
    out_tiles = out.rearrange("b (t p) m -> b p t m", p=P)
    xn_tiles = xn_rows.rearrange("(b t p) m -> b p t m", t=2, p=P)

    def steps(eng, step):
        step(-2, 0, max_part=False, score_part=False, out_part=False)
        step(-1, 1, score_part=False, out_part=False)
        step(0, 0, out_part=False)
        with eng.Fori(0, (B - 4) // 2) as it:
            step(2 * it + 1, 1)
            step(2 * it + 2, 0)
        step(B - 3, (B - 3) % 2)
        step(B - 2, (B - 2) % 2, proj_part=False)
        step(B - 1, (B - 1) % 2, proj_part=False, max_part=False)
        step(B, B % 2, proj_part=False, max_part=False, score_part=False)

    def max_unit(u):
        g, part = divmod(u, 3)
        return (1, HPG * g + 2 * part, 2) if part < 2 else (0, HPG * g, HPG)

    def is_head(max_part, score_part):
        return max_part and not score_part

    def is_late(proj_part, score_part):
        return score_part and not proj_part

    def first(s, n):
        return isinstance(s, int) and s < n

    def weight_views(n, dst):
        if n >= 2:
            return [(dst[:, n].rearrange("p a b -> p (a b)"), w_raw[:, n].rearrange("p a b -> p (a b)"))]
        out = []
        for k in range(2):
            src = w_raw[:, n, k, :].rearrange("p (h f d) -> p f d h", f=2, d=HD)
            to = dst[:, n, k, :].rearrange("p (f d h) -> p f d h", f=2, d=HD)
            out += [(to[:, f], src[:, f]) for f in range(2)]
        return out

    block = nc.Block()
    with block:

        @block.sync
        def _(sp):
            sp.dma_start(x_all[:, 0:2, :], x_tiles[:, 0:2, :]).then_inc(x0_loaded, 16)
            sp.dma_start(c_sb[:, :, :], ctx_tiles[0]).then_inc(ctx_loaded, 16)
            sp.dma_start(w_raw[:, 0], Wq.rearrange("(k p) n -> p k n", p=P)).then_inc(wqkvo_loaded[0], 16)
            sp.dma_start(w_raw[:, 1], Wk.rearrange("(k p) n -> p k n", p=P)).then_inc(wqkvo_loaded[1], 16)
            sp.dma_start(w_raw[:, 2], Wv.rearrange("(k p) n -> p k n", p=P)).then_inc(wqkvo_loaded[2], 16)
            sp.dma_start(w_raw[:, 3], Wo.rearrange("(k p) n -> p k n", p=P)).then_inc(wqkvo_loaded[3], 16)
            sp.dma_start(x_all[:, 2:, :], x_tiles[:, 2:, :]).then_inc(x_loaded, 16)

            def stack(dst, row, src, done):
                sp.dma_start(dst[row:row + HD, :, :].rearrange("d (h f) t -> d h (f t)", f=2).bitcast(F32),
                             src[:, :, :].rearrange("p f t -> p (f t)").bitcast(F32)).then_inc(done, 16)

            def step(s, q, proj_part=True, max_part=True, score_part=True, out_part=True):
                def stack_maxima():
                    wait_alone(sp, started, nmT_ready, s + 2)
                    sp.dma_start(Qs[1 - q][ROWS:ROWS + 2, :, :].bitcast(F32),
                                 nmT[:, :]).then_inc(max_stacked, 16)

                if proj_part and not (isinstance(s, int) and s + 3 >= B):
                    wait_alone(sp, started, tc_done, s + 3)
                    sp.dma_start(c_sb[:, :, :], ctx_tiles[s + 3]).then_inc(ctx_loaded, 16)
                if out_part:
                    wait_alone(sp, started, x2n_ready, 2 * s)
                    sp.dma_start(xn_tiles[s - 1], x2n[:, :, :]).then_inc(x2n_stored, 16)
                    sp.dma_start(out_tiles[s - 1], x_all[:, bass.ds(2 * (s - 1), 2), :]).then_inc(x2_stored, 16)
                if is_head(max_part, score_part):
                    stack_maxima()
                if proj_part:
                    if first(s, 0):
                        sp.wait_ge(ones_ready, 2 * (s + 2) + 1)
                    else:
                        wait_alone(sp, started, b_done, GROUPS * (s + 1))
                    sp.wait_ge(q_hi_ready, s + 3)
                    stack(Qs[q], 0, q_hi, q_stacked)
                    stack(Qs[q], 2 * HD, q_hi, q_stacked)
                    sp.wait_ge(q_lo_ready, s + 3)
                    stack(Qs[q], HD, q_lo, q_stacked)
                    wait_alone(sp, started, k_hi_ready, s + 3)
                    stack(Ks[q], 0, k_hi, k_stacked)
                    stack(Ks[q], HD, k_hi, k_stacked)
                    sp.wait_ge(k_lo_ready, s + 3)
                    stack(Ks[q], 2 * HD, k_lo, k_stacked)
                if max_part and score_part:
                    stack_maxima()

            steps(sp, step)
            sp.wait_ge(x2n_stored, 16 * (B + 1))
            sp.wait_ge(x2_stored, 16 * B)

        @block.gpsimd
        def _(pool):
            pool.dma_start(bv_bc[:, :], bv.rearrange("(a n) -> a n", a=1).broadcast_to([P, D])).then_inc(small_loaded, 16)
            pool.dma_start(bo_bc[:, :], bo.rearrange("(a n) -> a n", a=1).broadcast_to([P, D])).then_inc(small_loaded, 16)
            pool.dma_start(wg_sb[:, :, :], wg.rearrange("(k p) e -> p k e", p=P)).then_inc(small_loaded, 16)
            pool.memset(ident[:, :], 1.0).then_inc(const_tmp, 1)
            pool.wait_ge(const_tmp, 1)
            pool.affine_select(ident[:, :], ident[:, :], [[-1, P]], ALU.is_equal, 0.0, base=0, channel_multiplier=1).then_inc(const_ready, 1)

            def buffer_constants(q):
                pool.memset(Ks[q][:, :, :].bitcast(F32), 1.0).then_inc(ones_ready, 1)
                pool.memset(V[q][:, :, :, HD:], 0.0).then_inc(v_padded, 1)
                pool.wait_ge(v_padded, q + 1)
                pool.memset(V[q][:, :, :, HD:HD + 1], 1.0).then_inc(ones_ready, 1)

            def mask_constants():
                pool.memset(identb[:, :], 1.0).then_inc(const_tmp, 1)
                pool.memset(mask0[:, :, :], 0.0).then_inc(const_tmp, 1)
                pool.memset(mask1[:, :, :], 0.0).then_inc(const_tmp, 1)
                pool.wait_ge(const_tmp, 4)
                pool.affine_select(identb[:, :], identb[:, :], [[-1, P]], ALU.is_equal, 0.0, base=0, channel_multiplier=1).then_inc(const_ready, 1)
                pool.affine_select(mask1[:, :, :], mask1[:, :, :], [[0, 2], [-1, P]], ALU.is_gt, MASKED, base=0, channel_multiplier=1).then_inc(const_ready, 1)
                pool.affine_select(mask0[:, :, :], mask0[:, :, :], [[0, HPG], [-1, P]], ALU.is_gt, MASKED, base=0, channel_multiplier=1).then_inc(const_tmp, 1)
                pool.wait_ge(const_tmp, 5)
                pool.memset(mask0[0:1, :, 0:1], 0.0).then_inc(const_ready, 1)

            def routing_constants():
                exact = dict(allow_small_or_imprecise_dtypes=True)
                pool.memset(tri[:, :], -1.0).then_inc(const_tmp, 1)
                pool.memset(onesb[:, :], 1.0).then_inc(const_tmp, 1)
                pool.memset(carry[:, :, :], 1.0).then_inc(const_tmp, 1)
                pool.iota(iota_e[:, :], [[1, EXPERTS]], base=0, channel_multiplier=0, **exact).then_inc(const_tmp, 1)
                pool.iota(iota_s[:, :], [[1, P]], base=0, channel_multiplier=0, **exact).then_inc(const_tmp, 1)
                pool.iota(iota_g[:, :], [[1, iota_g.shape[1]]], base=0, channel_multiplier=0, **exact).then_inc(const_tmp, 1)
                pool.iota(iota_k[:, :], [[1, iota_k.shape[1]]], base=1, channel_multiplier=0, **exact).then_inc(const_tmp, 1)
                pool.iota(iota_p[:, :], [[1, 1]], base=0, channel_multiplier=1, **exact).then_inc(const_tmp, 1)
                pool.wait_ge(const_tmp, 8)
                pool.affine_select(tri[:, :], tri[:, :], [[-1, P]], ALU.is_ge, 0.0, base=0, channel_multiplier=1).then_inc(const_tmp, 1)
                pool.memset(carry[:, :, 0:1], 0.0).then_inc(const_tmp, 1)

            def powers(n, stats, mv, ve, rs, done):
                wait_alone(pool, started, stats, 4 * n + 4)
                pool.tensor_scalar(ve[:, 0, :], mv[:, :, 1], EPS, None, ALU.add).then_inc(done, 1)
                pool.tensor_scalar(ve[:, 1, :], mv[:, :, 0], -1.0, None, ALU.mult).then_inc(done, 1)
                wait_alone(pool, started, done, 4 * n + 2)
                pool.tensor_tensor(rs[:, 0, :], ve[:, 0, :], half[:, :], ALU.pow).then_inc(done, 1)
                wait_alone(pool, started, done, 4 * n + 3)
                pool.tensor_tensor(rs[:, 1, :], ve[:, 1, :], rs[:, 0, :], ALU.mult).then_inc(done, 1)

            def norm_powers(n):
                powers(n, ln1_stats, mv1, ve1, rs1, ln1_pow)

            def add_bias(n):
                pool.wait_ge(xn_ready, 2 * (n + 1))
                if first(n, 1):
                    pool.wait_ge(small_loaded, 48)
                xs = x_all[:, bass.ds(2 * n, 2), :]
                pool.tensor_tensor(xs, xs, bo_bc[:, :].unsqueeze(1).broadcast_to([P, 2, D]), ALU.add).then_inc(xbo_ready, 1)

            def step(s, q, proj_part=True, max_part=True, score_part=True, out_part=True):
                def mask(g):
                    wait_alone(pool, started, exp_done, GROUPS * s + g + 1)
                    p0 = PT[g % 2][:, 0:HPG * S].rearrange("p (h i) -> p h i", h=HPG)
                    p1 = PT[g % 2][:, HPG * S:].rearrange("p (h i) -> p h i", h=HPG)
                    pool.affine_select(p0[:, :, 0:1], p0[:, :, 0:1], [[0, HPG], [0, 1]], ALU.is_ge, 0.0, base=0, channel_multiplier=-1)
                    pool.affine_select(p0[:, :, 1:P], p0[:, :, 1:P], [[0, HPG], [1, P - 1]], ALU.is_gt, 0.0, base=1, channel_multiplier=-1).then_inc(mask_done, 1)
                    pool.affine_select(p1, p1, [[0, HPG], [1, P]], ALU.is_gt, 0.0, base=0, channel_multiplier=-1).then_inc(mask_done, 1)

                if first(s, -1):
                    norm_powers(0)
                if proj_part:
                    add_bias(s + 2)
                if first(s, -1):
                    buffer_constants(0)
                    mask_constants()
                if score_part:
                    mask(0)
                if is_late(proj_part, score_part):
                    mask(1)
                if out_part:
                    powers(s - 1, ln2_stats, mv2, ve2, rs2, ln2_pow)
                if score_part and not is_late(proj_part, score_part):
                    mask(1)
                if proj_part and not (isinstance(s, int) and s + 3 >= B):
                    norm_powers(s + 3)
                if first(s, -1):
                    buffer_constants(1)
                    routing_constants()
                if score_part:
                    mask(2)
                    mask(3)

            steps(pool, step)
            pool.wait_ge(const_tmp, 15)

        @block.scalar
        def _(act):
            def prefetch(n):
                e = n // 2
                if n % 2 == 0:
                    act.dma_start(raw1[e][:, :, :], w1[e].rearrange("(k p) h -> p k h", p=P)).then_inc(weights_loaded[e], 16)
                    act.dma_start(b1_sb[e][:, :], b1[e].rearrange("(p c) -> p c", p=P)).then_inc(biases_loaded[e], 16)
                else:
                    act.dma_start(raw2[e][:, :, :], w2[e].rearrange("(p c) m -> p c m", p=P)).then_inc(weights_loaded[e], 16)
                    act.dma_start(b2_bc[e][:, :], b2[e:e + 1, :].broadcast_to([P, D])).then_inc(biases_loaded[e], 16)

            def round_weights(n):
                act.wait_ge(wqkvo_loaded[n], 16)
                for dst, src in weight_views(n, w_hi):
                    act.activation(dst, src, ACT.Copy).then_inc(w_hi_ready, 1)

            def round_bank(dst, src):
                return act.activation(dst[:, :, :].rearrange("p a b -> p (a b)"), src, ACT.Copy)

            def normalise(dst, n, mean_scale, done):
                for t in range(2):
                    x_tile = x_all[:, bass.ds(2 * n + t, 1), :].rearrange("p a m -> p (a m)")
                    act.activation(dst[:, t, :], x_tile, ACT.Identity, bias=mean_scale[:, 1, t:t + 1],
                                   scale=mean_scale[:, 0, t:t + 1]).then_inc(done, 1)

            def norm_x(n):
                wait_alone(act, started, ln1_pow, 4 * (n + 1))
                if not first(n, 1):
                    wait_alone(act, started, tx_done, n)
                normalise(xn, n, rs1, xn_ready)

            def step(s, q, proj_part=True, max_part=True, score_part=True, out_part=True):
                def exp(g):
                    act.wait_ge(b_done, GROUPS * s + g + 1)
                    if g >= 2:
                        act.wait_ge(av_done, GROUPS * s + g - 1)
                    elif not first(s, 1):
                        act.wait_ge(av_done, GROUPS * (s - 1) + g + 3)
                    act.activation(PT[g % 2][:, :], prob_score, ACT.Exp, scale=float(HD) ** -0.5).then_inc(exp_done, 1)

                def values(n):
                    act.wait_ge(av_done, GROUPS * s + 2 * n + 2)
                    if not first(s, 1):
                        act.wait_ge(ott_done, 2 * s)
                    act.activation(OT[:, 2 * n:2 * n + 2, :].rearrange("p a b -> p (a b)"), value_bank, ACT.Copy).then_inc(ot_ready, 1)

                def round_attention():
                    act.wait_ge(at_done, s)
                    round_bank(aT_hi, bank[1]).then_inc(aT_hi_ready, 1)

                def round_x():
                    act.wait_ge(tx_done, s + 3)
                    if not first(s, -1):
                        act.wait_ge(q_done, s + 2)
                    round_bank(xT_hi, bank[0]).then_inc(xT_hi_ready, 1)

                def round_context():
                    act.wait_ge(tc_done, s + 3)
                    if not first(s, -1):
                        act.wait_ge(v_done, s + 2)
                    round_bank(cT_hi, bank[0]).then_inc(cT_hi_ready, 1)

                def round_queries():
                    act.wait_ge(q_done, s + 3)
                    if not first(s, -1):
                        act.wait_ge(q_stacked, 48 * (s + 2))
                    round_bank(q_hi, bank[1]).then_inc(q_hi_ready, 1)

                def round_keys():
                    act.wait_ge(k_done, s + 3)
                    if not first(s, -1):
                        act.wait_ge(k_stacked, 48 * (s + 2))
                    round_bank(k_hi, bank[0]).then_inc(k_hi_ready, 1)

                def normalise_x2():
                    act.wait_ge(ln2_pow, 4 * s)
                    act.wait_ge(x2n_stored, 16 * s)
                    normalise(x2n, s - 1, rs2, x2n_ready)

                def copy_x2():
                    act.wait_ge(x2t_done, s)
                    round_bank(x2T, bank[1]).then_inc(x2T_ready, 1)

                def copy_maxima():
                    act.wait_ge(nmT_done, s + 2)
                    if not first(s, 0):
                        act.wait_ge(max_stacked, 16 * (s + 1))
                    act.activation(nmT[:, :], bank[1][0:2 * HEADS, 0:S], ACT.Copy).then_inc(nmT_ready, 1)

                if is_head(max_part, score_part):
                    round_x()
                    round_context()
                    copy_maxima()
                    norm_x(s + 3)
                    round_queries()
                    round_keys()
                elif is_late(proj_part, score_part):
                    if score_part:
                        exp(0)
                    if out_part:
                        round_attention()
                    if score_part:
                        exp(1)
                        exp(2)
                    if out_part:
                        normalise_x2()
                    if score_part:
                        values(0)
                        exp(3)
                    if out_part:
                        copy_x2()
                    if max_part:
                        copy_maxima()
                    if score_part:
                        values(1)
                    prefetch(s - (B - 2) + 2)
                else:
                    if out_part:
                        round_attention()
                    if proj_part:
                        round_x()
                    if score_part:
                        exp(0)
                        exp(1)
                    if proj_part:
                        round_context()
                    if first(s, -1):
                        round_weights(2)
                    if proj_part:
                        round_queries()
                    if out_part:
                        normalise_x2()
                    if proj_part:
                        round_keys()
                    if first(s, -1):
                        round_weights(3)
                    if out_part:
                        copy_x2()
                    if score_part:
                        exp(2)
                    if isinstance(s, int) and s in (0, B - 3):
                        prefetch(s != 0)
                    if proj_part and not (isinstance(s, int) and s + 3 >= B):
                        norm_x(s + 3)
                    if score_part:
                        values(0)
                        exp(3)
                        values(1)
                    if max_part:
                        copy_maxima()

            round_weights(0)
            norm_x(0)
            round_weights(1)
            steps(act, step)

        @block.vector
        def _(dve):
            dve.memset(half[:, :], -0.5).then_inc(started, 1)
            dve.memset(x2n[:, :, :], 0.0).then_inc(x2n_stored, 16)

            def norm_stats(tiles, st, mv, stats, n):
                for t in range(2):
                    dve.bn_stats(st[:, t, :], tiles[:, t, :]).then_inc(stats, 1)
                wait_alone(dve, started, stats, 4 * n + 2)
                for t in range(2):
                    dve.bn_aggr(mv[:, t, :], st[:, t, :]).then_inc(stats, 1)

            def split_weights(n):
                for m, ((lo, src), (hi, _)) in enumerate(zip(weight_views(n, w_lo), weight_views(n, w_hi))):
                    dve.wait_ge(w_hi_ready, WEIGHT_PARTS[n] + m + 1)
                    dve.tensor_tensor(lo, src, hi.bitcast(F32), ALU.subtract).then_inc(w_lo_ready, 1)

            def split_lo(lo, hi, src, hi_ready, n, done):
                dve.wait_ge(hi_ready, n)
                dve.tensor_tensor(lo[:, :, :].rearrange("p a b -> p (a b)"), src,
                                  hi[:, :, :].rearrange("p a b -> p (a b)").bitcast(F32), ALU.subtract).then_inc(done, 1)

            def top_two(n):
                wait_alone(dve, started, lg_ready, n + 1)
                for t in range(2):
                    dve.max(top8[:, t, :], lg[:, t, :]).then_inc(top_ready, 1)
                wait_alone(dve, started, top_ready, 4 * n + 2)
                for t in range(2):
                    dve.max_index(idx8[:, t, :], top8[:, t, :], lg[:, t, :]).then_inc(top_ready, 1)
                dve.tensor_tensor(dl_all[:, bass.ds(2 * n, 2)], top8[:, :, 1], top8[:, :, 0], ALU.subtract).then_inc(top_used, 1)
                dve.wait_ge(top_ready, 4 * n + 4)
                for k in range(TOPK):
                    dve.tensor_copy(expert_all[:, k, bass.ds(2 * n, 2)], idx8[:, :, k]).then_inc(top_used, 1)

            def step(s, q, proj_part=True, max_part=True, score_part=True, out_part=True):
                def maxima(pair):
                    for u in (2 * pair, 2 * pair + 1):
                        dve.wait_ge(a_done, UNITS * (s + 1) + u + 1)
                        if u == 0 and not first(s, 0):
                            dve.wait_ge(nm_ready, 2 * (s + 1))
                        tile, h, count = max_unit(u)
                        dve.tensor_reduce(nm[:, tile, h:h + count], max_bank[u % 2].rearrange("p (h j) -> p h j", h=count),
                                          AX_X, ALU.max, negate=True).then_inc(max_done, 1)

                def normalise(t):
                    dve.wait_ge(ott_done, 2 * (s - 1) + t + 1)
                    heads = bank[1 - t].rearrange("p (h c) -> p h c", c=VW)
                    dve.reciprocal(rec[:, t, :], heads[:, :, HD]).then_inc(rec_ready, 1)
                    dve.wait_ge(rec_ready, 2 * (s - 1) + t + 1)
                    dve.tensor_tensor(attn[:, t], heads[:, :, 0:HD], rec[:, t, :].unsqueeze(2).broadcast_to([P, HEADS, HD]),
                                      ALU.mult).then_inc(norm_done, 1)

                if first(s, -1):
                    dve.wait_ge(x0_loaded, 16)
                    norm_stats(x_all[:, 0:2, :], st1, mv1, ln1_stats, 0)
                    split_weights(0)
                    split_weights(1)
                def add_value_bias():
                    dve.wait_ge(v_done, s + 2)
                    if first(s, 1):
                        dve.wait_ge(ones_ready, 2 * (s + 2))
                        dve.wait_ge(small_loaded, 48)
                    dve.tensor_tensor(V[1 - q][:, :, :, 0:HD],
                                      bank[0].rearrange("p (t h d) -> p t h d", t=2, h=HEADS),
                                      bv_bc[:, :].rearrange("p (h d) -> p h d", h=HEADS).unsqueeze(1).broadcast_to([P, 2, HEADS, HD]),
                                      ALU.add).then_inc(v_ready, 1)

                def add_output():
                    x2 = x_all[:, bass.ds(2 * (s - 1), 2), :]
                    dve.wait_ge(op_done, s)
                    dve.wait_ge(xbo_ready, s)
                    dve.tensor_tensor(x2, bank[1].rearrange("p (t m) -> p t m", t=2), x2, ALU.add).then_inc(x2_ready, 1)
                    wait_alone(dve, started, x2_ready, s)
                    norm_stats(x2, st2, mv2, ln2_stats, s - 1)

                def next_stats():
                    if first(s, -1):
                        dve.wait_ge(x_loaded, 16)
                    dve.wait_ge(xn_ready, 2 * (s + 3))
                    norm_stats(x_all[:, bass.ds(2 * (s + 3), 2), :], st1, mv1, ln1_stats, s + 3)

                def logits():
                    dve.wait_ge(rt_done, s)
                    dve.tensor_copy(lg[:, :, :], bank[0][:, 0:2 * EXPERTS].rearrange("p (t e) -> p t e", t=2)).then_inc(lg_ready, 1)
                    top_two(s - 1)

                def split_maxima():
                    dve.wait_ge(max_done, UNITS * (s + 2))
                    if not first(s, 0):
                        dve.wait_ge(nmT_done, s + 1)
                    dve.tensor_copy(nm_s[:, :, 0, :], nm[:, :, :]).then_inc(nm_ready, 1)
                    dve.wait_ge(nm_ready, 2 * (s + 1) + 1)
                    dve.tensor_tensor(nm_s[:, :, 1, :], nm[:, :, :], nm_s[:, :, 0, :].bitcast(F32), ALU.subtract).then_inc(nm_ready, 1)

                def split_x():
                    split_lo(xT_lo, xT_hi, bank[0], xT_hi_ready, s + 3, xT_lo_ready)

                def split_context():
                    split_lo(cT_lo, cT_hi, bank[0], cT_hi_ready, s + 3, cT_lo_ready)

                def split_queries():
                    split_lo(q_lo, q_hi, bank[1], q_hi_ready, s + 3, q_lo_ready)

                def split_keys():
                    split_lo(k_lo, k_hi, bank[0], k_hi_ready, s + 3, k_lo_ready)

                def split_attention():
                    split_lo(aT_lo, aT_hi, bank[1], aT_hi_ready, s, aT_lo_ready)

                if is_head(max_part, score_part):
                    add_value_bias()
                    split_x()
                    maxima(0)
                    split_context()
                    for pair in range(1, UNITS // 2):
                        maxima(pair)
                    split_maxima()
                    next_stats()
                    split_queries()
                    split_keys()
                elif is_late(proj_part, score_part):
                    if max_part:
                        add_value_bias()
                    if out_part:
                        normalise(0)
                        normalise(1)
                    if max_part:
                        maxima(0)
                    if out_part:
                        split_attention()
                    if max_part:
                        maxima(1)
                    if out_part:
                        add_output()
                    if max_part:
                        maxima(2)
                        maxima(3)
                        maxima(4)
                        maxima(5)
                        split_maxima()
                    if out_part:
                        logits()
                else:
                    if max_part:
                        add_value_bias()
                    if out_part:
                        normalise(0)
                        normalise(1)
                        split_attention()
                    if proj_part:
                        split_x()
                    if max_part:
                        maxima(0)
                    if out_part:
                        add_output()
                    if max_part:
                        maxima(1)
                    if proj_part:
                        split_context()
                    if first(s, -1):
                        split_weights(2)
                    if proj_part:
                        split_queries()
                    if proj_part and not first(s, -1) and not (isinstance(s, int) and s + 3 >= B):
                        next_stats()
                    if proj_part:
                        split_keys()
                    if first(s, -1):
                        next_stats()
                        split_weights(3)
                    if max_part:
                        maxima(2)
                        maxima(3)
                    if out_part:
                        logits()
                    if max_part:
                        maxima(4)
                        maxima(5)
                        split_maxima()

            steps(dve, step)
            dve.wait_ge(top_used, 3 * B)

        @block.tensor
        def _(pe):
            def step(s, q, proj_part=True, max_part=True, score_part=True, out_part=True):
                def a_scores(pair):
                    Q, K = Qs[1 - q], Ks[1 - q]
                    for u in (2 * pair, 2 * pair + 1):
                        if u == 0:
                            pe.wait_ge(q_stacked, 48 * (s + 2))
                            pe.wait_ge(k_stacked, 48 * (s + 2))
                            if first(s, 0):
                                pe.wait_ge(const_ready, 4)
                        if not (first(s, 0) and u < 2):
                            pe.wait_ge(max_done, UNITS * (s + 1) + u - 1)
                        tile, h0, count = max_unit(u)
                        width = (tile + 1) * P
                        for h in range(count):
                            pe.matmul(max_bank[u % 2][:, h * width:(h + 1) * width], Q[0:ROWS, h0 + h, tile * P:(tile + 1) * P],
                                      K[0:ROWS, h0 + h, 0:width], start=(h == 0), stop=False, skip_group_check=True)
                        diag = max_bank[u % 2].rearrange("p (h j) -> p h j", h=count)[:, :, tile * P:]
                        pe.matmul(diag, identb[:, :], mask1[:, :, :] if tile else mask0[:, :, :],
                                  start=False, stop=True, skip_group_check=True).then_inc(a_done, 1)

                def b_scores(g):
                    if g == 0:
                        pe.wait_ge(max_stacked, 16 * (s + 1))
                    if not (first(s, 1) and g == 0):
                        pe.wait_ge(exp_done, GROUPS * s + g)
                    for hh in range(HPG):
                        h = HPG * g + hh
                        pe.matmul(prob_score[:, hh * S:(hh + 1) * S], Ks[q][:, h, 0:P], Qs[q][:, h, :], start=True, stop=True)
                    for hh in range(HPG):
                        h = HPG * g + hh
                        last = pe.matmul(prob_score[:, HPG * S + hh * P:HPG * S + (hh + 1) * P], Ks[q][:, h, P:S], Qs[q][:, h, P:S],
                                         start=True, stop=True)
                    last.then_inc(b_done, 1)

                def values(g):
                    pe.wait_ge(mask_done, 2 * (GROUPS * s + g + 1))
                    if g == 0:
                        pe.wait_ge(v_ready, s + 1)
                        if not first(s, 1):
                            pe.wait_ge(ot_ready, 2 * s)
                    if g == 2:
                        pe.wait_ge(ot_ready, 2 * s + 1)
                    for hh in range(HPG):
                        h = HPG * g + hh
                        out = value_bank[VW * hh:VW * hh + VW, (g % 2) * S:(g % 2) * S + S]
                        pe.matmul(out, V[q][:, 0, h, :], PT[g % 2][:, hh * S:(hh + 1) * S], start=True, stop=False)
                        last = pe.matmul(out[:, P:S], V[q][:, 1, h, :], PT[g % 2][:, HPG * S + hh * P:HPG * S + (hh + 1) * P],
                                         start=False, stop=True)
                    last.then_inc(av_done, 1)

                def turn_values(t):
                    if t == 0:
                        pe.wait_ge(ot_ready, 2 * s)
                        if not (isinstance(s, int) and s > B - 1):
                            pe.wait_ge(nmT_ready, s + 1)
                    elif max_part:
                        pe.wait_ge(v_ready, s + 2)
                    elif not score_part:
                        pe.wait_ge(lg_ready, s - 1)
                    for g in range(GROUPS):
                        last = pe.transpose(bank[1 - t][:, g * P:(g + 1) * P], OT[:, g, t * P:(t + 1) * P], ident[:, :])
                    last.then_inc(ott_done, 1)

                def turn(to, tile, done):
                    for k in range(2):
                        for t in range(2):
                            last = pe.transpose(to[:, k * S + t * P:k * S + (t + 1) * P], tile(t)[:, k * P:(k + 1) * P], ident[:, :])
                    last.then_inc(done, 1)

                def turn_x():
                    pe.wait_ge(xn_ready, 2 * (s + 3))
                    if out_part:
                        pe.wait_ge(norm_done, 2 * s)
                    elif max_part:
                        pe.wait_ge(v_ready, s + 2)
                    else:
                        pe.wait_ge(const_ready, 1)
                    turn(bank[0], lambda t: xn[:, t, :], tx_done)

                def turn_context():
                    pe.wait_ge(ctx_loaded, 16 * (s + 3))
                    pe.wait_ge(xT_lo_ready, s + 3)
                    turn(bank[0], lambda t: c_sb[:, t, :], tc_done)

                def turn_attention():
                    pe.wait_ge(norm_done, 2 * s)
                    turn(bank[1], lambda t: attn[:, t].rearrange("p h d -> p (h d)"), at_done)

                def turn_x2():
                    pe.wait_ge(x2n_ready, 2 * s)
                    if proj_part:
                        pe.wait_ge(q_lo_ready, s + 3)
                    turn(bank[1], lambda t: x2n[:, t, :], x2t_done)

                def turn_maxima():
                    pe.wait_ge(nm_ready, 2 * (s + 2))
                    if out_part:
                        pe.wait_ge(lg_ready, s)
                    elif score_part:
                        pe.wait_ge(k_lo_ready, s + 3)
                    else:
                        pe.wait_ge(k_lo_ready, s + 2)
                    for t in range(2):
                        last = pe.transpose(bank[1][0:2 * HEADS, t * P:(t + 1) * P],
                                            nm_s[:, t].rearrange("p a h -> p (a h)").bitcast(F32), ident[:, :])
                    last.then_inc(nmT_done, 1)

                def project_turned(to, n, hi, lo, done):
                    for f in range(2):
                        m = 0
                        for k in range(2):
                            for w, a in ((w_hi, hi), (w_lo, hi), (w_hi, lo)):
                                m += 1
                                last = pe.matmul(to[:, f * S:(f + 1) * S], w[:, n, k, f * P:(f + 1) * P], a[:, k, :],
                                                 start=(m == 1), stop=(m == 6))
                    last.then_inc(done, 1)

                def project(to, n, hi, lo, done):
                    for t in range(2):
                        m = 0
                        for k in range(2):
                            for a, w in ((hi, w_hi), (lo, w_hi), (hi, w_lo)):
                                m += 1
                                last = pe.matmul(to[:, t * D:(t + 1) * D], a[:, k, t * P:(t + 1) * P], w[:, n, k, :],
                                                 start=(m == 1), stop=(m == 6))
                    last.then_inc(done, 1)

                def queries():
                    pe.wait_ge(xT_lo_ready, s + 3)
                    if first(s, -1):
                        pe.wait_ge(w_lo_ready, WEIGHT_PARTS[1])
                    elif out_part:
                        pe.wait_ge(x2_ready, s)
                    elif first(s, 0):
                        pe.wait_ge(nmT_ready, s + 2)
                    else:
                        pe.wait_ge(q_lo_ready, s + 2)
                    project_turned(bank[1], 0, xT_hi, xT_lo, q_done)

                def keys():
                    pe.wait_ge(cT_lo_ready, s + 3)
                    if first(s, -1):
                        pe.wait_ge(w_lo_ready, WEIGHT_PARTS[2])
                    project_turned(bank[0], 1, cT_hi, cT_lo, k_done)

                def project_values():
                    if first(s, 1):
                        pe.wait_ge(k_lo_ready, s + 2)
                        pe.wait_ge(w_lo_ready, WEIGHT_PARTS[4])
                    project(bank[0], 2, cT_hi, cT_lo, v_done)

                def outputs():
                    pe.wait_ge(aT_lo_ready, s)
                    project(bank[1], 3, aT_hi, aT_lo, op_done)

                def router():
                    pe.wait_ge(x2T_ready, s)
                    if first(s, 2):
                        pe.wait_ge(small_loaded, 48)
                    if proj_part:
                        pe.wait_ge(k_lo_ready, s + 3)
                    elif max_part:
                        pe.wait_ge(v_ready, s + 2)
                    for t in range(2):
                        for k in range(2):
                            last = pe.matmul(bank[0][:, t * EXPERTS:(t + 1) * EXPERTS], x2T[:, k, t * P:(t + 1) * P],
                                             wg_sb[:, k, :], start=(k == 0), stop=(k == 1))
                    last.then_inc(rt_done, 1)

                if is_head(max_part, score_part):
                    project_values()
                    turn_x()
                    a_scores(0)
                    turn_context()
                    for pair in range(1, UNITS // 2):
                        a_scores(pair)
                    turn_maxima()
                    queries()
                    keys()
                elif is_late(proj_part, score_part):
                    if max_part:
                        project_values()
                    if out_part:
                        turn_values(0)
                        turn_values(1)
                    if score_part:
                        b_scores(0)
                    if max_part:
                        a_scores(0)
                    if out_part:
                        turn_attention()
                    if score_part:
                        b_scores(1)
                    if max_part:
                        a_scores(1)
                    if out_part:
                        outputs()
                    if score_part:
                        values(0)
                    if max_part:
                        a_scores(2)
                    if score_part:
                        b_scores(2)
                    if max_part:
                        a_scores(3)
                    if score_part:
                        values(1)
                        b_scores(3)
                    if max_part:
                        a_scores(4)
                    if out_part:
                        turn_x2()
                    if score_part:
                        values(2)
                    if max_part:
                        a_scores(5)
                    if out_part:
                        router()
                    if max_part:
                        turn_maxima()
                    if score_part:
                        values(3)
                else:
                    if max_part:
                        project_values()
                    if out_part:
                        turn_values(0)
                        turn_values(1)
                    if score_part:
                        b_scores(0)
                    if out_part:
                        turn_attention()
                    if proj_part:
                        turn_x()
                    if max_part:
                        a_scores(0)
                    if out_part:
                        outputs()
                    if score_part:
                        b_scores(1)
                    if proj_part:
                        turn_context()
                    if max_part:
                        a_scores(1)
                    if proj_part:
                        queries()
                    if score_part:
                        values(0)
                    if proj_part:
                        keys()
                    if max_part:
                        a_scores(2)
                    if out_part:
                        turn_x2()
                    if score_part:
                        b_scores(2)
                    if max_part:
                        a_scores(3)
                    if out_part:
                        router()
                    if score_part:
                        values(1)
                        b_scores(3)
                    if max_part:
                        a_scores(4)
                    if score_part:
                        values(2)
                    if max_part:
                        a_scores(5)
                    if score_part:
                        values(3)
                    if max_part:
                        turn_maxima()

            steps(pe, step)


def experts(nc, sem, sb, persist, out, w1, b1, w2, b2, xn_rows):
    E, D, H = w1.shape
    T = xn_rows.shape[0]
    TILES = T // P
    KT = TOPK * TILES
    CAP = TOPK * T // E
    ST = CAP // P
    SLOTS = E * ST
    C = H // P
    ident, dl_all, expert_all, ps = (persist[k] for k in ("ident", "dl_all", "expert_all", "ps"))
    raw1, raw2, b1_sb, b2_bc = (persist[k] for k in ("raw1", "raw2", "b1_sb", "b2_bc"))
    tri, onesb, carry = (persist[k] for k in ("tri", "onesb", "carry"))
    iota_e, iota_s, iota_g, iota_k, iota_p = (persist[k] for k in ("iota_e", "iota_s", "iota_g", "iota_k", "iota_p"))
    weights_loaded, biases_loaded, started = (persist[k] for k in ("weights_loaded", "biases_loaded", "started"))

    onehot = sb("onehot", [P, E, KT], BF16)
    base = sb("base", [P, E, KT], F32)
    pos = sb("pos", [P, KT], F32)
    c3 = sb("c3", [P, KT], F32)
    spart = sb("spart", [P, KT], BF16)
    grp = sb("grp", [P, KT], BF16)
    in_slot = sb("in_slot", [P, KT, P], BF16)
    in_tile = sb("in_tile", [P, KT, 2, SLOTS], BF16)
    eq = sb("eq", [P, KT, SLOTS], BF16)
    row = sb("row", [P, SLOTS], F32)
    adj = sb("adj", [P, SLOTS], F32)
    from_row = sb("from_row", [P, SLOTS], F32)
    to_row = sb("to_row", [P, SLOTS], F32)
    ratio = sb("ratio", [P, TILES], F32)
    den = sb("den", [P, TILES], F32)
    gates = sb("gates", [P, TOPK, TILES], F32)
    part = sb("part", [P, 3, KT], BF16)
    rest = sb("rest", [P, 2, KT], F32)
    in_gate = sb("in_gate", [P, KT, 3, SLOTS], BF16)
    slot_gate = sb("slot_gate", [P, SLOTS], F32)
    gather_idx = [sb(f"gather_idx{q}", [P, ST], I32) for q in range(2)]
    scatter_idx = [sb(f"scatter_idx{q}", [P, ST], I32) for q in range(2)]
    w1_hi = [sb(f"w1_hi{q}", [P, 2, C, P], F32R) for q in range(2)]
    w1_lo = [sb(f"w1_lo{q}", [P, 2, C, P], F32R) for q in range(2)]
    w2_hi = [sb(f"w2_hi{q}", [P, C, D], F32R) for q in range(2)]
    w2_lo = [sb(f"w2_lo{q}", [P, C, D], F32R) for q in range(2)]
    Xg = [sb(f"Xg{q}", [P, ST, D], F32) for q in range(2)]
    XT_hi = [sb(f"XT_hi{q}", [P, 2, CAP], F32R) for q in range(2)]
    XT_lo = [sb(f"XT_lo{q}", [P, 2, CAP], F32R) for q in range(2)]
    hr = [sb(f"hr{c}", [P, CAP], F32) for c in range(2)]
    h_hi = [sb(f"h_hi{c}", [P, CAP], F32R) for c in range(4)]
    h_lo = [sb(f"h_lo{c}", [P, CAP], F32R) for c in range(4)]
    Yb = sb("Yb", [P, ST, D], F32)
    Y = [sb(f"Y{q}", [P, ST, D], F32) for q in range(2)]

    counted, placed_a, placed_b, table_done = sem("counted"), sem("placed_a"), sem("placed_b"), sem("table_done")
    placed_k, ratio_ready = sem("placed_k"), sem("ratio_ready")
    gate_parts, in_gate_ready, gate_table_done, slot_gate_ready = (sem(n) for n in ("gate_parts", "in_gate_ready", "gate_table_done", "slot_gate_ready"))
    biased = sem("biased")
    gidx_ready, sidx_ready = sem("gidx_ready"), sem("sidx_ready")
    gathered = [[sem(f"gathered{q}_{j}") for j in range(ST)] for q in range(2)]
    scattered = [sem(f"scattered{q}") for q in range(2)]
    xt_done, xt_hi_ready, xt_lo_ready = sem("xt_done"), sem("xt_hi_ready"), sem("xt_lo_ready")
    wh_ready, wl_ready = sem("wh_ready"), sem("wl_ready")
    h_done, hr_ready, hh_ready, hl_ready = sem("h_done"), sem("hr_ready"), sem("hh_ready"), sem("hl_ready")
    f2_part, y_ready = sem("f2_part"), sem("y_ready")

    xt_bank = ps[:, 0:2, :]
    h_bank = [ps[:, 2, :], ps[:, 3, :], ps[:, 4, :], ps[:, 7, :]]
    y_bank = [ps[:, 5, :], ps[:, 6, :]]
    out_rows = out.rearrange("b s m -> (b s) m")

    def steps(step):
        def run(eng):
            step(0, 0, 0)
            step(1, 1, 0)
            with eng.Fori(1, E // 2 - 1) as it:
                step(2 * it, 0, it)
                step(2 * it + 1, 1, it)
            step(E - 2, 0, E // 2 - 1)
            step(E - 1, 1, E // 2 - 1)
        return run

    def static(e, n):
        return isinstance(e, int) and e >= n

    block = nc.Block()
    with block:

        @block.sync
        def _(sp):
            def step(e, q, it):
                if static(e, E - 2):
                    return
                sp.wait_ge(wh_ready, 4 * (e + 1))
                wait_alone(sp, started, wl_ready, 4 * (e + 1))
                sp.dma_start(raw1[q][:, :, :], w1[e + 2].rearrange("(k p) h -> p k h", p=P)).then_inc(weights_loaded[q], 16)
                sp.dma_start(raw2[q][:, :, :], w2[e + 2].rearrange("(p c) m -> p c m", p=P)).then_inc(weights_loaded[q], 16)
                wait_alone(sp, started, hr_ready, C * (e + 1))
                sp.dma_start(b1_sb[q][:, :], b1[e + 2].rearrange("(p c) -> p c", p=P)).then_inc(biases_loaded[q], 16)
                wait_alone(sp, started, biased, 2 * (e + 1))
                sp.dma_start(b2_bc[q][:, :], b2[bass.ds(e + 2, 1), :].broadcast_to([P, D])).then_inc(biases_loaded[q], 16)

            steps(step)(sp)
            for q in range(2):
                sp.wait_ge(scattered[q], 16 * ST * (E // 2))

        @block.gpsimd
        def _(pool):
            def gather(e, q):
                wait_alone(pool, started, gidx_ready, e + 1)
                if not (isinstance(e, int) and e < 2):
                    wait_alone(pool, started, xt_done, e - 1)
                for j in range(ST):
                    pool.indirect_dma_start(Xg[q][:, j, :], None, xn_rows[:, :],
                                            bass.IndirectOffsetOnAxis(ap=gather_idx[q][:, j:j + 1], axis=0)).then_inc(gathered[q][j], 16)

            def step(e, q, it):
                if not static(e, E - 2):
                    gather(e + 2, q)
                pool.wait_ge(sidx_ready, e + 1)
                if not (isinstance(e, int) and e < 1):
                    wait_alone(pool, started, scattered[1 - q], 16 * ST * (it + q))
                for j in range(ST):
                    wait_alone(pool, started, y_ready, ST * e + j + 1)
                    pool.indirect_dma_start(out_rows[:, :], bass.IndirectOffsetOnAxis(ap=scatter_idx[q][:, j:j + 1], axis=0),
                                            Y[q][:, j, :], None, bounds_check=T - 1, oob_is_err=False, compute_op=ALU.add).then_inc(scattered[q], 16)

            pool.wait_ge(placed_b, 1)
            pool.tensor_tensor(in_tile[:, :, 1, :], eq[:, :, :], iota_k[:, :].unsqueeze(2).broadcast_to([P, KT, SLOTS]), ALU.mult).then_inc(placed_k, 1)
            gather(0, 0)
            gather(1, 1)
            pool.wait_ge(gate_parts, 5)
            for n in range(3):
                pool.tensor_tensor(in_gate[:, :, n, :], eq[:, :, :], part[:, n, :].unsqueeze(2).broadcast_to([P, KT, SLOTS]), ALU.mult).then_inc(in_gate_ready, 1)
            steps(step)(pool)

        @block.scalar
        def _(act):
            act.activation(ratio[:, :], dl_all[:, :], ACT.Exp).then_inc(ratio_ready, 1)

            def split_weights(e, q, it):
                act.wait_ge(weights_loaded[q], 32 * (it + 1))
                if not (isinstance(e, int) and e < 2):
                    act.wait_ge(f2_part, C * (e - 1))
                for k in range(2):
                    act.activation(w1_hi[q][:, k].rearrange("p c j -> p j c"), raw1[q][:, k, :].rearrange("p (j c) -> p j c", c=C), ACT.Copy).then_inc(wh_ready, 1)
                for k in range(2):
                    act.activation(w2_hi[q][:, 4 * k:4 * k + 4], raw2[q][:, 4 * k:4 * k + 4], ACT.Copy).then_inc(wh_ready, 1)

            def turn_rows(e, q):
                act.wait_ge(xt_done, e + 1)
                if not (isinstance(e, int) and e < 2):
                    act.wait_ge(h_done, C * (e - 1))
                for k in range(2):
                    act.activation(XT_hi[q][:, k, :], xt_bank[:, k, :], ACT.Copy).then_inc(xt_hi_ready, 1)

            def step(e, q, it):
                act.wait_ge(biases_loaded[q], 32 * (it + 1))
                for c in range(C):
                    act.wait_ge(h_done, C * e + c + 1)
                    if c >= 2:
                        act.wait_ge(hl_ready, C * e + c - 1)
                    elif not (isinstance(e, int) and e < 1):
                        act.wait_ge(hl_ready, C * e + c - 1)
                    act.activation(hr[c % 2][:, :], h_bank[c % 4], ACT.Relu, bias=b1_sb[q][:, c:c + 1]).then_inc(hr_ready, 1)
                    if c == 1 and not static(e, E - 1):
                        split_weights(e + 1, 1 - q, it + q)
                if not static(e, E - 1):
                    turn_rows(e + 1, 1 - q)

            act.wait_ge(placed_b, 1)
            act.activation(in_tile[:, :, 0, :], eq[:, :, :], ACT.Copy, scale=iota_p[:, 0:1]).then_inc(placed_k, 1)
            split_weights(0, 0, 0)
            turn_rows(0, 0)
            steps(step)(act)

        @block.vector
        def _(dve):
            chain = [0]

            def then(ins):
                chain[0] += 1
                ins.then_inc(placed_a, 1)
                dve.wait_ge(placed_a, chain[0])

            queue = expert_all[:, :, :].rearrange("p k t -> p (k t)")
            then(dve.tensor_tensor(onehot[:, :, :], queue.unsqueeze(1).broadcast_to([P, E, KT]),
                                   iota_e[:, :].unsqueeze(2).broadcast_to([P, E, KT]), ALU.is_equal))
            dve.wait_ge(counted, 1)
            not_before = ps[:, 0, 0:E * KT]
            total = ps[:, 0, E * KT:2 * E * KT]
            flat = base[:, :, :].rearrange("p e n -> p (e n)")
            then(dve.tensor_tensor_scan(flat, carry[:, :, :].rearrange("p e n -> p (e n)"), total, 0.0, ALU.mult, ALU.add))
            then(dve.tensor_tensor(flat, flat, not_before, ALU.add))
            then(dve.tensor_tensor(flat, flat, onehot[:, :, :].rearrange("p e n -> p (e n)"), ALU.mult))
            then(dve.tensor_reduce(pos[:, :], base[:, :, :].rearrange("p e n -> p n e"), AX_X, ALU.add))
            then(dve.tensor_scalar(c3[:, :], pos[:, :], float(P), None, ALU.is_ge))
            for n in range(2, ST):
                then(dve.scalar_tensor_tensor(c3[:, :], pos[:, :], float(n * P), c3[:, :], ALU.is_ge, ALU.add))
            then(dve.scalar_tensor_tensor(spart[:, :], c3[:, :], -float(P), pos[:, :], ALU.mult, ALU.add))
            then(dve.scalar_tensor_tensor(grp[:, :], queue, float(ST), c3[:, :], ALU.mult, ALU.add))
            dve.tensor_tensor(eq[:, :, :], grp[:, :].unsqueeze(2).broadcast_to([P, KT, SLOTS]),
                              iota_g[:, :].unsqueeze(1).broadcast_to([P, KT, SLOTS]), ALU.is_equal).then_inc(placed_b, 1)
            for n in range(KT // 8):
                dve.tensor_tensor(in_slot[:, 8 * n:8 * n + 8, :], spart[:, 8 * n:8 * n + 8].unsqueeze(2).broadcast_to([P, 8, P]),
                                  iota_s[:, :].unsqueeze(1).broadcast_to([P, 8, P]), ALU.is_equal).then_inc(placed_b, 1)
            dve.wait_ge(table_done, 1)
            then(dve.tensor_scalar(row[:, :], ps[:, 1, SLOTS:2 * SLOTS], float(P), -float(P), ALU.mult, ALU.add))
            then(dve.tensor_tensor(row[:, :], row[:, :], ps[:, 1, 0:SLOTS], ALU.add))
            then(dve.tensor_scalar(adj[:, :], row[:, :], float(T), -float(T), ALU.is_ge, ALU.mult))
            then(dve.tensor_tensor(row[:, :], row[:, :], adj[:, :], ALU.add))
            then(dve.tensor_scalar(from_row[:, :], row[:, :], 0.0, None, ALU.max))
            dve.tensor_copy(gather_idx[0][:, :], from_row[:, 0:ST]).then_inc(gidx_ready, 1)
            dve.tensor_copy(gather_idx[1][:, :], from_row[:, ST:2 * ST]).then_inc(gidx_ready, 1)
            then(dve.tensor_scalar(adj[:, :], row[:, :], 0.0, 1e6, ALU.is_lt, ALU.mult))
            then(dve.tensor_tensor(to_row[:, :], row[:, :], adj[:, :], ALU.add))

            def scatter_rows(e, q, it):
                if not (isinstance(e, int) and e < 2):
                    dve.wait_ge(scattered[q], 16 * ST * it)
                dve.tensor_copy(scatter_idx[q][:, :], to_row[:, bass.ds(ST * e, ST)]).then_inc(sidx_ready, 1)

            def weights_part(e, q, n):
                dve.wait_ge(wh_ready, 4 * e + n + 1)
                if n < 2:
                    dve.tensor_tensor(w1_lo[q][:, n].rearrange("p c j -> p j c"), raw1[q][:, n, :].rearrange("p (j c) -> p j c", c=C),
                                      w1_hi[q][:, n].rearrange("p c j -> p j c").bitcast(F32), ALU.subtract).then_inc(wl_ready, 1)
                else:
                    k = n - 2
                    dve.tensor_tensor(w2_lo[q][:, 4 * k:4 * k + 4], raw2[q][:, 4 * k:4 * k + 4],
                                      w2_hi[q][:, 4 * k:4 * k + 4].bitcast(F32), ALU.subtract).then_inc(wl_ready, 1)

            def turn_rows(e, q):
                for k in range(2):
                    dve.wait_ge(xt_hi_ready, 2 * e + k + 1)
                    dve.tensor_tensor(XT_lo[q][:, k, :], xt_bank[:, k, :], XT_hi[q][:, k, :].bitcast(F32), ALU.subtract).then_inc(xt_lo_ready, 1)

            def step(e, q, it):
                if not static(e, E - 2):
                    dve.wait_ge(xt_done, e + 1)
                    dve.tensor_copy(gather_idx[q][:, :], from_row[:, bass.ds(ST * (e + 2), ST)]).then_inc(gidx_ready, 1)
                for c in range(C):
                    dve.wait_ge(hr_ready, C * e + c + 1)
                    if not (isinstance(e, int) and e < 1 and c < 4):
                        dve.wait_ge(f2_part, C * e + c - 3)
                    dve.tensor_copy(h_hi[c % 4][:, :], hr[c % 2][:, :]).then_inc(hh_ready, 1)
                    dve.wait_ge(hh_ready, C * e + c + 1)
                    dve.tensor_tensor(h_lo[c % 4][:, :], hr[c % 2][:, :], h_hi[c % 4][:, :].bitcast(F32), ALU.subtract).then_inc(hl_ready, 1)
                    if c % 2 and not static(e, E - 1):
                        weights_part(e + 1, 1 - q, c // 2)
                    if isinstance(e, int) and e < 1 and c == C - 1:
                        dve.wait_ge(gate_table_done, 1)
                        dve.tensor_reduce(slot_gate[:, :], h_bank[0][:, 0:3 * SLOTS].rearrange("p (a g) -> p g a", a=3), AX_X, ALU.add).then_inc(slot_gate_ready, 1)
                        dve.wait_ge(slot_gate_ready, 1)
                if not static(e, E - 1):
                    turn_rows(e + 1, 1 - q)
                scatter_rows(e, q, it)
                dve.wait_ge(f2_part, C * (e + 1))
                for n in range(2):
                    dve.tensor_tensor(Yb[:, 2 * n:2 * n + 2, :], y_bank[n].rearrange("p (j m) -> p j m", j=2),
                                      b2_bc[q][:, :].unsqueeze(1).broadcast_to([P, 2, D]), ALU.add).then_inc(biased, 1)
                for j in range(ST):
                    if j % 2 == 0:
                        wait_alone(dve, started, biased, 2 * e + j // 2 + 1)
                    dve.tensor_scalar(Y[q][:, j, :], Yb[:, j, :], slot_gate[:, bass.ds(ST * e + j, 1)], None, ALU.mult).then_inc(y_ready, 1)

            for n in range(4):
                weights_part(0, 0, n)
            dve.wait_ge(ratio_ready, 1)
            then(dve.tensor_scalar(den[:, :], ratio[:, :], 1.0, None, ALU.add))
            then(dve.reciprocal(gates[:, 0, :], den[:, :]))
            then(dve.tensor_tensor(gates[:, 1, :], gates[:, 0, :], ratio[:, :], ALU.mult))
            left = gates[:, :, :].rearrange("p k t -> p (k t)")
            for n in range(3):
                dve.tensor_copy(part[:, n, :], left).then_inc(gate_parts, 1)
                if n < 2:
                    dve.wait_ge(gate_parts, 2 * n + 1)
                    dve.tensor_tensor(rest[:, n, :], left, part[:, n, :], ALU.subtract).then_inc(gate_parts, 1)
                    left = rest[:, n, :]
                    dve.wait_ge(gate_parts, 2 * n + 2)
            turn_rows(0, 0)
            steps(step)(dve)

        @block.tensor
        def _(pe):
            pe.wait_ge(placed_a, 1)
            oh = onehot[:, :, :].rearrange("p e n -> p (e n)")
            pe.matmul(ps[:, 0, 0:E * KT], tri[:, :], oh, start=True, stop=True)
            pe.matmul(ps[:, 0, E * KT:2 * E * KT], onesb[:, :], oh, start=True, stop=True).then_inc(counted, 1)
            pe.wait_ge(placed_k, 2)
            for n in range(KT):
                if n % 8 == 0:
                    pe.wait_ge(placed_b, n // 8 + 2)
                last = pe.matmul(ps[:, 1, 0:2 * SLOTS], in_slot[:, n, :], in_tile[:, n].rearrange("p a g -> p (a g)"),
                                 start=(n == 0), stop=(n == KT - 1))
            last.then_inc(table_done, 1)

            def turn_rows(e, q, it):
                if isinstance(e, int) and e < 1:
                    pe.wait_ge(gidx_ready, 2)
                else:
                    pe.wait_ge(xt_lo_ready, 2 * e)
                for j in range(ST):
                    pe.wait_ge(gathered[q][j], 16 * (it + 1))
                    for k in range(2):
                        last = pe.transpose(xt_bank[:, k, j * P:(j + 1) * P], Xg[q][:, j, k * P:(k + 1) * P], ident[:, :])
                last.then_inc(xt_done, 1)

            def step(e, q, it):
                def layer1(c):
                    if c == 0:
                        pe.wait_ge(wl_ready, 4 * (e + 1))
                    if not (isinstance(e, int) and e < 1 and c < 4):
                        pe.wait_ge(hr_ready, C * e + c - 3)
                    if isinstance(e, int) and e == 1 and c == 0:
                        pe.wait_ge(slot_gate_ready, 1)
                    n = 0
                    for k in range(2):
                        if c == 0:
                            pe.wait_ge(xt_lo_ready, 2 * e + k + 1)
                        for w, a in ((w1_hi, XT_hi), (w1_lo, XT_hi), (w1_hi, XT_lo)):
                            n += 1
                            last = pe.matmul(h_bank[c % 4], w[q][:, k, c, :], a[q][:, k, :], start=(n == 1), stop=(n == 6))
                    last.then_inc(h_done, 1)

                def layer2(c):
                    pe.wait_ge(hl_ready, C * e + c + 1)
                    if c == 0 and not (isinstance(e, int) and e < 1):
                        pe.wait_ge(biased, 2 * e)
                    for j in range(ST):
                        for n, (a, w) in enumerate(((h_hi, w2_hi), (h_lo, w2_hi), (h_hi, w2_lo))):
                            last = pe.matmul(y_bank[j // 2][:, (j % 2) * D:(j % 2 + 1) * D], a[c % 4][:, j * P:(j + 1) * P], w[q][:, c, :],
                                             start=(c == 0 and n == 0 and j % 2 == 0), stop=(c == C - 1 and n == 2), skip_group_check=True)
                    last.then_inc(f2_part, 1)

                layer1(0)
                layer1(1)
                layer1(2)
                for c in range(C):
                    layer2(c)
                    if c + 3 < C:
                        layer1(c + 3)
                    if c == C - 4 and isinstance(e, int) and e < 1:
                        pe.wait_ge(in_gate_ready, 3)
                        pe.wait_ge(hr_ready, 5)
                        for n in range(KT):
                            last = pe.matmul(h_bank[0][:, 0:3 * SLOTS], in_slot[:, n, :], in_gate[:, n].rearrange("p a g -> p (a g)"),
                                             start=(n == 0), stop=(n == KT - 1))
                        last.then_inc(gate_table_done, 1)
                    if c == C - 4 and not static(e, E - 1):
                        turn_rows(e + 1, 1 - q, it + q)

            turn_rows(0, 0, 0)
            steps(step)(pe)


def program(nc, x, ctx_1024, Wq, Wk, Wv, bv, Wo, bo, wg, w1, b1, w2, b2, out):
    B, S, D = x.shape
    T = B * S
    C = w1.shape[2] // P
    KT = TOPK * T // P
    with ExitStack() as ctx:
        def sem(name):
            return ctx.enter_context(nc.semaphore(name))

        def sb(name, shape, dt):
            return ctx.enter_context(nc.sbuf_tensor(name, shape, dt))

        xn_rows = nc.dram_tensor("xn_rows", [T, D], F32, kind="Internal").ap()
        persist = {
            "x_all": sb("x_all", [P, T // P, D], F32),
            "ident": sb("ident", [P, P], F32),
            "dl_all": sb("dl_all", [P, T // P], F32),
            "expert_all": sb("expert_all", [P, TOPK, T // P], F32),
            "tri": sb("tri", [P, P], BF16),
            "onesb": sb("onesb", [P, P], BF16),
            "carry": sb("carry", [P, EXPERTS, KT], F32),
            "iota_e": sb("iota_e", [P, EXPERTS], F32),
            "iota_s": sb("iota_s", [P, P], BF16),
            "iota_g": sb("iota_g", [P, TOPK * T // P], BF16),
            "iota_k": sb("iota_k", [P, KT], F32),
            "iota_p": sb("iota_p", [P, 1], F32),
            "raw1": [sb(f"raw1_{q}", [P, 2, C * P], F32) for q in range(2)],
            "raw2": [sb(f"raw2_{q}", [P, C, D], F32) for q in range(2)],
            "b1_sb": [sb(f"b1_sb{q}", [P, C], F32) for q in range(2)],
            "b2_bc": [sb(f"b2_bc{q}", [P, D], F32) for q in range(2)],
            "ps": ctx.enter_context(nc.psum_tensor("ps", [P, 8, 512], F32)),
            "weights_loaded": [sem(f"weights_loaded{q}") for q in range(2)],
            "biases_loaded": [sem(f"biases_loaded{q}") for q in range(2)],
            "started": sem("started"),
        }
        for part, args in ((attention, (x, ctx_1024, Wq, Wk, Wv, bv, Wo, bo, wg, w1, b1, w2, b2, xn_rows, out)),
                           (experts, (out, w1, b1, w2, b2, xn_rows))):
            with ExitStack() as own:
                part(nc, sem, lambda n, s, d: own.enter_context(nc.sbuf_tensor(n, s, d)), persist, *args)


_INS = ['x', 'ctx_1024', 'L0_xattn_W_q', 'L0_xattn_W_k', 'L0_xattn_W_v', 'L0_xattn_b_v', 'L0_xattn_W_o', 'L0_xattn_b_o',
        'L0_ffn_wg', 'L0_ffn_w1', 'L0_ffn_b1', 'L0_ffn_w2', 'L0_ffn_b2']


def kernel(**inputs):
    import numpy as _np
    import concourse.bacc as _bacc
    from concourse import mybir as _mybir
    from concourse.bass_utils import run_bass_kernel_spmd as _run

    nc = _bacc.Bacc("TRN2", target_bir_lowering=False, num_devices=1)
    arrays, args = {}, []
    for name in _INS:
        a = _np.ascontiguousarray(inputs[name])
        arrays[f"in_{name}_dram"] = a
        args.append(nc.dram_tensor(f"in_{name}_dram", a.shape, _mybir.dt.from_np(a.dtype), kind="ExternalInput").ap())
    out = nc.dram_tensor("out_0_dram", inputs["x"].shape, F32, kind="ExternalOutput").ap()
    program(nc, *args, out)
    r = _run(nc, [arrays], core_ids=[0])
    return r.results[0]["out_0_dram"]
```
